# Optimizing a Trainium2 kernel written in Bass

```python
import numpy as np
import jax
import jax.numpy as jnp

def _softmax(x, axis=-1):
    return jax.nn.softmax(x, axis=axis)

def _gelu(x):
    return jax.nn.gelu(x, approximate=True)

def _silu(x):
    return jax.nn.silu(x)

def _sigmoid(x):
    return jax.nn.sigmoid(x)

def _layernorm(x, axis=-1, eps=1e-05):
    m = jnp.mean(x, axis=axis, keepdims=True)
    v = jnp.var(x, axis=axis, keepdims=True)
    return (x - m) / jnp.sqrt(v + eps)

def _scatter_add(tgt, idx, src, axis=0):
    return tgt.at[idx].add(src)

def _segment_sum(src, seg, n):
    return jax.ops.segment_sum(src, seg, n)
kernel_name = 'mk_decoder_postln_d2_seqx_r8_2ffb65'

def setup_inputs(seed: int=0):
    np.random.seed(seed)
    _w = jnp.asarray

    def _rec_inputs():
        import jax
        import jax.numpy as jnp
        _rk = jax.random.key(seed)
        x = -0.000125 + 0.9999 * jax.random.normal(jax.random.fold_in(_rk, 1), (2, 256, 512), jnp.float32)
        _lenS = 256 - jax.random.randint(jax.random.fold_in(_rk, 7), (2,), 0, max(1, 256 // 4) + 1, jnp.int32)
        _lenS2 = 512 - jax.random.randint(jax.random.fold_in(_rk, 8), (2,), 0, max(1, 512 // 4) + 1, jnp.int32)
        _ctx_4096P = jax.random.normal(jax.random.fold_in(_rk, 11), (2, 16, 512), jnp.float32)
        _ctx_4096c = jax.random.dirichlet(jax.random.fold_in(_rk, 511), 0.3 * jnp.ones((16,), jnp.float32), (2, 512))
        _ctx_4096t = jnp.einsum('bsk,bkd->bsd', _ctx_4096c, _ctx_4096P)
        _ctx_4096t = _ctx_4096t * jax.lax.rsqrt(jnp.mean(jnp.square(_ctx_4096t)) + 1e-12) * 0.953939
        ctx_4096 = -5.72187e-05 + 0.999849 * (_ctx_4096t + 0.3 * jax.random.normal(jax.random.fold_in(_rk, 611), (2, 512, 512), jnp.float32))
        _validS = jnp.arange(256)[None, :] < _lenS[:, None]
        _validS2 = jnp.arange(512)[None, :] < _lenS2[:, None]
        _causal = jnp.tril(jnp.ones((256, 256), dtype=bool))
        mask_1x1xSxS2_ff0 = jnp.where(jnp.ones((1, 1, 256, 512), dtype=bool), 0.0, -1000000000.0).astype(jnp.float32)
        return (x, ctx_4096, mask_1x1xSxS2_ff0)
    x, ctx_4096, mask_1x1xSxS2_ff0 = _rec_inputs()

    def _L0_attn_setup():
        import jax, jax.numpy as jnp
        import numpy as np
        import math
        B, S, D = (1, 256, 512)
        H, KV, HD = (32, 8, 128)
        GROUPS = H // KV
        SYS_LEN, IMG_LEN = (35, 72)
        ENH, SUP = (1.5, 0.5)
        ROPE_BASE = 10000.0

        def _rope_cos_sin(seq_len, dtype):
            inv_freq = 1.0 / ROPE_BASE ** (jnp.arange(0, HD, 2, dtype=jnp.float32) / HD)
            pos = jnp.arange(seq_len, dtype=jnp.float32)
            freqs = pos[:, None] * inv_freq[None, :]
            emb = jnp.concatenate([freqs, freqs], axis=-1)
            return (jnp.cos(emb).astype(dtype), jnp.sin(emb).astype(dtype))

        def _rotate_half(x):
            x1, x2 = (x[..., :HD // 2], x[..., HD // 2:])
            return jnp.concatenate([-x2, x1], axis=-1)
        key = jax.random.key(seed)
        ks = jax.random.split(key, 5)
        scale = 0.02
        return {'hidden_states': jax.random.normal(ks[0], (B, S, D), dtype=jnp.float32), 'wq': jax.random.normal(ks[1], (H * HD, D), dtype=jnp.float32) * scale, 'wk': jax.random.normal(ks[2], (KV * HD, D), dtype=jnp.float32) * scale, 'wv': jax.random.normal(ks[3], (KV * HD, D), dtype=jnp.float32) * scale, 'wo': jax.random.normal(ks[4], (D, H * HD), dtype=jnp.float32) * scale}
    _L0_attn_all = _L0_attn_setup()
    _L0_attn_in = {k: v for k, v in _L0_attn_all.items() if k in ('wq', 'wk', 'wv', 'wo')}
    del _L0_attn_all

    def _L0_xattn_setup():
        import jax, jax.numpy as jnp
        import numpy as np
        QMIN = 0.0
        QMAX = 255.0

        def fake_quant(x, scale, zp):
            s = scale.reshape(())
            z = zp.reshape(())
            q = jnp.clip(jnp.round(x / s + z), QMIN, QMAX)
            return (q - z) * s
        key = jax.random.key(seed)
        k1, k2 = jax.random.split(key)
        B, M, K, N = (4, 256, 512, 512)
        x1 = jax.random.normal(k1, (B, M, K), dtype=jnp.float32)
        x2 = jax.random.normal(k2, (B, K, N), dtype=jnp.float32)
        x1_scale = jnp.full((1,), 8.0 / 255.0, dtype=jnp.float32)
        x1_zp = jnp.full((1,), 128.0, dtype=jnp.float32)
        x2_scale = jnp.full((1,), 8.0 / 255.0, dtype=jnp.float32)
        x2_zp = jnp.full((1,), 128.0, dtype=jnp.float32)
        return {'x1': x1, 'x2': x2, 'x1_scale': x1_scale, 'x1_zp': x1_zp, 'x2_scale': x2_scale, 'x2_zp': x2_zp}
    _L0_xattn_all = _L0_xattn_setup()
    _L0_xattn_in = {k: v for k, v in _L0_xattn_all.items() if k in ('x1_scale', 'x1_zp', 'x2_scale', 'x2_zp')}
    del _L0_xattn_all

    def _L0_ffn_setup():
        import jax, jax.numpy as jnp
        import numpy as np
        N_STREAMS = 4
        DIM = 128
        SINKHORN_ITERS = 50
        SINKHORN_TAU = 0.1
        RMS_EPS = 1.1920929e-07

        def sinkhorn_log(logits, num_iters=SINKHORN_ITERS, tau=SINKHORN_TAU):
            Z = logits / tau
            u0 = jnp.zeros(Z.shape[:-1], Z.dtype)
            v0 = jnp.zeros_like(u0)

            def step(carry, _):
                u, v = carry
                u = -jax.nn.logsumexp(Z + v[..., None, :], axis=-1)
                v = -jax.nn.logsumexp(Z + u[..., :, None], axis=-2)
                return ((u, v), None)
            (u, v), _ = jax.lax.scan(step, (u0, v0), None, length=num_iters)
            return jnp.exp(Z + u[..., :, None] + v[..., None, :])
        key = jax.random.key(seed)
        ks = jax.random.split(key, 6)
        B, T = (4, 256)
        n, C = (N_STREAMS, DIM)
        wd = n * C
        x = jax.random.normal(ks[0], (B, T, wd), dtype=jnp.float32)
        W_res = 0.01 * jax.random.normal(ks[1], (n * n, wd), dtype=jnp.float32)
        W_pre = 0.01 * jax.random.normal(ks[2], (n, wd), dtype=jnp.float32)
        W_post = 0.01 * jax.random.normal(ks[3], (n, wd), dtype=jnp.float32)
        H_res_base = jnp.full((n, n), -0.5, dtype=jnp.float32)
        H_res_base = H_res_base.at[jnp.arange(n), jnp.arange(n)].set(0.0)
        H_pre_base = jnp.zeros((n,), dtype=jnp.float32).at[0].set(1.0)
        H_post_base = jnp.zeros((n,), dtype=jnp.float32)
        gate = jnp.array([5.0], dtype=jnp.float32)
        W_branch = 1.0 / np.sqrt(C) * jax.random.normal(ks[4], (C, C), dtype=jnp.float32)
        return {'x': x, 'W_res': W_res, 'W_pre': W_pre, 'W_post': W_post, 'H_res_base': H_res_base, 'H_pre_base': H_pre_base, 'H_post_base': H_post_base, 'gate': gate, 'W_branch': W_branch}
    _L0_ffn_all = _L0_ffn_setup()
    _L0_ffn_in = {k: v for k, v in _L0_ffn_all.items() if k in ('W_res', 'W_pre', 'W_post', 'H_res_base', 'H_pre_base', 'H_post_base', 'gate', 'W_branch')}
    del _L0_ffn_all

    def _L1_attn_setup():
        import jax, jax.numpy as jnp
        import numpy as np
        from jax import lax
        H, KVH, D, CHUNK = (32, 8, 128, 128)
        ROPE_THETA = 10000.0
        RMS_EPS = 1e-05

        def _rope_tables(L):
            inv_freq = 1.0 / ROPE_THETA ** (jnp.arange(0, D, 2, dtype=jnp.float32) / D)
            ang = jnp.arange(L, dtype=jnp.float32)[:, None] * inv_freq
            cos = jnp.concatenate([jnp.cos(ang), jnp.cos(ang)], axis=-1)[:, None, :]
            sin = jnp.concatenate([jnp.sin(ang), jnp.sin(ang)], axis=-1)[:, None, :]
            return (cos, sin)

        def _apply_rope(x, cos, sin):
            half = D // 2
            rot = jnp.concatenate([-x[..., half:], x[..., :half]], axis=-1)
            return x * cos + rot * sin
        key = jax.random.key(seed)
        ks = jax.random.split(key, 10)
        B, L, HID = (1, 512, 512)
        s = lambda fan: 1.0 / np.sqrt(fan)
        return {'hidden_states': jax.random.normal(ks[0], (B, L, HID), jnp.float32), 'Wq': jax.random.normal(ks[1], (H * D, HID), jnp.float32) * s(HID), 'Wk': jax.random.normal(ks[2], (KVH * D, HID), jnp.float32) * s(HID), 'Wv': jax.random.normal(ks[3], (KVH * D, HID), jnp.float32) * s(HID), 'Wo': jax.random.normal(ks[4], (HID, H * D), jnp.float32) * s(H * D), 'Wg': jax.random.normal(ks[5], (H * D, HID), jnp.float32) * (s(HID) * 2 ** (-2.5)), 'Win': jax.random.normal(ks[6], (H, HID), jnp.float32) * s(HID), 'dt_bias': jnp.zeros((H,), jnp.float32), 'A_log_bias': jnp.log(jax.random.uniform(ks[7], (H,), jnp.float32, 1.0, 16.0)), 'gnorm_w': jnp.ones((D,), jnp.float32)}
    _L1_attn_all = _L1_attn_setup()
    _L1_attn_in = {k: v for k, v in _L1_attn_all.items() if k in ('Wq', 'Wk', 'Wv', 'Wo', 'Wg', 'Win', 'dt_bias', 'A_log_bias', 'gnorm_w')}
    del _L1_attn_all

    def _L1_xattn_setup():
        import jax, jax.numpy as jnp
        import numpy as np
        B, Q, K, D = (1, 128, 6404, 512)
        H, KVH, HD = (32, 8, 128)
        GROUPS = H // KVH
        EPS = 1e-05

        def _rmsnorm(x, w):
            xf = x.astype(jnp.float32)
            var = jnp.mean(xf * xf, axis=-1, keepdims=True)
            return (xf * jax.lax.rsqrt(var + EPS)).astype(x.dtype) * w
        key = jax.random.key(seed)
        ks = jax.random.split(key, 8)
        s = 0.02
        return {'hidden_states': jax.random.normal(ks[0], (B, Q, D), jnp.float32), 'cross_attention_states': jax.random.normal(ks[1], (B, K, D), jnp.float32), 'attention_mask': jnp.zeros((B, 1, Q, K), jnp.float32), 'Wq': jax.random.normal(ks[2], (H * HD, D), jnp.float32) * s, 'Wk': jax.random.normal(ks[3], (KVH * HD, D), jnp.float32) * s, 'Wv': jax.random.normal(ks[4], (KVH * HD, D), jnp.float32) * s, 'Wo': jax.random.normal(ks[5], (D, H * HD), jnp.float32) * s, 'q_norm_w': jnp.ones((HD,), jnp.float32), 'k_norm_w': jnp.ones((HD,), jnp.float32)}
    _L1_xattn_all = _L1_xattn_setup()
    _L1_xattn_in = {k: v for k, v in _L1_xattn_all.items() if k in ('Wq', 'Wk', 'Wv', 'Wo', 'q_norm_w', 'k_norm_w')}
    del _L1_xattn_all

    def _L1_ffn_setup():
        import jax, jax.numpy as jnp
        import numpy as np
        LORA_RANK = 16
        LORA_ALPHA = 16
        LORA_SCALE = LORA_ALPHA / LORA_RANK
        key = jax.random.key(seed)
        k1, k2, k3, k4, k5 = jax.random.split(key, 5)
        B, S, D_IN, D_OUT, N_LORA, R = (8, 256, 512, 512, 3, LORA_RANK)
        std = 1.0 / np.sqrt(D_IN)
        x = jax.random.normal(k1, (B, S, D_IN), dtype=jnp.float32)
        weight = jax.random.truncated_normal(k2, -3.0, 3.0, (D_OUT, D_IN), dtype=jnp.float32) * std
        bias = jax.random.normal(k3, (D_OUT,), dtype=jnp.float32) * 0.01
        lora_A = jax.random.normal(k4, (N_LORA, R, D_IN), dtype=jnp.float32) * std
        lora_B = jax.random.normal(k5, (N_LORA, D_OUT, R), dtype=jnp.float32) * 0.02
        lora_start_indices = jnp.arange(4, dtype=jnp.int64) * 2
        return {'x': x, 'weight': weight, 'bias': bias, 'lora_A': lora_A, 'lora_B': lora_B, 'lora_start_indices': lora_start_indices}
    _L1_ffn_all = _L1_ffn_setup()
    _L1_ffn_in = {k: v for k, v in _L1_ffn_all.items() if k in ('weight', 'bias', 'lora_A', 'lora_B', 'lora_start_indices')}
    del _L1_ffn_all
    return {'x': x, 'ctx_4096': ctx_4096, 'mask_1x1xSxS2_ff0': mask_1x1xSxS2_ff0, 'L0_attn_wq': _L0_attn_in['wq'], 'L0_attn_wk': _L0_attn_in['wk'], 'L0_attn_wv': _L0_attn_in['wv'], 'L0_attn_wo': _L0_attn_in['wo'], 'L0_xattn_x1_scale': _L0_xattn_in['x1_scale'], 'L0_xattn_x1_zp': _L0_xattn_in['x1_zp'], 'L0_xattn_x2_scale': _L0_xattn_in['x2_scale'], 'L0_xattn_x2_zp': _L0_xattn_in['x2_zp'], 'L0_ffn_W_res': _L0_ffn_in['W_res'], 'L0_ffn_W_pre': _L0_ffn_in['W_pre'], 'L0_ffn_W_post': _L0_ffn_in['W_post'], 'L0_ffn_H_res_base': _L0_ffn_in['H_res_base'], 'L0_ffn_H_pre_base': _L0_ffn_in['H_pre_base'], 'L0_ffn_H_post_base': _L0_ffn_in['H_post_base'], 'L0_ffn_gate': _L0_ffn_in['gate'], 'L0_ffn_W_branch': _L0_ffn_in['W_branch'], 'L1_attn_Wq': _L1_attn_in['Wq'], 'L1_attn_Wk': _L1_attn_in['Wk'], 'L1_attn_Wv': _L1_attn_in['Wv'], 'L1_attn_Wo': _L1_attn_in['Wo'], 'L1_attn_Wg': _L1_attn_in['Wg'], 'L1_attn_Win': _L1_attn_in['Win'], 'L1_attn_dt_bias': _L1_attn_in['dt_bias'], 'L1_attn_A_log_bias': _L1_attn_in['A_log_bias'], 'L1_attn_gnorm_w': _L1_attn_in['gnorm_w'], 'L1_xattn_Wq': _L1_xattn_in['Wq'], 'L1_xattn_Wk': _L1_xattn_in['Wk'], 'L1_xattn_Wv': _L1_xattn_in['Wv'], 'L1_xattn_Wo': _L1_xattn_in['Wo'], 'L1_xattn_q_norm_w': _L1_xattn_in['q_norm_w'], 'L1_xattn_k_norm_w': _L1_xattn_in['k_norm_w'], 'L1_ffn_weight': _L1_ffn_in['weight'], 'L1_ffn_bias': _L1_ffn_in['bias'], 'L1_ffn_lora_A': _L1_ffn_in['lora_A'], 'L1_ffn_lora_B': _L1_ffn_in['lora_B'], 'L1_ffn_lora_start_indices': _L1_ffn_in['lora_start_indices']}

def reference(x, ctx_4096, mask_1x1xSxS2_ff0, L0_attn_wq, L0_attn_wk, L0_attn_wv, L0_attn_wo, L0_xattn_x1_scale, L0_xattn_x1_zp, L0_xattn_x2_scale, L0_xattn_x2_zp, L0_ffn_W_res, L0_ffn_W_pre, L0_ffn_W_post, L0_ffn_H_res_base, L0_ffn_H_pre_base, L0_ffn_H_post_base, L0_ffn_gate, L0_ffn_W_branch, L1_attn_Wq, L1_attn_Wk, L1_attn_Wv, L1_attn_Wo, L1_attn_Wg, L1_attn_Win, L1_attn_dt_bias, L1_attn_A_log_bias, L1_attn_gnorm_w, L1_xattn_Wq, L1_xattn_Wk, L1_xattn_Wv, L1_xattn_Wo, L1_xattn_q_norm_w, L1_xattn_k_norm_w, L1_ffn_weight, L1_ffn_bias, L1_ffn_lora_A, L1_ffn_lora_B, L1_ffn_lora_start_indices):
    import jax
    import jax.numpy as jnp

    def _L0_attn_ref(hidden_states, wq, wk, wv, wo):
        import jax, jax.numpy as jnp
        import numpy as np
        import math
        B, S, D = (1, 256, 512)
        H, KV, HD = (32, 8, 128)
        GROUPS = H // KV
        SYS_LEN, IMG_LEN = (35, 72)
        ENH, SUP = (1.5, 0.5)
        ROPE_BASE = 10000.0

        def _rope_cos_sin(seq_len, dtype):
            inv_freq = 1.0 / ROPE_BASE ** (jnp.arange(0, HD, 2, dtype=jnp.float32) / HD)
            pos = jnp.arange(seq_len, dtype=jnp.float32)
            freqs = pos[:, None] * inv_freq[None, :]
            emb = jnp.concatenate([freqs, freqs], axis=-1)
            return (jnp.cos(emb).astype(dtype), jnp.sin(emb).astype(dtype))

        def _rotate_half(x):
            x1, x2 = (x[..., :HD // 2], x[..., HD // 2:])
            return jnp.concatenate([-x2, x1], axis=-1)
        bsz, q_len, _ = hidden_states.shape
        dt = hidden_states.dtype
        q = (hidden_states @ wq.T).reshape(bsz, q_len, H, HD).transpose(0, 2, 1, 3)
        k = (hidden_states @ wk.T).reshape(bsz, q_len, KV, HD).transpose(0, 2, 1, 3)
        v = (hidden_states @ wv.T).reshape(bsz, q_len, KV, HD).transpose(0, 2, 1, 3)
        cos, sin = _rope_cos_sin(q_len, dt)
        q = q * cos + _rotate_half(q) * sin
        k = k * cos + _rotate_half(k) * sin
        k = jnp.repeat(k, GROUPS, axis=1)
        v = jnp.repeat(v, GROUPS, axis=1)
        scores = jnp.einsum('bhqd,bhkd->bhqk', q, k) / math.sqrt(HD)
        kpos = jnp.arange(q_len)
        key_scale = jnp.where(kpos < SYS_LEN, SUP, jnp.where(kpos < SYS_LEN + IMG_LEN, ENH, 1.0)).astype(dt)
        qpos = jnp.arange(q_len)
        row_sel = (qpos >= SYS_LEN + IMG_LEN)[:, None]
        scale = jnp.where(row_sel, key_scale[None, :], jnp.ones((), dt))
        scores = scores * scale
        causal = jnp.where(qpos[:, None] >= kpos[None, :], 0.0, jnp.finfo(jnp.float32).min)
        scores = scores + causal.astype(dt)
        probs = jax.nn.softmax(scores.astype(jnp.float32), axis=-1).astype(dt)
        attn = jnp.einsum('bhqk,bhkd->bhqd', probs, v)
        attn = attn.transpose(0, 2, 1, 3).reshape(bsz, q_len, H * HD)
        return attn @ wo.T

    def _L0_xattn_ref(x1, x2, x1_scale, x1_zp, x2_scale, x2_zp):
        import jax, jax.numpy as jnp
        import numpy as np
        QMIN = 0.0
        QMAX = 255.0

        def fake_quant(x, scale, zp):
            s = scale.reshape(())
            z = zp.reshape(())
            q = jnp.clip(jnp.round(x / s + z), QMIN, QMAX)
            return (q - z) * s
        q1 = fake_quant(x1, x1_scale, x1_zp)
        q2 = fake_quant(x2, x2_scale, x2_zp)
        return jnp.matmul(q1, q2)

    def _L0_ffn_ref(x, W_res, W_pre, W_post, H_res_base, H_pre_base, H_post_base, gate, W_branch):
        import jax, jax.numpy as jnp
        import numpy as np
        N_STREAMS = 4
        DIM = 128
        SINKHORN_ITERS = 50
        SINKHORN_TAU = 0.1
        RMS_EPS = 1.1920929e-07

        def sinkhorn_log(logits, num_iters=SINKHORN_ITERS, tau=SINKHORN_TAU):
            Z = logits / tau
            u0 = jnp.zeros(Z.shape[:-1], Z.dtype)
            v0 = jnp.zeros_like(u0)

            def step(carry, _):
                u, v = carry
                u = -jax.nn.logsumexp(Z + v[..., None, :], axis=-1)
                v = -jax.nn.logsumexp(Z + u[..., :, None], axis=-2)
                return ((u, v), None)
            (u, v), _ = jax.lax.scan(step, (u0, v0), None, length=num_iters)
            return jnp.exp(Z + u[..., :, None] + v[..., None, :])
        B, T, nC = x.shape
        n = N_STREAMS
        C = nC // n
        x_norm = x * jax.lax.rsqrt(jnp.mean(x * x, axis=-1, keepdims=True) + RMS_EPS)
        H_res_logits = (x_norm @ W_res.T).reshape(B, T, n, n) + H_res_base
        H_pre_logits = x_norm @ W_pre.T + H_pre_base
        H_post_logits = x_norm @ W_post.T + H_post_base
        H_res = sinkhorn_log(H_res_logits)
        H_pre = jax.nn.softmax(H_pre_logits, axis=-1)
        H_post = jax.nn.softmax(H_post_logits, axis=-1)
        g = jax.nn.sigmoid(gate)[0]
        I = jnp.eye(n, dtype=H_res.dtype)
        H_res = (1.0 - g) * I + g * H_res
        x_streams = x.reshape(B, T, n, C)
        x_pre = jnp.einsum('btnc,btn->btc', x_streams, H_pre)
        y = x_pre @ W_branch
        x_mixed = jnp.einsum('btij,btjc->btic', H_res, x_streams)
        y_distributed = jnp.einsum('btc,btn->btnc', y, H_post)
        return (x_mixed + y_distributed).reshape(B, T, nC)

    def _L1_attn_ref(hidden_states, Wq, Wk, Wv, Wo, Wg, Win, dt_bias, A_log_bias, gnorm_w):
        import jax, jax.numpy as jnp
        import numpy as np
        from jax import lax
        H, KVH, D, CHUNK = (32, 8, 128, 128)
        ROPE_THETA = 10000.0
        RMS_EPS = 1e-05

        def _rope_tables(L):
            inv_freq = 1.0 / ROPE_THETA ** (jnp.arange(0, D, 2, dtype=jnp.float32) / D)
            ang = jnp.arange(L, dtype=jnp.float32)[:, None] * inv_freq
            cos = jnp.concatenate([jnp.cos(ang), jnp.cos(ang)], axis=-1)[:, None, :]
            sin = jnp.concatenate([jnp.sin(ang), jnp.sin(ang)], axis=-1)[:, None, :]
            return (cos, sin)

        def _apply_rope(x, cos, sin):
            half = D // 2
            rot = jnp.concatenate([-x[..., half:], x[..., :half]], axis=-1)
            return x * cos + rot * sin
        B, L, HID = hidden_states.shape
        NC = L // CHUNK
        q = (hidden_states @ Wq.T).reshape(B, L, H, D)
        k = (hidden_states @ Wk.T).reshape(B, L, KVH, D)
        v = (hidden_states @ Wv.T).reshape(B, L, KVH, D)
        cos, sin = _rope_tables(L)
        q = _apply_rope(q, cos, sin)
        k = _apply_rope(k, cos, sin)
        k = jnp.repeat(k, H // KVH, axis=2)
        v = jnp.repeat(v, H // KVH, axis=2)
        dt = jax.nn.softplus(hidden_states @ Win.T + dt_bias)
        A = -jnp.exp(A_log_bias)
        g = dt * A

        def chunked(t):
            return t.transpose(0, 2, 1, 3).reshape(B, H, NC, CHUNK, D)
        qc, kc = (chunked(q), chunked(k))
        xc = chunked(v * dt[..., None])
        gc = g.transpose(0, 2, 1).reshape(B, H, NC, CHUNK)
        G = jnp.cumsum(gc, axis=-1)
        scores = jnp.einsum('bhnid,bhnjd->bhnij', qc, kc)
        idx = jnp.arange(CHUNK)
        causal = idx[:, None] >= idx[None, :]
        decay = jnp.where(causal, jnp.exp(G[..., :, None] - G[..., None, :]), 0.0)
        y_intra = jnp.einsum('bhnij,bhnjd->bhnid', scores * decay, xc)
        Glast = G[..., -1:]
        k_dec = kc * jnp.exp(Glast - G)[..., None]
        cstates = jnp.einsum('bhnjd,bhnje->bhnde', k_dec, xc)
        chunk_decay = jnp.exp(G[..., -1])

        def step(state, inp):
            dec, cs = inp
            return (state * dec + cs, state)
        init = jnp.zeros((B, H, D, D), hidden_states.dtype)
        _, prev = lax.scan(step, init, (chunk_decay.transpose(2, 0, 1)[..., None, None], cstates.transpose(2, 0, 1, 3, 4)))
        prev = prev.transpose(1, 2, 0, 3, 4)
        y_inter = jnp.einsum('bhnid,bhnde->bhnie', qc * jnp.exp(G)[..., None], prev)
        y = (y_intra + y_inter).reshape(B, H, L, D).transpose(0, 2, 1, 3)
        rms = jnp.sqrt(jnp.mean(jnp.square(y), axis=-1, keepdims=True) + RMS_EPS)
        y = y / rms * gnorm_w
        gate = (hidden_states @ Wg.T).reshape(B, L, H, D)
        y = y * (gate * jax.nn.sigmoid(gate))
        return y.reshape(B, L, H * D) @ Wo.T

    def _L1_xattn_ref(hidden_states, cross_attention_states, attention_mask, Wq, Wk, Wv, Wo, q_norm_w, k_norm_w):
        import jax, jax.numpy as jnp
        import numpy as np
        B, Q, K, D = (1, 128, 6404, 512)
        H, KVH, HD = (32, 8, 128)
        GROUPS = H // KVH
        EPS = 1e-05

        def _rmsnorm(x, w):
            xf = x.astype(jnp.float32)
            var = jnp.mean(xf * xf, axis=-1, keepdims=True)
            return (xf * jax.lax.rsqrt(var + EPS)).astype(x.dtype) * w
        bsz, q_len, _ = hidden_states.shape
        kv_len = cross_attention_states.shape[1]
        q = (hidden_states @ Wq.T).reshape(bsz, q_len, H, HD).transpose(0, 2, 1, 3)
        k = (cross_attention_states @ Wk.T).reshape(bsz, kv_len, KVH, HD).transpose(0, 2, 1, 3)
        v = (cross_attention_states @ Wv.T).reshape(bsz, kv_len, KVH, HD).transpose(0, 2, 1, 3)
        q = _rmsnorm(q, q_norm_w)
        k = jnp.repeat(k, GROUPS, axis=1)
        v = jnp.repeat(v, GROUPS, axis=1)
        k = _rmsnorm(k, k_norm_w)
        scale = 1.0 / np.sqrt(HD)
        scores = jnp.einsum('bhqd,bhkd->bhqk', q, k) * scale
        scores = scores + attention_mask[:, :, :, :kv_len]
        probs = jax.nn.softmax(scores.astype(jnp.float32), axis=-1).astype(q.dtype)
        out = jnp.einsum('bhqk,bhkd->bhqd', probs, v)
        out = out.transpose(0, 2, 1, 3).reshape(bsz, q_len, H * HD)
        return out @ Wo.T

    def _L1_ffn_ref(x, weight, bias, lora_A, lora_B, lora_start_indices):
        import jax, jax.numpy as jnp
        import numpy as np
        LORA_RANK = 16
        LORA_ALPHA = 16
        LORA_SCALE = LORA_ALPHA / LORA_RANK
        y = jnp.einsum('bsd,od->bso', x, weight) + bias
        B = x.shape[0]
        seg = jnp.searchsorted(lora_start_indices, jnp.arange(B), side='right') - 1
        adapter_idx = jnp.clip(seg - 1, 0, lora_A.shape[0] - 1)
        A = lora_A[adapter_idx]
        Bw = lora_B[adapter_idx]
        lo = jnp.einsum('bsr,bor->bso', jnp.einsum('bsd,brd->bsr', x, A), Bw) * LORA_SCALE
        use_lora = (seg > 0)[:, None, None]
        return y + jnp.where(use_lora, lo, jnp.zeros((), dtype=y.dtype))
    x = _layernorm(x + _L0_attn_ref(x, L0_attn_wq, L0_attn_wk, L0_attn_wv, L0_attn_wo), axis=-1)
    x = _layernorm(x + _L0_xattn_ref(x, ctx_4096, L0_xattn_x1_scale, L0_xattn_x1_zp, L0_xattn_x2_scale, L0_xattn_x2_zp), axis=-1)
    x = _layernorm(x + _L0_ffn_ref(x, L0_ffn_W_res, L0_ffn_W_pre, L0_ffn_W_post, L0_ffn_H_res_base, L0_ffn_H_pre_base, L0_ffn_H_post_base, L0_ffn_gate, L0_ffn_W_branch), axis=-1)
    x = _layernorm(x + _L1_attn_ref(x, L1_attn_Wq, L1_attn_Wk, L1_attn_Wv, L1_attn_Wo, L1_attn_Wg, L1_attn_Win, L1_attn_dt_bias, L1_attn_A_log_bias, L1_attn_gnorm_w), axis=-1)
    x = _layernorm(x + _L1_xattn_ref(x, ctx_4096, mask_1x1xSxS2_ff0, L1_xattn_Wq, L1_xattn_Wk, L1_xattn_Wv, L1_xattn_Wo, L1_xattn_q_norm_w, L1_xattn_k_norm_w), axis=-1)
    x = _layernorm(x + _L1_ffn_ref(x, L1_ffn_weight, L1_ffn_bias, L1_ffn_lora_A, L1_ffn_lora_B, L1_ffn_lora_start_indices), axis=-1)
    return x

_drawn_inputs = setup_inputs


def setup_inputs(seed=0):
    import zlib

    import numpy as np

    out = dict(_drawn_inputs(seed))
    spreads = {'L0_ffn_H_post_base': (0.0, 0.8),
     'L1_attn_dt_bias': (0.0, 2.0),
     'L1_attn_gnorm_w': (1.0, 0.6),
     'L1_xattn_q_norm_w': (1.0, 0.6),
     'L1_xattn_k_norm_w': (1.0, 0.6)}
    factors = {'L0_ffn_W_pre': 3.727, 'L0_ffn_W_post': 3.379, 'L1_ffn_bias': 7.901}
    for name, (base, spread) in spreads.items():
        noise = np.random.default_rng([zlib.crc32(name.encode()), seed]).standard_normal(out[name].shape)
        drawn = base * np.exp(spread * noise) if base else spread * noise
        out[name] = jnp.asarray(drawn.astype(out[name].dtype))
    for name, factor in factors.items():
        out[name] = (out[name] * factor).astype(out[name].dtype)
    return out
```

```python
from contextlib import ExitStack
import math

import concourse.bass as bass
from concourse import mybir

F32 = mybir.dt.float32
BF16 = mybir.dt.bfloat16
I32 = mybir.dt.int32
ALU = mybir.AluOpType
ACT = mybir.ActivationFunctionType
AX = mybir.AxisListType

P = 128
B, L, D = 2, 256, 512
T = B * L
NT = T // P
KC = D // P
C = 512
CT = C // P
HD = 128
NG, GH = 8, 4
STEPS = GH * B
SCALE = 1.0 / math.sqrt(HD)
MASKED = -1.0e30
LN_EPS = 1e-5
SINK_ITERS = 50
SINK_BLOCK = 10
TAU = 0.1
STREAMS = 4
LORA, RANK = 3, 16
ROUND = 12582912.0


def decoder_kernel(nc, a, out):
    sems = {}
    with ExitStack() as ctx:
        def sb(name, shape, dt=F32):
            return ctx.enter_context(nc.sbuf_tensor(name, shape, dt))

        def sem(name):
            if name not in sems:
                sems[name] = ctx.enter_context(nc.semaphore(name))
            return sems[name]

        def due(value):
            return not isinstance(value, int) or value > 0

        x = sb("x", [P, NT, D])
        xT = sb("xT", [P, KC, T])
        wq = [sb(f"wq{i}", [P, KC, GH * HD]) for i in range(2)]
        wkv = [sb(f"wkv{i}", [P, KC, 2 * HD]) for i in range(2)]
        wo = [sb(f"wo{i}", [P, GH, D]) for i in range(2)]
        wg = [sb(f"wg{i}", [P, KC, GH * HD]) for i in range(2)]
        qT = [sb(f"qT{i}", [P, GH, T]) for i in range(2)]
        kT = [sb(f"kT{i}", [P, B * C]) for i in range(2)]
        v = [sb(f"v{i}", [P, B * CT, HD]) for i in range(2)]
        attT = [sb(f"attT{i}", [P, GH, T]) for i in range(2)]
        tmp = [sb(f"tmp{i}", [P, T]) for i in range(8)]
        logit = [sb(f"logit{i}", [P, 2, C]) for i in range(2)]
        prob = [sb(f"prob{i}", [P, 2, C]) for i in range(2)]
        probT = [sb(f"probT{i}", [P, CT, L]) for i in range(2)]
        ident = sb("ident", [P, P])
        identb = sb("identb", [P, P], BF16)
        cos = sb("cos", [P, L])
        sin = sb("sin", [P, L])
        keys = sb("keys", [P, P + L])
        causal = sb("causal", [P, P], BF16)
        rmax = [sb(f"rmax{i}", [P, 8]) for i in range(2)]
        rsum = [sb(f"rsum{i}", [P, 8]) for i in range(2)]
        stat = sb("stat", [P, NT, 6])
        mv = sb("mv", [P, NT, 2])
        lnr = sb("lnr", [P, 3, NT])
        half = sb("half", [P, NT])
        bank = [ctx.enter_context(nc.psum_tensor(f"bank{i}", [P, 512], F32)) for i in range(8)]
        q2 = sb("q2", [P, B * CT, D])
        quant = sb("quant", [P, 6])
        wmix = sb("wmix", [P, KC, 24])
        base = sb("base", [P, 24])
        gate = sb("gate", [P, 4])
        branch = sb("branch", [P, P])
        eye4 = sb("eye4", [P, 16])
        mix = sb("mix", [P, NT, 24])
        zlog = sb("zlog", [P, NT, 16])
        ztmp = sb("ztmp", [P, NT, 16])
        hres = sb("hres", [P, NT, 16])
        uv = sb("uv", [P, 2, 16])
        fac = sb("fac", [P, 2, 16])
        zsm = sb("zsm", [P, 6, 16])
        soft = sb("soft", [P, 3, 32])
        ssq = sb("ssq", [P, 3, NT])
        cols = sb("cols", [P, 10, NG * GH])
        gc = [sb(f"gc{i}", [P, 10, GH]) for i in range(2)]
        win = sb("win", [P, KC, NG * GH])
        hvec = sb("hvec", [NG * GH, 6])
        lower = sb("lower", [P, P])
        ones = sb("ones", [P, P])
        dvec = sb("dvec", [P, 4])
        yss = [sb(f"yss{i}", [P, 3, GH]) for i in range(2)]
        amask = sb("amask", [P, 2, C])
        kss = sb("kss", [P, 3, B * CT])
        qss = [sb(f"qss{i}", [P, 2, GH, NT]) for i in range(2)]
        loraA = sb("loraA", [P, KC, LORA * RANK])
        loraB = sb("loraB", [LORA * RANK + 1, D])
        low = sb("low", [64, T])
        starts = sb("starts", [LORA * RANK, 4], I32)
        lim = sb("lim", [LORA * RANK, 2])
        sel = sb("sel", [LORA * RANK, 16])
        sig = [sb(f"sig{i}", [P, GH * HD]) for i in range(2)]
        ysq = sb("ysq", [P, 2, GH * HD], BF16)
        def groups(engine, body, count=NG):
            for g in range(2):
                body(g, g)
            with engine.Fori(1, count // 2) as i:
                for p in range(2):
                    body(2 * i + p, p)

        def piped_groups(engine, body):
            for g in range(2):
                body(g, g, False)
            with engine.Fori(1, NG // 2 - 1) as i:
                for p in range(2):
                    body(2 * i + p, p, False)
            for g in range(NG - 2, NG):
                body(g, g % 2, g == NG - 1)

        def rope_psum_copies(eng, l, g, j, src):
            eng.wait_ge(sem(f"{l}_proj"), 5 * g + j + 1)
            if due(5 * g + j - 1):
                eng.wait_ge(sem(f"{l}_rope"), 5 * g + j - 1)
            eng.activation(tmp[j % 2][:, :], src[:, :], ACT.Copy)
            eng.activation(tmp[2 + j % 2][0:64, :], src[64:128, :], ACT.Copy)
            eng.activation(tmp[2 + j % 2][64:128, :], src[0:64, :], ACT.Copy).then_inc(sem(f"{l}_unproj"), 1)

        def rope_sin_part(eng, l, g, j):
            eng.wait_ge(sem(f"{l}_unproj"), 5 * g + j + 1)
            if due(5 * g + j - 1):
                eng.wait_ge(sem(f"{l}_rope"), 5 * g + j - 1)
            eng.tensor_tensor(halves(tmp[4 + j % 2]), halves(tmp[2 + j % 2]), per_batch(sin),
                              ALU.mult).then_inc(sem(f"{l}_sinp"), 1)

        def rope_sum(eng, l, g, j, dst):
            eng.wait_ge(sem(f"{l}_unproj"), 5 * g + j + 1)
            eng.tensor_tensor(halves(tmp[j % 2]), halves(tmp[j % 2]), per_batch(cos),
                              ALU.mult).then_inc(sem(f"{l}_cosp"), 1)
            eng.wait_ge(sem(f"{l}_cosp"), 5 * g + j + 1)
            eng.wait_ge(sem(f"{l}_sinp"), 5 * g + j + 1)
            eng.tensor_tensor(dst, tmp[j % 2][:, :], tmp[4 + j % 2][:, :],
                              ALU.add).then_inc(sem(f"{l}_rope"), 1)

        def halves(t):
            return t[:, :].rearrange("p (b l) -> p b l", b=B)

        def per_batch(t):
            return t[:, :].unsqueeze(1).broadcast_to([P, B, L])

        def project(eng, dst, w, cols, rhs, done=None):
            for c in range(KC):
                last = eng.matmul(dst, w[:, c, cols], rhs[:, c, :], start=(c == 0), stop=(c == KC - 1))
            if done:
                last.then_inc(sem(done), 1)

        def out_mm(eng, l, p, dst, t, heads, cnt=None):
            for h in heads:
                last = eng.matmul(dst[:, :], attT[p][:, h, t * P:(t + 1) * P], wo[p][:, h, :],
                                  start=(h == 0), stop=(h == GH - 1))
            if heads[-1] == GH - 1:
                last.then_inc(sem(f"{l}_out"), 1)

        def residual_add(eng, l, g, t, src):
            eng.wait_ge(sem(f"{l}_out"), 4 * g + t + 1)
            if due(4 * (g - 1) + t + 1):
                eng.wait_ge(sem(f"{l}_added"), 4 * (g - 1) + t + 1)
            eng.tensor_tensor(x[:, t, :], x[:, t, :], src[:, :], ALU.add).then_inc(sem(f"{l}_added"), 1)

        OUT_BANKS = [3, 4, 1, 0]

        def load_group(sp, l, g, p, extra=(), before=()):
            for name, per in before:
                sp.wait_ge(sem(name), per * (NG - 1 + g))
            for name, dst, src, used, per in (("wkv", wkv, a[f"{l}_wkv"], *(("kvproj", 4) if l == "x" else ("kvdone", 1))),
                                              ("wq", wq, a[f"{l}_wq"], "proj", 4 if l == "x" else 5), *extra,
                                              ("wo", wo, a[f"{l}_wo"], "out", 4)):
                if due(per * (g - 1)):
                    sp.wait_ge(sem(f"{l}_{used}"), per * (g - 1))
                sp.dma_start(dst[p][:, :, :], src[bass.ds(g, 1)].rearrange("a p c n -> (a p) c n"))\
                  .then_inc(sem(f"{l}_{name}{p}"), 16)

        def l0_tensor(pe):
            def loads(n, p):
                return 8 * (n - p) + 16

            def key(n, p):
                pe.wait_ge(sem(f"l0_wkv{p}"), loads(n, p))
                if due(5 * n):
                    pe.wait_ge(sem("l0_unproj"), 5 * n)
                project(pe, bank[0][:, :], wkv[p], slice(0, HD), xT, "l0_proj")

            def value(n, p):
                if due(8 * (n - 1)):
                    pe.wait_ge(sem("l0_headed"), 8 * (n - 1))
                for t in range(NT):
                    for c in range(KC):
                        last = pe.matmul(bank[2][:, t * P:(t + 1) * P], xT[:, c, t * P:(t + 1) * P],
                                         wkv[p][:, c, HD:2 * HD], start=(c == 0), stop=(c == KC - 1))
                last.then_inc(sem("l0_kvdone"), 1)

            def query(n, p, h):
                if h == 0:
                    pe.wait_ge(sem(f"l0_wq{p}"), loads(n, p))
                if due(5 * n + h):
                    pe.wait_ge(sem("l0_unproj"), 5 * n + h)
                project(pe, bank[(h + 1) % 2][:, :], wq[p], slice(h * HD, (h + 1) * HD), xT, "l0_proj")

            def body(g, p, last):
                turn = 8 * (g - p) + 16

                def scores(s):
                    h, b = s // B, s % B
                    dst = bank[3 + s % 2]
                    if due(8 * g + s - 1):
                        pe.wait_ge(sem("l0_scaled"), 8 * g + s - 1)
                    pe.wait_ge(sem("l0_rope"), 5 * g + 2 + h)
                    k0 = kT[p][:, b * L:b * L + P]
                    q0 = qT[p][:, h, b * L:b * L + P]
                    q1 = qT[p][:, h, b * L + P:(b + 1) * L]
                    pe.matmul(dst[:, 0:P], q0, k0, start=True, stop=False)
                    pe.matmul(dst[:, 0:P], identb[:, :], causal[:, :], start=False, stop=True)
                    pe.matmul(dst[:, P:3 * P], q1, kT[p][:, b * L:(b + 1) * L], start=True, stop=False,
                              skip_group_check=True)
                    pe.matmul(dst[:, 2 * P:3 * P], identb[:, :], causal[:, :], start=False, stop=True,
                              skip_group_check=True).then_inc(sem("l0_score"), 1)

                def turn_probs(s):
                    dst = bank[5 + s % 2]
                    pe.wait_ge(sem("l0_norm"), 8 * g + s + 1)
                    if due(8 * g + s - 1):
                        pe.wait_ge(sem("l0_turned"), 8 * g + s - 1)
                    src = prob[s % 2][:, 0, :]
                    for at in (0, P, 2 * P):
                        done = pe.transpose(dst[:, at:at + P], src[:, at:at + P], ident[:, :])
                    done.then_inc(sem("l0_turn"), 1)

                def values(s):
                    h, b = s // B, s % B
                    dst = bank[7 if s % 2 == 0 else 2]
                    pe.wait_ge(sem("l0_turned"), 8 * g + s + 1)
                    pe.wait_ge(sem("l0_v"), g + 1 if last else g + 2)
                    if due(8 * g + s - 1):
                        pe.wait_ge(sem("l0_headed"), 8 * g + s - 1)
                    pt = probT[s % 2][:, :, :].rearrange("p a b -> p (a b)")
                    pe.matmul(dst[:, 0:L], v[p][:, 2 * b, :], pt[:, 0:L], start=True, stop=False,
                              skip_group_check=True)
                    pe.matmul(dst[:, P:L], v[p][:, 2 * b + 1, :], pt[:, L:L + P], start=False, stop=True,
                              skip_group_check=True).then_inc(sem("l0_value"), 1)

                def pair(step, h):
                    step(B * h)
                    step(B * h + 1)

                n = None if last else g + 1
                if due(4 * g):
                    pe.wait_ge(sem("l0_added"), 4 * g)
                pair(scores, 0)
                if not last:
                    key(n, 1 - p)
                pair(turn_probs, 0)
                pair(scores, 1)
                if not last:
                    value(n, 1 - p)
                pair(values, 0)
                pair(turn_probs, 1)
                pair(scores, 2)
                if not last:
                    query(n, 1 - p, 0)
                pair(values, 1)
                if not last:
                    query(n, 1 - p, 1)
                pair(turn_probs, 2)
                pair(scores, 3)
                if not last:
                    query(n, 1 - p, 2)
                pair(values, 2)
                if not last:
                    query(n, 1 - p, 3)
                pair(turn_probs, 3)
                pe.wait_ge(sem(f"l0_wo{p}"), turn)
                pe.wait_ge(sem("l0_scaled"), 8 * g + 8)
                pe.wait_ge(sem("l0_headed"), 8 * g + 6)
                out_mm(pe, "l0", p, bank[3], 0, [0, 1, 2])
                pair(values, 3)
                out_mm(pe, "l0", p, bank[4], 1, [0, 1, 2])
                pe.wait_ge(sem("l0_headed"), 8 * g + 8)
                out_mm(pe, "l0", p, bank[3], 0, [3])
                out_mm(pe, "l0", p, bank[4], 1, [3])
                pe.wait_ge(sem("l0_unproj"), 5 * (g + 2) if not last else 5 * NG)
                out_mm(pe, "l0", p, bank[1], 2, [0, 1, 2, 3])
                out_mm(pe, "l0", p, bank[0], 3, [0, 1, 2, 3])

            key(0, 0)
            value(0, 0)
            for h in range(GH):
                query(0, 0, h)
            piped_groups(nc.tensor, body)

        def l0_scalar(act):
            def value(n, p):
                act.wait_ge(sem("l0_kvdone"), n + 1)
                if due(8 * (n - 1)):
                    act.wait_ge(sem("l0_value"), 8 * (n - 1))
                act.activation(v[p][:, 0:NT, :].rearrange("p a b -> p (a b)"), bank[2][:, :], ACT.Copy)\
                   .then_inc(sem("l0_v"), 1)

            def body(g, p, last):
                def exps(s):
                    act.wait_ge(sem("l0_max"), 8 * g + s + 1)
                    if due(8 * g + s - 1):
                        act.wait_ge(sem("l0_turn"), 8 * g + s - 1)
                    for n, (at, to) in enumerate(((0, P), (P, 3 * P))):
                        done = act.activation(prob[s % 2][:, 0, at:to], logit[s % 2][:, 0, at:to], ACT.Exp,
                                              bias=rmax[s % 2][:, n:n + 1],
                                              accum_out=rsum[s % 2][:, n:n + 1])
                    done.then_inc(sem("l0_exp"), 1)

                def turned(s):
                    act.wait_ge(sem("l0_turn"), 8 * g + s + 1)
                    if due(8 * g + s - 1):
                        act.wait_ge(sem("l0_value"), 8 * g + s - 1)
                    act.activation(probT[s % 2][:, :, :].rearrange("p a b -> p (a b)")[:, 0:3 * P],
                                   bank[5 + s % 2][:, 0:3 * P], ACT.Copy).then_inc(sem("l0_turned"), 1)

                def headed(s):
                    h, b = s // B, s % B
                    act.wait_ge(sem("l0_value"), 8 * g + s + 1)
                    act.activation(attT[p][:, h, b * L:(b + 1) * L], bank[7 if s % 2 == 0 else 2][:, 0:L],
                                   ACT.Copy).then_inc(sem("l0_headed"), 1)

                def pair(step, h):
                    step(B * h)
                    step(B * h + 1)

                n = None if last else g + 1
                pair(exps, 0)
                if not last:
                    rope_psum_copies(act, "l0", n, 0, bank[0])
                pair(turned, 0)
                pair(exps, 1)
                if not last:
                    value(n, 1 - p)
                if due(4 * (g - 1)):
                    act.wait_ge(sem("l0_out"), 4 * (g - 1))
                pair(headed, 0)
                pair(turned, 1)
                pair(exps, 2)
                if not last:
                    rope_psum_copies(act, "l0", n, 1, bank[1])
                pair(headed, 1)
                if not last:
                    rope_psum_copies(act, "l0", n, 2, bank[0])
                pair(turned, 2)
                pair(exps, 3)
                if not last:
                    rope_psum_copies(act, "l0", n, 3, bank[1])
                pair(headed, 2)
                if not last:
                    rope_psum_copies(act, "l0", n, 4, bank[0])
                pair(turned, 3)
                pair(headed, 3)

            rope_psum_copies(act, "l0", 0, 0, bank[0])
            value(0, 0)
            for h in range(GH):
                rope_psum_copies(act, "l0", 0, h + 1, bank[(h + 1) % 2])
            piped_groups(nc.scalar, body)

        def l0_gpsimd(pool):
            def body(g, p):
                for j in range(5):
                    rope_sin_part(pool, "l0", g, j)

            groups(nc.gpsimd, body)

        def l0_vector(dve):
            def body(g, p, last):
                def maxima(s):
                    dve.wait_ge(sem("l0_score"), 8 * g + s + 1)
                    if due(8 * g + s - 1):
                        dve.wait_ge(sem("l0_exp"), 8 * g + s - 1)
                    dve.tensor_tensor(logit[s % 2][:, 0, 0:3 * P], bank[3 + s % 2][:, 0:3 * P], keys[:, :],
                                      ALU.mult).then_inc(sem("l0_scaled"), 1)
                    dve.wait_ge(sem("l0_scaled"), 8 * g + s + 1)
                    for n, (at, to) in enumerate(((0, P), (P, 3 * P))):
                        done = dve.tensor_reduce(rmax[s % 2][:, n:n + 1], logit[s % 2][:, 0, at:to], AX.X,
                                                 ALU.max, negate=True)
                    done.then_inc(sem("l0_max"), 1)

                def normalise(s):
                    dve.wait_ge(sem("l0_exp"), 8 * g + s + 1)
                    dve.reciprocal(rsum[s % 2][:, 2:4], rsum[s % 2][:, 0:2]).then_inc(sem("l0_recip"), 1)
                    dve.wait_ge(sem("l0_recip"), 8 * g + s + 1)
                    for n, (at, to) in enumerate(((0, P), (P, 3 * P))):
                        done = dve.tensor_scalar(prob[s % 2][:, 0, at:to], prob[s % 2][:, 0, at:to],
                                                 rsum[s % 2][:, 2 + n:3 + n], None, ALU.mult)
                    done.then_inc(sem("l0_norm"), 1)

                def pair(step, h):
                    step(B * h)
                    step(B * h + 1)

                n = None if last else g + 1
                pair(maxima, 0)
                pair(normalise, 0)
                pair(maxima, 1)
                if not last:
                    if due(8 * (n - 1)):
                        dve.wait_ge(sem("l0_score"), 8 * (n - 1))
                    rope_sum(dve, "l0", n, 0, kT[1 - p][:, 0:T])
                pair(normalise, 1)
                pair(maxima, 2)
                pair(normalise, 2)
                if not last:
                    rope_sum(dve, "l0", n, 1, qT[1 - p][:, 0, :])
                pair(maxima, 3)
                if not last:
                    rope_sum(dve, "l0", n, 2, qT[1 - p][:, 1, :])
                pair(normalise, 3)
                if not last:
                    rope_sum(dve, "l0", n, 3, qT[1 - p][:, 2, :])
                    rope_sum(dve, "l0", n, 4, qT[1 - p][:, 3, :])
                for t in range(NT):
                    residual_add(dve, "l0", g, t, bank[OUT_BANKS[t]])
                if isinstance(g, int) and g == 1:
                    dve.wait_ge(sem("ld_ctx"), 16)
                    for t in range(0, B * CT, 4):
                        fake_quant(dve, q2[:, t:t + 4, :], 1, "quant_c", t)

            rope_sum(dve, "l0", 0, 0, kT[0][:, 0:T])
            for h in range(GH):
                rope_sum(dve, "l0", 0, h + 1, qT[0][:, h, :])
            piped_groups(nc.vector, body)

        TURN_BANKS = [5, 6, 7, 2]

        def ln_vector(dve, n, after=None):
            for t in range(NT):
                if after:
                    dve.wait_ge(sem(after[0]), after[1] + t)
                dve.bn_stats(stat[:, t, :], x[:, t, :]).then_inc(sem("ln_stat"), 1)
            for t in range(NT):
                dve.wait_ge(sem("ln_stat"), NT * n + t + 1)
                dve.bn_aggr(mv[:, t, :], stat[:, t, :]).then_inc(sem("ln_aggr"), 1)
            dve.wait_ge(sem("ln_aggr"), NT * (n + 1))
            dve.tensor_scalar(lnr[:, 0, :], mv[:, :, 1], LN_EPS, None, ALU.add).then_inc(sem("ln_var"), 1)
            dve.wait_ge(sem("ln_rstd"), n + 1)
            for t in range(NT):
                dve.tensor_scalar(x[:, t, :], x[:, t, :], mv[:, t, 0:1], lnr[:, 1, t:t + 1],
                                  ALU.subtract, ALU.mult).then_inc(sem("ln_x"), 1)

        def ln_gpsimd(pool, n):
            pool.wait_ge(sem("ln_var"), n + 1)
            pool.wait_ge(sem("half"), 1)
            pool.tensor_tensor(lnr[:, 1, :], lnr[:, 0, :], half[:, :], ALU.pow).then_inc(sem("ln_rstd"), 1)

        def ln_tensor(pe, n):
            for t in range(NT):
                pe.wait_ge(sem("ln_x"), NT * n + t + 1)
                for c in range(KC):
                    last = pe.transpose(bank[TURN_BANKS[t]][:, c * P:(c + 1) * P], x[:, t, c * P:(c + 1) * P],
                                        ident[:, :])
                last.then_inc(sem("ln_turn"), 1)

        def ln_scalar(act, n):
            for t in range(NT):
                act.wait_ge(sem("ln_turn"), NT * n + t + 1)
                act.activation(xT[:, :, t * P:(t + 1) * P],
                               bank[TURN_BANKS[t]][:, :].rearrange("p (c t) -> p c t", c=KC), ACT.Copy)\
                   .then_inc(sem("ln_xT"), 1)

        def fake_quant(eng, t, k, done, seen=0):
            s, z, r = quant[:, 2 * k:2 * k + 1], quant[:, 2 * k + 1:2 * k + 2], quant[:, 4 + k:5 + k]
            src, dst = t if isinstance(t, tuple) else (t, t)
            for n, (a0, a1, o0, o1) in enumerate(((r, z, ALU.mult, ALU.add), (0.0, 255.0, ALU.max, ALU.min),
                                                  (ROUND, ROUND, ALU.add, ALU.subtract),
                                                  (z, s, ALU.subtract, ALU.mult))):
                if n:
                    if due(seen + n):
                        eng.wait_ge(sem(done), seen + n)
                eng.tensor_scalar(dst, src if n == 0 else dst, a0, a1, o0, o1).then_inc(sem(done), 1)

        def cross_vector(dve):
            q1 = attT[0]
            for t in range(NT):
                dve.wait_ge(sem("ln_xT"), t + 1)
                cols = slice(t * P, (t + 1) * P)
                fake_quant(dve, (xT[:, :, cols], q1[:, :, cols]), 0, "quant_x", 4 * t)
            for t in range(NT):
                dve.wait_ge(sem("cross"), t + 1)
                dve.tensor_tensor(x[:, t, :], x[:, t, :], bank[OUT_BANKS[t]][:, :], ALU.add)\
                   .then_inc(sem("cross_added"), 1)

        def cross_tensor(pe):
            q1 = attT[0]
            pe.wait_ge(sem("quant_c"), B * CT)
            for t in range(NT):
                pe.wait_ge(sem("quant_x"), 4 * (t + 1))
                for c in range(KC):
                    last = pe.matmul(bank[OUT_BANKS[t]][:, :], q1[:, c, t * P:(t + 1) * P],
                                     q2[:, (t // 2) * CT + c, :], start=(c == 0), stop=(c == KC - 1))
                last.then_inc(sem("cross"), 1)

        BRANCH_BANKS = [1, 3, 4, 5]

        def mix_tensor(pe):
            for t in range(NT):
                pe.wait_ge(sem("ln_xT"), NT * 1 + t + 1)
                for c in range(KC):
                    last = pe.matmul(bank[0][:, t * 24:(t + 1) * 24], xT[:, c, t * P:(t + 1) * P], wmix[:, c, :],
                                     start=(c == 0), stop=(c == KC - 1))
            last.then_inc(sem("mix_logits"), 1)
            for t in range(NT):
                for c in range(STREAMS):
                    last = pe.matmul(bank[BRANCH_BANKS[t]][:, c * P:(c + 1) * P], xT[:, c, t * P:(t + 1) * P],
                                     branch[:, :], start=True, stop=True)
                last.then_inc(sem("branch"), 1)

        def mix_scalar(act):
            for t in range(NT):
                act.wait_ge(sem("ln_x"), NT * 1 + t + 1)
                act.activation(tmp[t][:, :], x[:, t, :], ACT.Square, accum_out=ssq[:, 0, t:t + 1])\
                   .then_inc(sem("mix_ssq"), 1)
            ln_scalar(act, 1)

        def mix_gpsimd(pool):
            pool.wait_ge(sem("mix_mean"), 1)
            pool.tensor_tensor(ssq[:, 2, :], ssq[:, 1, :], half[:, :], ALU.pow).then_inc(sem("mix_rms"), 1)

        def rows4(t, j_outer=False):
            if j_outer:
                return t.rearrange("p t (i j) -> p t j i", i=4)
            return t.rearrange("p t (i j) -> p t i j", i=4)

        def vec4(t):
            return t.rearrange("p (t i) -> p t i", t=NT)

        def mix_vector(dve):
            tally = [0]

            def step(ins):
                tally[0] += 1
                ins.then_inc(sem("mix_step"), 1)
                dve.wait_ge(sem("mix_step"), tally[0])

            def over_rows(v):
                return vec4(v).unsqueeze(3).broadcast_to([P, NT, 4, 4])

            def over_cols(v):
                return vec4(v).unsqueeze(2).broadcast_to([P, NT, 4, 4])

            dve.wait_ge(sem("mix_ssq"), NT)
            dve.tensor_scalar(ssq[:, 1, :], ssq[:, 0, :], 1.0 / D, 1.1920929e-07, ALU.mult, ALU.add)\
               .then_inc(sem("mix_mean"), 1)
            dve.wait_ge(sem("mix_rms"), 1)
            dve.wait_ge(sem("mix_logits"), 1)
            for t in range(NT):
                last = dve.scalar_tensor_tensor(mix[:, t, :], bank[0][:, t * 24:(t + 1) * 24], ssq[:, 2, t:t + 1],
                                                base[:, :], ALU.mult, ALU.add)
            step(last)
            pp = mix[:, :, 16:24].rearrange("p t (k n) -> p t k n", k=2)
            e = soft[:, 0, :].rearrange("p (t k n) -> p t k n", t=NT, k=2)
            m = soft[:, 1, 0:8].rearrange("p (t k) -> p t k", t=NT)
            mb = m.unsqueeze(3).broadcast_to([P, NT, 2, 4])
            step(dve.tensor_reduce(m, pp, AX.X, ALU.max))
            dve.tensor_tensor(e, pp, mb, ALU.subtract).then_inc(sem("soft_in"), 1)
            z4, t4, h4 = rows4(zlog[:, :, :]), rows4(ztmp[:, :, :]), rows4(hres[:, :, :])
            step(dve.tensor_scalar(zlog[:, :, :], mix[:, :, 0:16], 1.0 / TAU, None, ALU.mult))
            for side in range(2):
                src = z4 if side == 0 else h4
                lines = src if side == 0 else rows4(hres[:, :, :], True)
                wide = over_rows if side == 0 else over_cols
                mx, ls = zsm[:, 0, :], zsm[:, 1, :]
                step(dve.tensor_reduce(vec4(mx), lines, AX.X, ALU.max))
                dve.tensor_tensor(t4, src, wide(mx), ALU.subtract).then_inc(sem("sink_in"), 1)
                dve.wait_ge(sem("sink_exp"), side + 1)
                t_lines = t4 if side == 0 else rows4(ztmp[:, :, :], True)
                dve.tensor_reduce(vec4(zsm[:, 2, :]), t_lines, AX.X, ALU.add).then_inc(sem("sink_sum"), 1)
                dve.wait_ge(sem("sink_ln"), side + 1)
                step(dve.tensor_tensor(ls, ls, mx, ALU.add))
                step(dve.tensor_scalar(uv[:, side, :], ls, -1.0, None, ALU.mult))
                last = dve.tensor_tensor(h4, src, wide(uv[:, side, :]), ALU.add)
                if side == 0:
                    step(last)
                else:
                    last.then_inc(sem("sink_zuv"), 1)
            dve.wait_ge(sem("soft_exp"), 1)
            step(dve.tensor_reduce(soft[:, 1, 8:16].rearrange("p (t k) -> p t k", t=NT), e, AX.X, ALU.add))
            step(dve.reciprocal(soft[:, 1, 16:24], soft[:, 1, 8:16]))
            rb = soft[:, 1, 16:24].rearrange("p (t k) -> p t k", t=NT).unsqueeze(3).broadcast_to([P, NT, 2, 4])
            step(dve.tensor_tensor(e, e, rb, ALU.mult))
            dve.wait_ge(sem("gate_exp"), 1)
            step(dve.tensor_scalar(gate[:, 2:3], gate[:, 1:2], 1.0, None, ALU.add))
            step(dve.reciprocal(gate[:, 3:4], gate[:, 2:3]))

            first = SINK_BLOCK - 1
            dve.wait_ge(sem("sink_h"), 1)
            sink_rounds(dve, "dve", 0, first, h4, over_rows, over_cols)
            with nc.vector.Fori(0, SINK_ITERS // SINK_BLOCK - 1) as i:
                dve.wait_ge(sem("fac_ln"), i + 1)
                dve.tensor_tensor(uv[:, :, :], uv[:, :, :], zsm[:, 0:2, :], ALU.add).then_inc(sem("absorb"), 1)
                dve.wait_ge(sem("absorb"), i * 3 + 1)
                dve.tensor_tensor(t4, z4, over_rows(uv[:, 0, :]), ALU.add).then_inc(sem("absorb"), 1)
                dve.wait_ge(sem("absorb"), i * 3 + 2)
                dve.tensor_tensor(t4, t4, over_cols(uv[:, 1, :]), ALU.add).then_inc(sem("absorb"), 1)
                dve.wait_ge(sem("sink_h"), i + 2)
                sink_rounds(dve, "dve", i * SINK_BLOCK + first, SINK_BLOCK, h4, over_rows, over_cols)
            dve.wait_ge(sem("norm4"), 6 * (SINK_ITERS - 1))
            step(dve.tensor_scalar(gate[:, 2:3], gate[:, 3:4], -1.0, 2.0, ALU.mult, ALU.add))
            step(dve.tensor_scalar(zsm[:, 0, :], eye4[:, :], gate[:, 2:3], None, ALU.mult))
            step(dve.scalar_tensor_tensor(hres[:, :, :], hres[:, :, :], gate[:, 3:4],
                                          zsm[:, 0, :].unsqueeze(1).broadcast_to([P, NT, 16]), ALU.mult, ALU.add))
            count = [0]

            def mark(ins):
                count[0] += 1
                ins.then_inc(sem("mixed"), 1)
                return count[0]

            for t in range(NT):
                y, acc = tmp[4 + t], qT[0][:, t, :]
                dve.wait_ge(sem("branch"), t + 1)
                y_at = 0
                at = [0] * STREAMS
                for j in range(STREAMS):
                    xj = x[:, t, j * P:(j + 1) * P]
                    yj = bank[BRANCH_BANKS[t]][:, j * P:(j + 1) * P]
                    pre = soft[:, 0, t * 8 + j:t * 8 + j + 1]
                    if due(y_at):
                        dve.wait_ge(sem("mixed"), y_at)
                    y_at = mark(dve.tensor_scalar(y[:, 0:P], yj, pre, None, ALU.mult) if j == 0 else
                                dve.scalar_tensor_tensor(y[:, 0:P], yj, pre, y[:, 0:P], ALU.mult, ALU.add))
                    for i in range(STREAMS):
                        acci = acc[:, i * P:(i + 1) * P]
                        h = hres[:, t, i * 4 + j:i * 4 + j + 1]
                        if due(at[i]):
                            dve.wait_ge(sem("mixed"), at[i])
                        at[i] = mark(dve.tensor_scalar(acci, xj, h, None, ALU.mult) if j == 0 else
                                     dve.scalar_tensor_tensor(acci, xj, h, acci, ALU.mult, ALU.add))
                if due(count[0]):
                    dve.wait_ge(sem("mixed"), count[0])
                for i in range(STREAMS):
                    mark(dve.scalar_tensor_tensor(x[:, t, i * P:(i + 1) * P], y[:, 0:P],
                                                  soft[:, 0, t * 8 + 4 + i:t * 8 + 5 + i],
                                                  acc[:, i * P:(i + 1) * P], ALU.mult, ALU.add))

        def sink_rounds(eng, who, r0, n, h4=None, over_rows=None, over_cols=None):
            for k in range(n):
                for side in range(2):
                    half_step = 2 * (r0 + k) + side
                    factor = zsm[:, 4 + side, :]
                    if who == "pool":
                        eng.wait_ge(sem("norm4"), 3 * half_step + 2)
                        if k:
                            if due(half_step):
                                eng.wait_ge(sem("gathered"), half_step)
                            eng.tensor_tensor(fac[:, side, :], fac[:, side, :], factor, ALU.mult)\
                               .then_inc(sem("gathered"), 1)
                        else:
                            eng.tensor_tensor(fac[:, side, :], factor, ones[:, 0:16], ALU.mult).then_inc(sem("gathered"), 1)
                        continue
                    lines = rows4(hres[:, :, :], side == 1)
                    wide = over_rows if side == 0 else over_cols
                    if due(3 * half_step):
                        eng.wait_ge(sem("norm4"), 3 * half_step)
                    eng.tensor_reduce(vec4(zsm[:, 2 + side, :]), lines, AX.X, ALU.add).then_inc(sem("norm4"), 1)
                    eng.wait_ge(sem("norm4"), 3 * half_step + 1)
                    if due(half_step - 1):
                        eng.wait_ge(sem("gathered"), half_step - 1)
                    eng.reciprocal(factor, zsm[:, 2 + side, :]).then_inc(sem("norm4"), 1)
                    eng.wait_ge(sem("norm4"), 3 * half_step + 2)
                    eng.tensor_tensor(h4, h4, wide(factor), ALU.mult).then_inc(sem("norm4"), 1)

        def sink_scalar(act):
            z, h = ztmp[:, :, :], hres[:, :, :]
            act.wait_ge(sem("soft_in"), 1)
            act.activation(soft[:, 0, :], soft[:, 0, :], ACT.Exp).then_inc(sem("soft_exp"), 1)
            act.activation(gate[:, 1:2], gate[:, 1:2], ACT.Exp).then_inc(sem("gate_exp"), 1)
            for side in range(2):
                act.wait_ge(sem("sink_in"), side + 1)
                act.activation(z, z, ACT.Exp).then_inc(sem("sink_exp"), 1)
                act.wait_ge(sem("sink_sum"), side + 1)
                act.activation(zsm[:, 1, :], zsm[:, 2, :], ACT.Ln).then_inc(sem("sink_ln"), 1)
            act.wait_ge(sem("sink_zuv"), 1)
            act.activation(h, h, ACT.Exp).then_inc(sem("sink_h"), 1)
            with nc.scalar.Fori(0, SINK_ITERS // SINK_BLOCK - 1) as i:
                if due(i * (2 * SINK_BLOCK) + 2 * (SINK_BLOCK - 1)):
                    act.wait_ge(sem("gathered"), i * (2 * SINK_BLOCK) + 2 * (SINK_BLOCK - 1))
                act.activation(zsm[:, 0:2, :], fac[:, :, :], ACT.Ln).then_inc(sem("fac_ln"), 1)
                act.wait_ge(sem("absorb"), i * 3 + 3)
                act.activation(h, z, ACT.Exp).then_inc(sem("sink_h"), 1)

        def sink_gpsimd(pool):
            sink_rounds(pool, "pool", 0, SINK_BLOCK - 1)
            with nc.gpsimd.Fori(0, SINK_ITERS // SINK_BLOCK - 1) as i:
                pool.wait_ge(sem("fac_ln"), i + 1)
                sink_rounds(pool, "pool", i * SINK_BLOCK + SINK_BLOCK - 1, SINK_BLOCK)

        def row(k):
            return qT[k // 4][0:NG * GH, k % 4, :]

        def grow(b, p):
            return (logit if p == 0 else prob)[b][:, :, :].rearrange("p a b -> p (a b)")\
                .rearrange("p (h q) -> p h q", h=GH)

        def decay(b, blk):
            flat = probT[b][:, :, :].rearrange("p a b -> p (a b)")
            return flat[:, blk * 512:(blk + 1) * 512] if blk < 2 else tmp[6 + b][:, :]

        L1_OUT = [1, 0, 3, 4]

        def dt_tensor(pe):
            pe.wait_ge(sem("ld_l1"), 16 * 5)
            pe.wait_ge(sem("ln_xT"), NT * 3)
            for c in range(KC):
                last = pe.matmul(bank[0][0:NG * GH, :], win[:, c, :], xT[:, c, :], start=(c == 0), stop=(c == KC - 1))
            last.then_inc(sem("dt"), 1)
            pe.wait_ge(sem("dtcols"), 1)
            for n in range(10):
                src, at = ((row(6), n * P), (row(5), (n - 4) * P), (row(7), (n - 8) * L))[(n >= 4) + (n >= 8)]
                last = pe.transpose(bank[1][:, n * 32:(n + 1) * 32], src[:, at:at + P], ident[0:32, 0:32])
            last.then_inc(sem("dt_turn"), 1)

        def dt_scalar(act):
            act.wait_ge(sem("ld_l1"), 16 * 5)
            act.activation(hvec[:, 2:3], hvec[:, 1:2], ACT.Exp).then_inc(sem("A_exp"), 1)
            act.wait_ge(sem("dt_abs"), 1)
            act.activation(row(1), row(1), ACT.Exp).then_inc(sem("dt_exp"), 1)
            act.wait_ge(sem("dt_u"), 1)
            act.activation(row(4), row(2), ACT.Ln).then_inc(sem("dt_ln"), 1)
            act.wait_ge(sem("dt_G"), 1)
            for b in range(B):
                last = act.activation(row(7)[:, b * L:b * L + P], row(6)[:, b * L:b * L + P], ACT.Exp, scale=-1.0,
                                      bias=row(6)[:, b * L + P - 1:b * L + P])
            last.then_inc(sem("dt_last"), 1)
            act.wait_ge(sem("dt_turn"), 1)
            act.activation(cols[:, :, :].rearrange("p a b -> p (a b)"), bank[1][:, 0:320], ACT.Copy)\
               .then_inc(sem("dt_cols"), 1)

        def dt_vector(dve):
            tally = [0]

            def step(ins):
                tally[0] += 1
                ins.then_inc(sem("dt_step"), 1)
                dve.wait_ge(sem("dt_step"), tally[0])

            dve.wait_ge(sem("A_exp"), 1)
            step(dve.tensor_scalar(hvec[:, 3:4], hvec[:, 2:3], -1.0, None, ALU.mult))
            dve.wait_ge(sem("dt"), 1)
            step(dve.tensor_scalar(row(0), bank[0][0:NG * GH, :], hvec[:, 0:1], None, ALU.add))
            dve.scalar_tensor_tensor(row(1), row(0), -1.0, row(0), ALU.mult, ALU.min).then_inc(sem("dt_abs"), 1)
            dve.wait_ge(sem("dt_exp"), 1)
            dve.tensor_scalar(row(2), row(1), 1.0, None, ALU.add).then_inc(sem("dt_u"), 1)
            dve.wait_ge(sem("dt_u"), 1)
            step(dve.scalar_tensor_tensor(row(3), row(2), -1.0, row(1), ALU.add, ALU.subtract))
            step(dve.scalar_tensor_tensor(row(3), row(0), 0.0, row(3), ALU.max, ALU.subtract))
            dve.wait_ge(sem("dt_ln"), 1)
            step(dve.tensor_tensor(row(5), row(3), row(4), ALU.add))
            step(dve.tensor_scalar(row(0), row(5), hvec[:, 3:4], None, ALU.mult))
            for t in range(NT):
                tile = slice(t * P, (t + 1) * P)
                last = dve.tensor_tensor_scan(row(6)[:, tile], ones[0:NG * GH, :], row(0)[:, tile], 0.0,
                                              ALU.mult, ALU.add)
            last.then_inc(sem("dt_G"), 1)
            dve.wait_ge(sem("dt_last"), 1)
            for b in range(B):
                last = dve.tensor_tensor(row(7)[:, b * L:b * L + P], row(7)[:, b * L:b * L + P],
                                         row(5)[:, b * L:b * L + P], ALU.mult)
            last.then_inc(sem("dtcols"), 1)

        def l1_load_rows(sp, g, p):
            for b in range(B):
                if due(2 * (g - 1)):
                    sp.wait_ge(sem("l1_dexp"), 2 * (g - 1))
                src = a["g_rows"][bass.ds(GH * g, GH), b * L:(b + 1) * L]
                sp.dma_start(grow(b, p), src.unsqueeze(0).broadcast_to([P, GH, L])).then_inc(sem(f"l1_rows{b}{p}"), 16)

        def l1_tensor(pe):
            def body(g, p):
                turn = 8 * (g - p) + 16

                def q(h, waits):
                    if due(waits):
                        pe.wait_ge(sem("l1_unproj"), waits)
                    project(pe, bank[(h + 1) % 2][:, :], wq[p], slice(h * HD, (h + 1) * HD), xT, "l1_proj")

                def gates(t):
                    if t < 2:
                        pe.wait_ge(sem("l1_unproj"), 5 * g + 4 + t)
                    else:
                        if due(4 * g + t - 1):
                            pe.wait_ge(sem("l1_gclamp"), 4 * g + t - 1)
                    for c in range(KC):
                        last = pe.matmul(bank[(t + 1) % 2][:, :], xT[:, c, t * P:(t + 1) * P], wg[p][:, c, :],
                                         start=(c == 0), stop=(c == KC - 1))
                    last.then_inc(sem("l1_gate"), 1)

                def scores(b):
                    for n, (kt, qt) in enumerate(((0, 0), (0, 1), (1, 1))):
                        if due(6 * g + 3 * (b - 1) + n + 1):
                            pe.wait_ge(sem("l1_w"), 6 * g + 3 * (b - 1) + n + 1)
                        pe.matmul(bank[3 + n][:, :], kT[p][:, b * L + kt * P:b * L + (kt + 1) * P],
                                  qT[p][:, :, b * L + qt * P:b * L + (qt + 1) * P], start=True, stop=True)\
                          .then_inc(sem("l1_score"), 1)

                def outputs(b):
                    pe.wait_ge(sem("l1_v"), g + 1)
                    for c in range(2):
                        n = 2 * b + c
                        pe.wait_ge(sem("l1_w"), 6 * g + 3 * b + (1 if c == 0 else 3))
                        if due(4 * g + n - 1):
                            pe.wait_ge(sem("l1_z"), 4 * g + n - 1)
                        for h in range(GH):
                            hs = slice(h * P, (h + 1) * P)
                            last = pe.matmul(bank[6 + c][:, hs], decay(b, c)[:, hs], v[p][:, 2 * b, :],
                                             start=True, stop=(c == 0))
                            if c:
                                last = pe.matmul(bank[6 + c][:, hs], decay(b, 2)[:, hs], v[p][:, 2 * b + 1, :],
                                                 start=False, stop=True)
                        last.then_inc(sem("l1_y"), 1)

                def turn_z(n):
                    pe.wait_ge(sem("l1_z"), 4 * g + n + 1)
                    pe.wait_ge(sem("l1_headed"), 4 * g + n)
                    for h in range(GH):
                        last = pe.transpose(bank[2][:, h * P:(h + 1) * P],
                                            q2[:, 4 * p + n, h * P:(h + 1) * P], ident[:, :])
                    last.then_inc(sem("l1_zturn"), 1)

                def out_tile(t):
                    pe.wait_ge(sem("l1_headed"), 4 * g + t + 1)
                    out_mm(pe, "l1", p, bank[L1_OUT[t]], t, [0, 1, 2, 3])

                pe.wait_ge(sem(f"l1_wkv{p}"), turn)
                if due(4 * (g - 1) + 2):
                    pe.wait_ge(sem("l1_added"), 4 * (g - 1) + 2)
                project(pe, bank[0][:, :], wkv[p], slice(0, HD), xT, "l1_proj")
                if due(4 * g):
                    pe.wait_ge(sem("l1_headed"), 4 * g)
                for t in range(NT):
                    for c in range(KC):
                        last = pe.matmul(bank[2][:, t * P:(t + 1) * P], xT[:, c, t * P:(t + 1) * P],
                                         wkv[p][:, c, HD:2 * HD], start=(c == 0), stop=(c == KC - 1))
                last.then_inc(sem("l1_kvdone"), 1)
                pe.wait_ge(sem(f"l1_wq{p}"), turn)
                q(0, 0)
                q(1, 5 * g + 1)
                q(2, 5 * g + 2)
                q(3, 5 * g + 3)
                pe.wait_ge(sem(f"l1_wg{p}"), turn)
                gates(0)
                gates(1)
                pe.wait_ge(sem("l1_rope"), 5 * g + 5)
                if due(4 * g):
                    pe.wait_ge(sem("l1_added"), 4 * g)
                scores(0)
                gates(2)
                gates(3)
                outputs(0)
                scores(1)
                pe.wait_ge(sem("l1_v"), g + 1)
                turn_z(0)
                turn_z(1)
                pe.wait_ge(sem(f"l1_wo{p}"), turn)
                pe.wait_ge(sem("l1_gclamp"), 4 * g + 4)
                out_tile(0)
                outputs(1)
                out_tile(1)
                turn_z(2)
                turn_z(3)
                pe.wait_ge(sem("l1_w"), 6 * g + 6)
                out_tile(2)
                out_tile(3)

            pe.wait_ge(sem("dt_cols"), 1)
            groups(nc.tensor, body)

        def l1_scalar(act):
            def body(g, p):
                def decays(b):
                    act.wait_ge(sem(f"l1_rows{b}{p}"), 8 * (g - p) + 16)
                    if due(4 * (g - 1) + 2 * b + 2):
                        act.wait_ge(sem("l1_y"), 4 * (g - 1) + 2 * b + 2)
                    act.activation(decay(b, 1).rearrange("p (h q) -> p h q", h=GH), grow(b, p)[:, :, P:L], ACT.Exp)
                    act.wait_ge(sem("l1_dsub"), 2 * g + b + 1)
                    act.activation(decay(b, 0), decay(b, 0), ACT.Exp)
                    act.activation(decay(b, 2), decay(b, 2), ACT.Exp).then_inc(sem("l1_dexp"), 1)

                def sigmoid(t):
                    s = sig[t % 2]
                    act.wait_ge(sem("l1_gclamp"), 4 * g + t + 1)
                    if due(4 * g + t - 1):
                        act.wait_ge(sem("l1_sil"), 4 * g + t - 1)
                    at = 3 * (4 * g + t)
                    act.activation(s[:, :], q2[:, 4 * p + t, :], ACT.Exp, scale=-1.0).then_inc(sem("l1_sig"), 1)
                    act.wait_ge(sem("l1_sig"), at + 1)
                    act.activation(s[:, :], s[:, :], ACT.Ln, bias=ones[:, 0:1]).then_inc(sem("l1_sig"), 1)
                    act.wait_ge(sem("l1_sig"), at + 2)
                    act.activation(s[:, :], s[:, :], ACT.Exp, scale=-1.0).then_inc(sem("l1_sig"), 1)

                def squares(n):
                    act.wait_ge(sem("l1_y"), 4 * g + n + 1)
                    if due(4 * g + n - 1):
                        act.wait_ge(sem("l1_yrms"), 4 * g + n - 1)
                    for h in range(GH):
                        last = act.activation(ysq[:, n % 2, h * P:(h + 1) * P], bank[6 + n % 2][:, h * P:(h + 1) * P],
                                              ACT.Square, accum_out=yss[n % 2][:, 0, h:h + 1])
                    last.then_inc(sem("l1_ysq"), 1)

                def headed(n):
                    act.wait_ge(sem("l1_zturn"), 4 * g + n + 1)
                    act.activation(attT[p][:, :, n * P:(n + 1) * P],
                                   bank[2][:, :].rearrange("p (h t) -> p h t", h=GH), ACT.Copy,
                                   scale=dvec[:, 0:1]).then_inc(sem("l1_headed"), 1)

                rope_psum_copies(act, "l1", g, 0, bank[0])
                act.wait_ge(sem("l1_kvdone"), g + 1)
                if due(4 * (g - 1)):
                    act.wait_ge(sem("l1_y"), 4 * (g - 1))
                act.activation(v[p][:, 0:NT, :].rearrange("p a b -> p (a b)"), bank[2][:, :], ACT.Copy)\
                   .then_inc(sem("l1_v"), 1)
                for j in range(4):
                    rope_psum_copies(act, "l1", g, j + 1, bank[(j + 1) % 2])
                decays(0)
                sigmoid(0)
                sigmoid(1)
                decays(1)
                sigmoid(2)
                sigmoid(3)
                squares(0)
                squares(1)
                if due(4 * (g - 1)):
                    act.wait_ge(sem("l1_out"), 4 * (g - 1))
                headed(0)
                headed(1)
                squares(2)
                squares(3)
                headed(2)
                headed(3)

            groups(nc.scalar, body)

        def l1_gpsimd(pool):
            def body(g, p):
                for j in range(5):
                    rope_sin_part(pool, "l1", g, j)
                for t in range(NT):
                    pool.wait_ge(sem("l1_sig"), 3 * (4 * g + t + 1))
                    pool.tensor_tensor(q2[:, 4 * p + t, :], q2[:, 4 * p + t, :], sig[t % 2][:, :],
                                       ALU.mult).then_inc(sem("l1_sil"), 1)
                for n in range(NT):
                    pool.wait_ge(sem("l1_ymean"), 4 * g + n + 1)
                    if due(4 * g + n - 1):
                        pool.wait_ge(sem("l1_z"), 4 * g + n - 1)
                    pool.tensor_tensor(yss[n % 2][:, 2, :], yss[n % 2][:, 1, :], half[:, :], ALU.pow)\
                        .then_inc(sem("l1_yrms"), 1)

            groups(nc.gpsimd, body)

        def l1_vector(dve):
            def body(g, p):
                def exponents(b):
                    dve.wait_ge(sem(f"l1_rows{b}{p}"), 8 * (g - p) + 16)
                    if due(4 * (g - 1) + 2 * b + 2):
                        dve.wait_ge(sem("l1_y"), 4 * (g - 1) + 2 * b + 2)
                    for c in range(2):
                        for h in range(GH):
                            last = dve.scalar_tensor_tensor(decay(b, 2 * c)[:, h * P:(h + 1) * P],
                                                            grow(b, p)[:, h, c * P:(c + 1) * P],
                                                            gc[p][:, 2 * b + c, h:h + 1], lower[:, :],
                                                            ALU.subtract, ALU.add)
                    last.then_inc(sem("l1_dsub"), 1)

                def clamp(t):
                    dve.wait_ge(sem("l1_gate"), 4 * g + t + 1)
                    if due(4 * (g - 1) + t - 3):
                        dve.wait_ge(sem("l1_zturn"), 4 * (g - 1) + t - 3)
                    dve.tensor_scalar(q2[:, 4 * p + t, :], bank[(t + 1) % 2][:, :], -44.0, None, ALU.max)\
                       .then_inc(sem("l1_gclamp"), 1)

                def weights(b):
                    dve.wait_ge(sem("l1_dexp"), 2 * g + b + 1)
                    for n, col in enumerate((4 + 2 * b, 8 + b, 5 + 2 * b)):
                        dve.wait_ge(sem("l1_score"), 6 * g + 3 * b + n + 1)
                        for h in range(GH):
                            hs = slice(h * P, (h + 1) * P)
                            last = dve.scalar_tensor_tensor(decay(b, n)[:, hs], bank[3 + n][:, hs],
                                                            gc[p][:, col, h:h + 1], decay(b, n)[:, hs],
                                                            ALU.mult, ALU.mult)
                        last.then_inc(sem("l1_w"), 1)

                def mean(n):
                    dve.wait_ge(sem("l1_ysq"), 4 * g + n + 1)
                    dve.tensor_scalar(yss[n % 2][:, 1, :], yss[n % 2][:, 0, :], 1.0 / HD, 1e-5,
                                      ALU.mult, ALU.add).then_inc(sem("l1_ymean"), 1)

                def gated(n):
                    dve.wait_ge(sem("l1_yrms"), 4 * g + n + 1)
                    dve.wait_ge(sem("l1_sil"), 4 * g + n + 1)
                    z = q2[:, 4 * p + n, :]
                    for h in range(GH):
                        hs = slice(h * P, (h + 1) * P)
                        last = dve.scalar_tensor_tensor(z[:, hs], bank[6 + n % 2][:, hs],
                                                        yss[n % 2][:, 2, h:h + 1], z[:, hs], ALU.mult, ALU.mult)
                    last.then_inc(sem("l1_z"), 1)

                if due(6 * (g - 1)):
                    dve.wait_ge(sem("l1_w"), 6 * (g - 1))
                dve.tensor_copy(gc[p][:, :, :], cols[:, :, bass.ds(GH * g, GH)]).then_inc(sem("l1_gc"), 1)
                dve.wait_ge(sem("l1_gc"), g + 1)
                exponents(0)
                if due(6 * (g - 1)):
                    dve.wait_ge(sem("l1_score"), 6 * (g - 1))
                rope_sum(dve, "l1", g, 0, kT[p][:, 0:T])
                for h in range(GH):
                    rope_sum(dve, "l1", g, h + 1, qT[p][:, h, :])
                exponents(1)
                clamp(0)
                clamp(1)
                weights(0)
                clamp(2)
                clamp(3)
                mean(0)
                mean(1)
                gated(0)
                gated(1)
                weights(1)
                mean(2)
                mean(3)
                gated(2)
                gated(3)
                for t in range(NT):
                    residual_add(dve, "l1", g, t, bank[L1_OUT[t]])

            dve.wait_ge(sem("dt_cols"), 1)
            dve.wait_ge(sem("rows_out"), 16)
            groups(nc.vector, body)

        def ctx_tile(b, c, t):
            return wg[b][:, c, t * P:(t + 1) * P]

        KV_BANKS = [2, 7, 2, 7]

        def kn(half):
            return tmp[half]

        def x_tensor(pe):
            def body(g, p):
                turn = 8 * (g - p) + 16

                def key_values(n):
                    if n < 2:
                        if due(8 * g):
                            pe.wait_ge(sem("x_headed"), 8 * g)
                    else:
                        if due(4 * g + n - 1):
                            pe.wait_ge(sem("x_kv"), 4 * g + n - 1)
                    for i in range(2):
                        t = 2 * n + i
                        for c in range(KC):
                            last = pe.matmul(bank[KV_BANKS[n]][:, i * 256:(i + 1) * 256],
                                             ctx_tile(t // CT, c, t % CT), wkv[p][:, c, :],
                                             start=(c == 0), stop=(c == KC - 1))
                    last.then_inc(sem("x_kvproj"), 1)
                    if n == 3:
                        pass

                def q(h):
                    if h >= 2:
                        if due(4 * g + h - 1):
                            pe.wait_ge(sem("x_qmean"), 4 * g + h - 1)
                    project(pe, bank[(h + 1) % 2][:, :], wq[p], slice(h * HD, (h + 1) * HD), xT, "x_proj")

                def q_sums(h):
                    pe.wait_ge(sem("x_q"), 4 * g + h + 1)
                    for t in range(NT):
                        last = pe.matmul(bank[(h + 1) % 2][:, t:t + 1], tmp[2 + h % 2][:, t * P:(t + 1) * P],
                                         ones[:, 0:1], start=True, stop=True)
                    last.then_inc(sem("x_qss"), 1)

                def turn_keys():
                    for half in range(2):
                        pe.wait_ge(sem("x_kn"), 2 * g + half + 1)
                        if due(16 * g):
                            pe.wait_ge(sem("x_turned"), 16 * g)
                        for t in range(4):
                            last = pe.transpose(bank[5 + half][:, t * P:(t + 1) * P],
                                                kn(half)[:, t * P:(t + 1) * P], ident[:, :])
                        last.then_inc(sem("x_kturn"), 1)

                def scores(s):
                    h, b = s // B, s % B
                    pe.wait_ge(sem("x_q"), 4 * g + h + 1)
                    pe.wait_ge(sem("x_k"), 2 * g + 2)
                    for c in range(2):
                        if due(16 * g + 2 * (s - 1) + c + 1):
                            pe.wait_ge(sem("x_scaled"), 16 * g + 2 * (s - 1) + c + 1)
                        pe.matmul(bank[3 + c][:, :], qT[p][:, h, b * L + c * P:b * L + (c + 1) * P],
                                  kT[p][:, b * C:(b + 1) * C], start=True, stop=True)\
                          .then_inc(sem("x_score"), 1)

                def turn_probs(s):
                    pe.wait_ge(sem("x_norm"), 8 * g + s + 1)
                    for half in range(2):
                        if due(16 * g + 2 * (s - 1) + half + 1):
                            pe.wait_ge(sem("x_turned"), 16 * g + 2 * (s - 1) + half + 1)
                        if s == 0:
                            pe.wait_ge(sem("x_k"), 2 * g + half + 1)
                        for kt in range(2):
                            for c in range(2):
                                last = pe.transpose(bank[5 + half][:, kt * L + c * P:kt * L + (c + 1) * P],
                                                    prob[s % 2][:, c, (2 * half + kt) * P:(2 * half + kt + 1) * P],
                                                    ident[:, :])
                        last.then_inc(sem("x_turn"), 1)

                def values(s):
                    b = s % B
                    dst = bank[2 if s % 2 == 0 else 7]
                    pe.wait_ge(sem("x_kv"), 4 * g + 4)
                    if due(8 * g + s - 1):
                        pe.wait_ge(sem("x_headed"), 8 * g + s - 1)
                    for kt in range(CT):
                        if kt % 2 == 0:
                            pe.wait_ge(sem("x_turned"), 16 * g + 2 * s + kt // 2 + 1)
                        last = pe.matmul(dst[:, 0:L], v[p][:, b * CT + kt, :], probT[s % 2][:, kt, :],
                                         start=(kt == 0), stop=(kt == CT - 1))
                    last.then_inc(sem("x_value"), 1)

                pe.wait_ge(sem(f"x_wkv{p}"), turn)
                for n in range(4):
                    if n == 2:
                        pe.wait_ge(sem(f"x_wq{p}"), turn)
                        if due(4 * (g - 1) + 2):
                            pe.wait_ge(sem("x_added"), 4 * (g - 1) + 2)
                        q(0)
                    key_values(n)
                q_sums(0)
                q(1)
                turn_keys()
                q_sums(1)
                if due(4 * g):
                    pe.wait_ge(sem("x_added"), 4 * g)
                scores(0)
                q(2)
                q_sums(2)
                scores(1)
                turn_probs(0)
                q(3)
                q_sums(3)
                scores(2)
                values(0)
                for s in range(1, STEPS - 2):
                    turn_probs(s)
                    scores(s + 2)
                    values(s)
                turn_probs(6)
                pe.wait_ge(sem(f"x_wo{p}"), turn)
                pe.wait_ge(sem("x_qmean"), 4 * g + 4)
                pe.wait_ge(sem("x_headed"), 8 * g + 4)
                out_mm(pe, "x", p, bank[1], 0, [0, 1])
                values(6)
                turn_probs(7)
                pe.wait_ge(sem("x_headed"), 8 * g + 6)
                out_mm(pe, "x", p, bank[0], 1, [0, 1, 2])
                values(7)
                out_mm(pe, "x", p, bank[1], 0, [2])
                pe.wait_ge(sem("x_scaled"), 16 * g + 16)
                out_mm(pe, "x", p, bank[3], 2, [0, 1, 2])
                pe.wait_ge(sem("x_headed"), 8 * g + 8)
                out_mm(pe, "x", p, bank[1], 0, [3])
                out_mm(pe, "x", p, bank[0], 1, [3])
                out_mm(pe, "x", p, bank[3], 2, [3])
                out_mm(pe, "x", p, bank[4], 3, [0, 1, 2, 3])

            for b in range(B):
                pe.wait_ge(sem(f"ld_ctxT{b}"), 16)
            groups(nc.tensor, body)

        def x_scalar(act):
            def body(g, p):
                def key_values(n):
                    act.wait_ge(sem("x_kvproj"), 4 * g + n + 1)
                    src = bank[KV_BANKS[n]][:, :].rearrange("p (t c) -> p t c", t=2)
                    if n == 0:
                        if due(8 * (g - 1)):
                            act.wait_ge(sem("x_value"), 8 * (g - 1))
                    if n % 2 == 0:
                        if due(2 * (g - 1) + n // 2 + 1):
                            act.wait_ge(sem("x_kturn"), 2 * (g - 1) + n // 2 + 1)
                    for i in range(2):
                        act.activation(ysq[:, n % 2, i * P:(i + 1) * P], src[:, i, 0:HD], ACT.Square,
                                       accum_out=kss[:, 0, 2 * n + i:2 * n + i + 1])
                    act.activation(kn(n // 2)[:, (n % 2) * 256:(n % 2 + 1) * 256].rearrange("p (t c) -> p t c", t=2),
                                   src[:, :, 0:HD], ACT.Copy)
                    act.activation(v[p][:, 2 * n:2 * n + 2, :], src[:, :, HD:2 * HD], ACT.Copy)\
                       .then_inc(sem("x_kv"), 1)

                def query(h):
                    act.wait_ge(sem("x_proj"), 4 * g + h + 1)
                    if due(4 * g + h - 1):
                        act.wait_ge(sem("x_qss"), 4 * g + h - 1)
                    if h == 0:
                        if due(16 * (g - 1)):
                            act.wait_ge(sem("x_score"), 16 * (g - 1))
                    act.activation(tmp[2 + h % 2][:, :], bank[(h + 1) % 2][:, :], ACT.Square)
                    act.activation(qT[p][:, h, :], bank[(h + 1) % 2][:, :], ACT.Copy).then_inc(sem("x_q"), 1)

                def keys_out():
                    for half in range(2):
                        act.wait_ge(sem("x_kturn"), 2 * g + half + 1)
                        act.activation(kT[p][:, half * C:(half + 1) * C], bank[5 + half][:, :], ACT.Copy,
                                       scale=dvec[:, 3:4]).then_inc(sem("x_k"), 1)

                def exps(s):
                    act.wait_ge(sem("x_max"), 8 * g + s + 1)
                    if due(16 * g + 2 * (s - 1)):
                        act.wait_ge(sem("x_turn"), 16 * g + 2 * (s - 1))
                    for c in range(2):
                        last = act.activation(prob[s % 2][:, c, :], logit[s % 2][:, c, :], ACT.Exp,
                                              bias=rmax[s % 2][:, c:c + 1], accum_out=rsum[s % 2][:, c:c + 1])
                    last.then_inc(sem("x_exp"), 1)

                def turned(s):
                    if due(8 * g + s - 1):
                        act.wait_ge(sem("x_value"), 8 * g + s - 1)
                    for half in range(2):
                        act.wait_ge(sem("x_turn"), 16 * g + 2 * s + half + 1)
                        act.activation(probT[s % 2][:, 2 * half:2 * half + 2, :].rearrange("p a b -> p (a b)"),
                                       bank[5 + half][:, :], ACT.Copy).then_inc(sem("x_turned"), 1)

                def headed(s):
                    h, b = s // B, s % B
                    act.wait_ge(sem("x_value"), 8 * g + s + 1)
                    act.activation(attT[p][:, h, b * L:(b + 1) * L], bank[2 if s % 2 == 0 else 7][:, 0:L],
                                   ACT.Copy).then_inc(sem("x_headed"), 1)

                key_values(0)
                key_values(1)
                query(0)
                key_values(2)
                key_values(3)
                query(1)
                keys_out()
                query(2)
                exps(0)
                turned(0)
                query(3)
                exps(1)
                if due(4 * (g - 1)):
                    act.wait_ge(sem("x_out"), 4 * (g - 1))
                headed(0)
                for s in range(1, STEPS - 1):
                    turned(s)
                    exps(s + 1)
                    headed(s)
                turned(7)
                headed(7)

            groups(nc.scalar, body)

        def x_gpsimd(pool):
            def body(g, p):
                def pow_q(h):
                    pool.wait_ge(sem("x_qmean"), 4 * g + h + 1)
                    pool.tensor_tensor(qss[p][:, 1, h, :], qss[p][:, 0, h, :], half[:, :], ALU.pow)\
                        .then_inc(sem("x_qrms"), 1)

                for half_ in range(2):
                    pool.wait_ge(sem("x_kmean"), 2 * g + half_ + 1)
                    pool.tensor_tensor(kss[:, 2, 4 * half_:4 * half_ + 4], kss[:, 1, 4 * half_:4 * half_ + 4],
                                       half[:, :], ALU.pow).then_inc(sem("x_krms"), 1)
                for h in range(GH):
                    pow_q(h)

            groups(nc.gpsimd, body)

        def x_vector(dve):
            def body(g, p):
                def norm_keys(half_):
                    cols4 = slice(4 * half_, 4 * half_ + 4)
                    dve.wait_ge(sem("x_kv"), 4 * g + 2 * half_ + 2)
                    dve.tensor_scalar(kss[:, 1, cols4], kss[:, 0, cols4], 1.0 / HD, 1e-5, ALU.mult, ALU.add)\
                       .then_inc(sem("x_kmean"), 1)
                    dve.wait_ge(sem("x_krms"), 2 * g + half_ + 1)
                    for t in range(4):
                        ks = kn(half_)[:, t * P:(t + 1) * P]
                        last = dve.tensor_scalar(ks, ks, kss[:, 2, 4 * half_ + t:4 * half_ + t + 1], None, ALU.mult)
                    last.then_inc(sem("x_kn"), 1)

                def q_mean(h):
                    dve.wait_ge(sem("x_qss"), 4 * g + h + 1)
                    if h == 0:
                        if due(16 * (g - 1)):
                            dve.wait_ge(sem("x_scaled"), 16 * (g - 1))
                    dve.tensor_scalar(qss[p][:, 0, h, :], bank[(h + 1) % 2][:, 0:NT], HD * 1e-5, None, ALU.add)\
                       .then_inc(sem("x_qmean"), 1)

                def logits(s):
                    h, b = s // B, s % B
                    dve.wait_ge(sem("x_qrms"), 4 * g + h + 1)
                    if due(8 * g + s - 1):
                        dve.wait_ge(sem("x_exp"), 8 * g + s - 1)
                    for c in range(2):
                        dve.wait_ge(sem("x_score"), 16 * g + 2 * s + c + 1)
                        dve.scalar_tensor_tensor(logit[s % 2][:, c, :], bank[3 + c][:, :],
                                                 qss[p][:, 1, h, 2 * b + c:2 * b + c + 1], amask[:, c, :],
                                                 ALU.mult, ALU.add).then_inc(sem("x_scaled"), 1)
                    dve.wait_ge(sem("x_scaled"), 16 * g + 2 * s + 2)
                    dve.tensor_reduce(rmax[s % 2][:, 0:2], logit[s % 2][:, :, :], AX.X, ALU.max, negate=True)\
                       .then_inc(sem("x_max"), 1)

                def normalise(s):
                    dve.wait_ge(sem("x_exp"), 8 * g + s + 1)
                    dve.reciprocal(rsum[s % 2][:, 2:4], rsum[s % 2][:, 0:2]).then_inc(sem("x_recip"), 1)
                    dve.wait_ge(sem("x_recip"), 8 * g + s + 1)
                    for c in range(2):
                        last = dve.tensor_scalar(prob[s % 2][:, c, :], prob[s % 2][:, c, :],
                                                 rsum[s % 2][:, 2 + c:3 + c], None, ALU.mult)
                    last.then_inc(sem("x_norm"), 1)

                norm_keys(0)
                norm_keys(1)
                q_mean(0)
                q_mean(1)
                logits(0)
                q_mean(2)
                normalise(0)
                logits(1)
                q_mean(3)
                for s in range(1, STEPS - 1):
                    normalise(s)
                    logits(s + 1)
                normalise(7)
                for t in range(NT):
                    residual_add(dve, "x", g, t, bank[L1_OUT[t]])

            dve.wait_ge(sem("ld_l1"), 16 * 5)
            dve.tensor_tensor(dvec[:, 3:4], dvec[:, 1:2], dvec[:, 2:3], ALU.mult).then_inc(sem("x_kn0"), 1)
            dve.wait_ge(sem("ld_mask"), 16)
            groups(nc.vector, body)

        NR = LORA * RANK

        def ffn_tensor(pe):
            pe.wait_ge(sem("ld_ffn"), 16 * 5)
            for c in range(KC):
                pe.wait_ge(sem("ln_xT"), NT * 5)
                last = pe.matmul(bank[7][0:NR, :], loraA[:, c, :], xT[:, c, :], start=(c == 0), stop=(c == KC - 1))
            last.then_inc(sem("lora"), 1)
            for t in range(NT):
                dst = bank[OUT_BANKS[t]]
                for c in range(KC):
                    pe.matmul(dst[:, :], xT[:, c, t * P:(t + 1) * P], wq[0][:, c, :], start=(c == 0), stop=False)
                pe.wait_ge(sem("low"), 2)
                pe.matmul(dst[:, :], low[0:NR + 1, t * P:(t + 1) * P], loraB[:, :], start=False, stop=True)\
                  .then_inc(sem("ffn"), 1)

        def ffn_select(dve):
            tally = [0]

            def step(ins):
                tally[0] += 1
                ins.then_inc(sem("select"), 1)
                dve.wait_ge(sem("select"), tally[0])

            dve.wait_ge(sem("ld_ffn"), 16 * 5)
            for b in range(B):
                step(dve.tensor_scalar(sel[:, 8:12], starts[:, :], float(b), None, ALU.is_le))
                step(dve.tensor_reduce(sel[:, 4:5], sel[:, 8:12], AX.X, ALU.add))
                step(dve.tensor_scalar(sel[:, 5:6], sel[:, 4:5], lim[:, 0:1], None, ALU.is_ge))
                step(dve.scalar_tensor_tensor(sel[:, b:b + 1], sel[:, 4:5], lim[:, 1:2], sel[:, 5:6],
                                              ALU.is_le, ALU.mult))

        def ffn_vector(dve):
            dve.wait_ge(sem("lora"), 1)
            dve.wait_ge(sem("low_ones"), 1)
            for b in range(B):
                dve.tensor_scalar(low[0:NR, b * L:(b + 1) * L], bank[7][0:NR, b * L:(b + 1) * L],
                                  sel[:, b:b + 1], None, ALU.mult).then_inc(sem("low"), 1)
            for t in range(NT):
                dve.wait_ge(sem("ffn"), t + 1)
                dve.tensor_tensor(x[:, t, :], x[:, t, :], bank[OUT_BANKS[t]][:, :], ALU.add)\
                   .then_inc(sem("ffn_added"), 1)

        block = ctx.enter_context(nc.Block())

        @block.sync
        def _(sp):
            sp.dma_start(xT[:, :, :], a["xT"]).then_inc(sem("ld_xT"), 16)
            load_group(sp, "l0", 0, 0)
            for dst, name in ((ident, "ident"), (cos, "cos"), (sin, "sin"), (keys, "keys"), (causal, "causal"),
                              (identb, "identb")):
                sp.dma_start(dst[:, :], a[name]).then_inc(sem("ld_const"), 16)
            sp.dma_start(x[:, :, :], a["x"]).then_inc(sem("ld_x"), 16)
            load_group(sp, "l0", 1, 1)
            for dst, name in ((quant[:, 0:4], "quant"), (base[:, :], "base"), (gate[:, 0:1], "gate")):
                sp.dma_start(dst, a[name].broadcast_to([P, dst.shape[1]])).then_inc(sem("ld_small"), 16)
            for dst, name in ((wmix[:, :, :], "wmix"), (branch[:, :], "branch"), (eye4[:, :], "eye4")):
                sp.dma_start(dst, a[name]).then_inc(sem("ld_small"), 16)
            sp.dma_start(q2[:, :, :], a["ctx"]).then_inc(sem("ld_ctx"), 16)
            with nc.sync.Fori(1, NG // 2) as i:
                for p in range(2):
                    load_group(sp, "l0", 2 * i + p, p)
            for dst, name in ((win[:, :, :], "win"), (hvec[:, 0:2], "hvec"), (lower[:, :], "lower"),
                              (ones[:, :], "ones"), (dvec[:, 0:3], "dvec")):
                sp.dma_start(dst, a[name]).then_inc(sem("ld_l1"), 16)
            gate_load = (("wg", wg, a["l1_wg"], "gate", 4),)
            for g in range(2):
                load_group(sp, "l1", g, g, gate_load, (("l0_kvdone", 1), ("l0_proj", 5), ("l0_out", 4)))
            sp.wait_ge(sem("dt_G"), 1)
            sp.dma_start(a["g_rows"], row(6)).then_inc(sem("rows_out"), 16)
            sp.wait_ge(sem("rows_out"), 16)
            for g in range(2):
                l1_load_rows(sp, g, g)
            with nc.sync.Fori(1, NG // 2) as i:
                for p in range(2):
                    load_group(sp, "l1", 2 * i + p, p, gate_load)
                    l1_load_rows(sp, 2 * i + p, p)
            for b in range(B):
                sp.wait_ge(sem("l1_gate"), 4 * (7 + b))
                sp.dma_start(wg[b][:, :, :], a["ctxT"][b]).then_inc(sem(f"ld_ctxT{b}"), 16)
            for g in range(2):
                load_group(sp, "x", g, g, (), (("l1_kvdone", 1), ("l1_proj", 5), ("l1_out", 4)))
            sp.dma_start(amask[:, :, :], a["amask"]).then_inc(sem("ld_mask"), 16)
            with nc.sync.Fori(1, NG // 2) as i:
                for p in range(2):
                    load_group(sp, "x", 2 * i + p, p)
            sp.wait_ge(sem("x_proj"), 4 * (NG - 1))
            sp.dma_start(wq[0][:, :, :], a["ffn_w"]).then_inc(sem("ld_ffn"), 16)
            for dst, name in ((loraA[:, :, :], "loraA"), (loraB[:, :], "loraB"), (lim[:, :], "lim")):
                sp.dma_start(dst, a[name]).then_inc(sem("ld_ffn"), 16)
            sp.dma_start(starts[:, :], a["starts"].broadcast_to([LORA * RANK, 4])).then_inc(sem("ld_ffn"), 16)
            for t in range(NT):
                sp.wait_ge(sem("ln_x"), NT * 5 + t + 1)
                sp.dma_start(out[t * P:(t + 1) * P, :], x[:, t, :]).then_inc(sem("stored"), 16)
            sp.wait_ge(sem("stored"), 16 * NT)

        @block.scalar
        def _(act):
            act.preload_act_table_set("natural_log_exp_and_others")
            l0_scalar(act)
            ln_scalar(act, 0)
            mix_scalar(act)
            sink_scalar(act)
            ln_scalar(act, 2)
            dt_scalar(act)
            l1_scalar(act)
            ln_scalar(act, 3)
            x_scalar(act)
            ln_scalar(act, 4)

        @block.gpsimd
        def _(pool):
            pool.memset(half[:, :], -0.5).then_inc(sem("half"), 1)
            pool.wait_ge(sem("ld_const"), 6 * 16)
            l0_gpsimd(pool)
            ln_gpsimd(pool, 0)
            ln_gpsimd(pool, 1)
            mix_gpsimd(pool)
            pool.wait_ge(sem("ld_l1"), 16 * 5)
            sink_gpsimd(pool)
            ln_gpsimd(pool, 2)
            l1_gpsimd(pool)
            ln_gpsimd(pool, 3)
            pool.memset(low[:, :], 1.0).then_inc(sem("low_ones"), 1)
            x_gpsimd(pool)
            ln_gpsimd(pool, 4)
            ln_gpsimd(pool, 5)

        @block.tensor
        def _(pe):
            pe.wait_ge(sem("ld_xT"), 16)
            pe.wait_ge(sem("ld_const"), 6 * 16)
            l0_tensor(pe)
            ln_tensor(pe, 0)
            cross_tensor(pe)
            ln_tensor(pe, 1)
            mix_tensor(pe)
            ln_tensor(pe, 2)
            dt_tensor(pe)
            l1_tensor(pe)
            ln_tensor(pe, 3)
            pe.wait_ge(sem("ln_xT"), NT * 4)
            x_tensor(pe)
            ln_tensor(pe, 4)
            ffn_tensor(pe)

        @block.vector
        def _(dve):
            dve.wait_ge(sem("ld_const"), 6 * 16)
            dve.wait_ge(sem("ld_x"), 16)
            dve.wait_ge(sem("ld_small"), 6 * 16)
            dve.reciprocal(quant[:, 4:6], quant[:, 0:4:2])
            dve.tensor_scalar(gate[:, 1:2], gate[:, 0:1], -1.0, 80.0, ALU.mult, ALU.min).then_inc(sem("quant"), 1)
            l0_vector(dve)
            ln_vector(dve, 0, ("l0_added", 4 * (NG - 1) + 1))
            cross_vector(dve)
            ln_vector(dve, 1, ("cross_added", 1))
            mix_vector(dve)
            ln_vector(dve, 2, ("mixed", NT * 24 - (NT - 1)))
            dve.wait_ge(sem("ld_l1"), 16 * 5)
            dt_vector(dve)
            l1_vector(dve)
            ln_vector(dve, 3, ("l1_added", 4 * (NG - 1) + 1))
            x_vector(dve)
            ffn_select(dve)
            ln_vector(dve, 4, ("x_added", 4 * (NG - 1) + 1))
            ffn_vector(dve)
            ln_vector(dve, 5, ("ffn_added", 1))


def kernel(**inputs):
    import numpy as np
    import concourse.bacc as bacc
    from concourse import mybir as mb
    from concourse.bass_utils import run_bass_kernel_spmd

    f32 = np.float32

    def feature_major(w):
        return w.T.reshape(KC, P, -1).transpose(1, 0, 2)

    def by_group(w):
        return w.reshape(NG, -1, KC, P).transpose(0, 3, 2, 1)

    def key_value(wk, wv):
        return np.concatenate([by_group(wk), by_group(wv)], axis=3)

    def out_by_group(w):
        return w.reshape(D, NG, GH, HD).transpose(1, 3, 2, 0)

    g = {k: np.asarray(v) for k, v in inputs.items()}
    rows = np.arange(L)
    freq = 1.0 / 10000.0 ** (np.arange(0, HD, 2, dtype=f32) / HD)
    angle = (rows.astype(f32)[:, None] * freq[None, :]).T
    cos, sin = np.cos(angle).astype(f32), np.sin(angle).astype(f32)
    key = np.where(rows < 35, 0.5, np.where(rows < 107, 1.5, 1.0)).astype(f32)
    first = np.where(rows[:P, None] >= 107, key[None, :P], f32(1.0))
    keys = (np.concatenate([first, np.broadcast_to(key, (P, L))], axis=1) * SCALE).astype(f32)
    upper = np.arange(P)[:, None] < np.arange(P)[None, :]
    arrays = {
        "x": g["x"].reshape(NT, P, D).transpose(1, 0, 2),
        "xT": feature_major(g["x"].reshape(T, D)),
        "ident": np.eye(P, dtype=f32),
        "identb": np.eye(P).astype(mb.dt.np(mb.dt.bfloat16)),
        "cos": np.concatenate([cos, cos]),
        "sin": np.concatenate([-sin, sin]),
        "keys": keys,
        "causal": np.where(upper, MASKED, 0.0).astype(mb.dt.np(mb.dt.bfloat16)),
        "l0_wq": by_group(g["L0_attn_wq"]),
        "l0_wkv": key_value(g["L0_attn_wk"], g["L0_attn_wv"]),
        "l0_wo": out_by_group(g["L0_attn_wo"]),
        "quant": np.concatenate([g["L0_xattn_x1_scale"], g["L0_xattn_x1_zp"],
                                 g["L0_xattn_x2_scale"], g["L0_xattn_x2_zp"]])[None, :],
        "ctx": g["ctx_4096"].reshape(B * CT, P, D).transpose(1, 0, 2),
        "base": np.concatenate([g["L0_ffn_H_res_base"].reshape(-1), g["L0_ffn_H_pre_base"],
                                g["L0_ffn_H_post_base"]])[None, :],
        "gate": g["L0_ffn_gate"][None, :],
        "wmix": feature_major(np.concatenate([g["L0_ffn_W_res"], g["L0_ffn_W_pre"], g["L0_ffn_W_post"]])),
        "branch": g["L0_ffn_W_branch"],
        "eye4": np.tile(np.eye(4, dtype=f32).reshape(1, 16), (P, 1)),
        "win": feature_major(g["L1_attn_Win"]),
        "hvec": np.stack([g["L1_attn_dt_bias"], g["L1_attn_A_log_bias"]], axis=1),
        "lower": np.where(upper.T, f32(MASKED), f32(0.0)),
        "ones": np.ones((P, P), f32),
        "dvec": np.stack([g["L1_attn_gnorm_w"], g["L1_xattn_q_norm_w"], g["L1_xattn_k_norm_w"]], axis=1),
        "l1_wq": by_group(g["L1_attn_Wq"]),
        "l1_wkv": key_value(g["L1_attn_Wk"], g["L1_attn_Wv"]),
        "l1_wo": out_by_group(g["L1_attn_Wo"]),
        "l1_wg": by_group(g["L1_attn_Wg"]),
        "x_wq": by_group(g["L1_xattn_Wq"]),
        "x_wkv": key_value(g["L1_xattn_Wk"], g["L1_xattn_Wv"]),
        "x_wo": out_by_group(g["L1_xattn_Wo"]),
        "ctxT": np.stack([feature_major(c) for c in g["ctx_4096"]]),
        "amask": g["mask_1x1xSxS2_ff0"].reshape(2, P, C).transpose(1, 0, 2),
        "ffn_w": feature_major(g["L1_ffn_weight"]),
        "loraA": feature_major(g["L1_ffn_lora_A"].reshape(LORA * RANK, D)),
        "loraB": np.concatenate([g["L1_ffn_lora_B"].transpose(0, 2, 1).reshape(LORA * RANK, D),
                                 g["L1_ffn_bias"][None, :]]),
        "lim": np.repeat(np.array([[2, 2], [3, 3], [4, 1000]], f32), RANK, axis=0),
        "starts": g["L1_ffn_lora_start_indices"].reshape(1, 4),

    }
    nc = bacc.Bacc("TRN2", target_bir_lowering=False, num_devices=1)
    arrays = {f"in_{n}": np.ascontiguousarray(v) for n, v in arrays.items()}
    aps = {n[3:]: nc.dram_tensor(n, v.shape, mb.dt.from_np(v.dtype), kind="ExternalInput").ap()
           for n, v in arrays.items()}
    aps["g_rows"] = nc.dram_tensor("g_rows", (NG * GH, T), mb.dt.float32, kind="Internal").ap()
    out = nc.dram_tensor("out", (T, D), mb.dt.float32, kind="ExternalOutput").ap()
    decoder_kernel(nc, aps, out)
    r = run_bass_kernel_spmd(nc, [arrays], core_ids=[0])
    return r.results[0]["out"].reshape(B, L, D)
```

```python
from contextlib import ExitStack
import math

import concourse.bass as bass
from concourse import mybir

F32 = mybir.dt.float32
F32R = mybir.dt.float32r
BF16 = mybir.dt.bfloat16
I32 = mybir.dt.int32
ALU = mybir.AluOpType
ACT = mybir.ActivationFunctionType
AX = mybir.AxisListType

P = 128
B, L, D = 2, 256, 512
T = B * L
NT = T // P
KC = D // P
C = 512
CT = C // P
HD = 128
NG, GH = 8, 4
STEPS = GH * B
SCALE = 1.0 / math.sqrt(HD)
MASKED = -1.0e30
LN_EPS = 1e-5
SINK_ITERS = 50
SINK_BLOCK = 10
TAU = 0.1
STREAMS = 4
LORA, RANK = 3, 16
ROUND = 12582912.0


def decoder_kernel(nc, a, out):
    sems = {}
    with ExitStack() as ctx:
        address = {}

        def sb(name, shape, dt=F32):
            address[name] = -(-nc.sbuf_base // 32) * 32
            return ctx.enter_context(nc.sbuf_tensor(name, shape, dt))

        def over(name, shape, host, skip=0):
            return nc.alloc_sbuf_tensor_at(name, shape, F32R, offset=address[host] + skip)

        def sem(name):
            if name not in sems:
                sems[name] = ctx.enter_context(nc.semaphore(name))
            return sems[name]

        def due(value):
            return not isinstance(value, int) or value > 0

        x = sb("x", [P, NT, D])
        xT = sb("xT", [P, KC, T])
        wq = [sb(f"wq{i}", [P, KC, GH * HD]) for i in range(2)]
        wkv = [sb(f"wkv{i}", [P, KC, 2 * HD]) for i in range(2)]
        wo = [sb(f"wo{i}", [P, GH, D]) for i in range(2)]
        wg = [sb(f"wg{i}", [P, KC, GH * HD]) for i in range(2)]
        qT = [sb(f"qT{i}", [P, GH, T]) for i in range(2)]
        kT = [sb(f"kT{i}", [P, B * C]) for i in range(2)]
        v = [sb(f"v{i}", [P, B * CT, HD]) for i in range(2)]
        attT = [sb(f"attT{i}", [P, GH, T]) for i in range(2)]
        tmp = [sb(f"tmp{i}", [P, T]) for i in range(8)]
        logit = [sb(f"logit{i}", [P, 2, C]) for i in range(2)]
        prob = [sb(f"prob{i}", [P, 2, C]) for i in range(2)]
        probT = [sb(f"probT{i}", [P, CT, L]) for i in range(2)]
        ident = sb("ident", [P, P])
        identb = sb("identb", [P, P], BF16)
        cos = sb("cos", [P, L])
        sin = sb("sin", [P, L])
        keys = sb("keys", [P, P + L])
        causal = sb("causal", [P, P], BF16)
        rmax = [sb(f"rmax{i}", [P, 8]) for i in range(2)]
        rsum = [sb(f"rsum{i}", [P, 8]) for i in range(2)]
        stat = sb("stat", [P, NT, 6])
        mv = sb("mv", [P, NT, 2])
        lnr = sb("lnr", [P, 3, NT])
        half = sb("half", [P, NT])
        bank = [ctx.enter_context(nc.psum_tensor(f"bank{i}", [P, 512], F32)) for i in range(8)]
        q2 = sb("q2", [P, B * CT, D])
        quant = sb("quant", [P, 6])
        wmix = sb("wmix", [P, KC, 24])
        base = sb("base", [P, 24])
        gate = sb("gate", [P, 4])
        branch = sb("branch", [P, P])
        eye4 = sb("eye4", [P, 16])
        mix = sb("mix", [P, NT, 24])
        zlog = sb("zlog", [P, NT, 16])
        ztmp = sb("ztmp", [P, NT, 16])
        hres = sb("hres", [P, NT, 16])
        uv = sb("uv", [P, 2, 16])
        fac = sb("fac", [P, 2, 16])
        zsm = sb("zsm", [P, 6, 16])
        soft = sb("soft", [P, 3, 32])
        ssq = sb("ssq", [P, 3, NT])
        cols = sb("cols", [P, 10, NG * GH])
        gc = [sb(f"gc{i}", [P, 10, GH]) for i in range(2)]
        win = sb("win", [P, KC, NG * GH])
        hvec = sb("hvec", [NG * GH, 6])
        lower = sb("lower", [P, P])
        ones = sb("ones", [P, P])
        dvec = sb("dvec", [P, 4])
        yss = [sb(f"yss{i}", [P, 3, GH]) for i in range(2)]
        amask = sb("amask", [P, 2, C])
        kss = sb("kss", [P, 3, B * CT])
        qss = [sb(f"qss{i}", [P, 2, GH, NT]) for i in range(2)]
        loraA = sb("loraA", [P, KC, LORA * RANK])
        loraB = sb("loraB", [LORA * RANK + 1, D])
        low = sb("low", [64, T])
        starts = sb("starts", [LORA * RANK, 4], I32)
        lim = sb("lim", [LORA * RANK, 2])
        sel = sb("sel", [LORA * RANK, 16])
        sig = [sb(f"sig{i}", [P, GH * HD]) for i in range(2)]
        ysq = sb("ysq", [P, 2, GH * HD], BF16)
        def groups(engine, body, count=NG):
            for g in range(2):
                body(g, g)
            with engine.Fori(1, count // 2) as i:
                for p in range(2):
                    body(2 * i + p, p)

        def piped_groups(engine, body):
            for g in range(2):
                body(g, g, False)
            with engine.Fori(1, NG // 2 - 1) as i:
                for p in range(2):
                    body(2 * i + p, p, False)
            for g in range(NG - 2, NG):
                body(g, g % 2, g == NG - 1)

        def rope_psum_copies(eng, l, g, j, src):
            eng.wait_ge(sem(f"{l}_proj"), 5 * g + j + 1)
            if due(5 * g + j - 1):
                eng.wait_ge(sem(f"{l}_rope"), 5 * g + j - 1)
            eng.activation(tmp[j % 2][:, :], src[:, :], ACT.Copy)
            eng.activation(tmp[2 + j % 2][0:64, :], src[64:128, :], ACT.Copy)
            eng.activation(tmp[2 + j % 2][64:128, :], src[0:64, :], ACT.Copy).then_inc(sem(f"{l}_unproj"), 1)

        def rope_sin_part(eng, l, g, j):
            eng.wait_ge(sem(f"{l}_unproj"), 5 * g + j + 1)
            if due(5 * g + j - 1):
                eng.wait_ge(sem(f"{l}_rope"), 5 * g + j - 1)
            eng.tensor_tensor(halves(tmp[4 + j % 2]), halves(tmp[2 + j % 2]), per_batch(sin),
                              ALU.mult).then_inc(sem(f"{l}_sinp"), 1)

        def rope_sum(eng, l, g, j, dst):
            eng.wait_ge(sem(f"{l}_unproj"), 5 * g + j + 1)
            eng.tensor_tensor(halves(tmp[j % 2]), halves(tmp[j % 2]), per_batch(cos),
                              ALU.mult).then_inc(sem(f"{l}_cosp"), 1)
            eng.wait_ge(sem(f"{l}_cosp"), 5 * g + j + 1)
            eng.wait_ge(sem(f"{l}_sinp"), 5 * g + j + 1)
            eng.tensor_tensor(dst, tmp[j % 2][:, :], tmp[4 + j % 2][:, :],
                              ALU.add).then_inc(sem(f"{l}_rope"), 1)

        def halves(t):
            return t[:, :].rearrange("p (b l) -> p b l", b=B)

        def per_batch(t):
            return t[:, :].unsqueeze(1).broadcast_to([P, B, L])

        def product(eng, dst, lhs, rhs, start, stop):
            (a_high, a_low), (b_high, b_low) = lhs, rhs
            eng.matmul(dst, a_high, b_high, start=start, stop=False)
            eng.matmul(dst, a_low, b_high, start=False, stop=False)
            return eng.matmul(dst, a_high, b_low, start=False, stop=stop)

        def project(eng, dst, w, cols, rhs, done=None):
            for c in range(KC):
                last = eng.matmul(dst, w[:, c, cols], rhs[:, c, :], start=(c == 0), stop=(c == KC - 1))
            if done:
                last.then_inc(sem(done), 1)

        def out_mm(eng, l, p, dst, t, heads, cnt=None):
            for h in heads:
                last = eng.matmul(dst[:, :], attT[p][:, h, t * P:(t + 1) * P], wo[p][:, h, :],
                                  start=(h == 0), stop=(h == GH - 1))
            if heads[-1] == GH - 1:
                last.then_inc(sem(f"{l}_out"), 1)

        def residual_add(eng, l, g, t, src):
            eng.wait_ge(sem(f"{l}_out"), 4 * g + t + 1)
            if due(4 * (g - 1) + t + 1):
                eng.wait_ge(sem(f"{l}_added"), 4 * (g - 1) + t + 1)
            eng.tensor_tensor(x[:, t, :], x[:, t, :], src[:, :], ALU.add).then_inc(sem(f"{l}_added"), 1)

        OUT_BANKS = [3, 4, 1, 0]

        def load_group(sp, l, g, p, extra=(), before=()):
            for name, per in before:
                sp.wait_ge(sem(name), per * (NG - 1 + g))
            for name, dst, src, used, per in (("wkv", wkv, a[f"{l}_wkv"], "kvdone", 1),
                                              ("wq", wq, a[f"{l}_wq"], "proj", 5), *extra,
                                              ("wo", wo, a[f"{l}_wo"], "out", 4)):
                if due(per * (g - 1)):
                    sp.wait_ge(sem(f"{l}_{used}"), per * (g - 1))
                sp.dma_start(dst[p][:, :, :], src[bass.ds(g, 1)].rearrange("a p c n -> (a p) c n"))\
                  .then_inc(sem(f"{l}_{name}{p}"), 16)

        def l0_tensor(pe):
            def loads(n, p):
                return 8 * (n - p) + 16

            def key(n, p):
                pe.wait_ge(sem(f"l0_wkv{p}"), loads(n, p))
                if due(5 * n):
                    pe.wait_ge(sem("l0_unproj"), 5 * n)
                project(pe, bank[0][:, :], wkv[p], slice(0, HD), xT, "l0_proj")

            def value(n, p):
                if due(8 * (n - 1)):
                    pe.wait_ge(sem("l0_headed"), 8 * (n - 1))
                for t in range(NT):
                    for c in range(KC):
                        last = pe.matmul(bank[2][:, t * P:(t + 1) * P], xT[:, c, t * P:(t + 1) * P],
                                         wkv[p][:, c, HD:2 * HD], start=(c == 0), stop=(c == KC - 1))
                last.then_inc(sem("l0_kvdone"), 1)

            def query(n, p, h):
                if h == 0:
                    pe.wait_ge(sem(f"l0_wq{p}"), loads(n, p))
                if due(5 * n + h):
                    pe.wait_ge(sem("l0_unproj"), 5 * n + h)
                project(pe, bank[(h + 1) % 2][:, :], wq[p], slice(h * HD, (h + 1) * HD), xT, "l0_proj")

            def body(g, p, last):
                turn = 8 * (g - p) + 16

                def scores(s):
                    h, b = s // B, s % B
                    dst = bank[3 + s % 2]
                    if due(8 * g + s - 1):
                        pe.wait_ge(sem("l0_scaled"), 8 * g + s - 1)
                    pe.wait_ge(sem("l0_rope"), 5 * g + 2 + h)
                    k0 = kT[p][:, b * L:b * L + P]
                    q0 = qT[p][:, h, b * L:b * L + P]
                    q1 = qT[p][:, h, b * L + P:(b + 1) * L]
                    pe.matmul(dst[:, 0:P], q0, k0, start=True, stop=False)
                    pe.matmul(dst[:, 0:P], identb[:, :], causal[:, :], start=False, stop=True)
                    pe.matmul(dst[:, P:3 * P], q1, kT[p][:, b * L:(b + 1) * L], start=True, stop=False,
                              skip_group_check=True)
                    pe.matmul(dst[:, 2 * P:3 * P], identb[:, :], causal[:, :], start=False, stop=True,
                              skip_group_check=True).then_inc(sem("l0_score"), 1)

                def turn_probs(s):
                    dst = bank[5 + s % 2]
                    pe.wait_ge(sem("l0_norm"), 8 * g + s + 1)
                    if due(8 * g + s - 1):
                        pe.wait_ge(sem("l0_turned"), 8 * g + s - 1)
                    src = prob[s % 2][:, 0, :]
                    for at in (0, P, 2 * P):
                        done = pe.transpose(dst[:, at:at + P], src[:, at:at + P], ident[:, :])
                    done.then_inc(sem("l0_turn"), 1)

                def values(s):
                    h, b = s // B, s % B
                    dst = bank[7 if s % 2 == 0 else 2]
                    pe.wait_ge(sem("l0_turned"), 8 * g + s + 1)
                    pe.wait_ge(sem("l0_v"), g + 1 if last else g + 2)
                    if due(8 * g + s - 1):
                        pe.wait_ge(sem("l0_headed"), 8 * g + s - 1)
                    pt = probT[s % 2][:, :, :].rearrange("p a b -> p (a b)")
                    pe.matmul(dst[:, 0:L], v[p][:, 2 * b, :], pt[:, 0:L], start=True, stop=False,
                              skip_group_check=True)
                    pe.matmul(dst[:, P:L], v[p][:, 2 * b + 1, :], pt[:, L:L + P], start=False, stop=True,
                              skip_group_check=True).then_inc(sem("l0_value"), 1)

                def pair(step, h):
                    step(B * h)
                    step(B * h + 1)

                n = None if last else g + 1
                if due(4 * g):
                    pe.wait_ge(sem("l0_added"), 4 * g)
                pair(scores, 0)
                if not last:
                    key(n, 1 - p)
                pair(turn_probs, 0)
                pair(scores, 1)
                if not last:
                    value(n, 1 - p)
                pair(values, 0)
                pair(turn_probs, 1)
                pair(scores, 2)
                if not last:
                    query(n, 1 - p, 0)
                pair(values, 1)
                if not last:
                    query(n, 1 - p, 1)
                pair(turn_probs, 2)
                pair(scores, 3)
                if not last:
                    query(n, 1 - p, 2)
                pair(values, 2)
                if not last:
                    query(n, 1 - p, 3)
                pair(turn_probs, 3)
                pe.wait_ge(sem(f"l0_wo{p}"), turn)
                pe.wait_ge(sem("l0_scaled"), 8 * g + 8)
                pe.wait_ge(sem("l0_headed"), 8 * g + 6)
                out_mm(pe, "l0", p, bank[3], 0, [0, 1, 2])
                pair(values, 3)
                out_mm(pe, "l0", p, bank[4], 1, [0, 1, 2])
                pe.wait_ge(sem("l0_headed"), 8 * g + 8)
                out_mm(pe, "l0", p, bank[3], 0, [3])
                out_mm(pe, "l0", p, bank[4], 1, [3])
                pe.wait_ge(sem("l0_unproj"), 5 * (g + 2) if not last else 5 * NG)
                out_mm(pe, "l0", p, bank[1], 2, [0, 1, 2, 3])
                out_mm(pe, "l0", p, bank[0], 3, [0, 1, 2, 3])

            key(0, 0)
            value(0, 0)
            for h in range(GH):
                query(0, 0, h)
            piped_groups(nc.tensor, body)

        def l0_scalar(act):
            def value(n, p):
                act.wait_ge(sem("l0_kvdone"), n + 1)
                if due(8 * (n - 1)):
                    act.wait_ge(sem("l0_value"), 8 * (n - 1))
                act.activation(v[p][:, 0:NT, :].rearrange("p a b -> p (a b)"), bank[2][:, :], ACT.Copy)\
                   .then_inc(sem("l0_v"), 1)

            def body(g, p, last):
                def exps(s):
                    act.wait_ge(sem("l0_max"), 8 * g + s + 1)
                    if due(8 * g + s - 1):
                        act.wait_ge(sem("l0_turn"), 8 * g + s - 1)
                    for n, (at, to) in enumerate(((0, P), (P, 3 * P))):
                        done = act.activation(prob[s % 2][:, 0, at:to], logit[s % 2][:, 0, at:to], ACT.Exp,
                                              bias=rmax[s % 2][:, n:n + 1],
                                              accum_out=rsum[s % 2][:, n:n + 1])
                    done.then_inc(sem("l0_exp"), 1)

                def turned(s):
                    act.wait_ge(sem("l0_turn"), 8 * g + s + 1)
                    if due(8 * g + s - 1):
                        act.wait_ge(sem("l0_value"), 8 * g + s - 1)
                    act.activation(probT[s % 2][:, :, :].rearrange("p a b -> p (a b)")[:, 0:3 * P],
                                   bank[5 + s % 2][:, 0:3 * P], ACT.Copy).then_inc(sem("l0_turned"), 1)

                def headed(s):
                    h, b = s // B, s % B
                    act.wait_ge(sem("l0_value"), 8 * g + s + 1)
                    act.activation(attT[p][:, h, b * L:(b + 1) * L], bank[7 if s % 2 == 0 else 2][:, 0:L],
                                   ACT.Copy).then_inc(sem("l0_headed"), 1)

                def pair(step, h):
                    step(B * h)
                    step(B * h + 1)

                n = None if last else g + 1
                pair(exps, 0)
                if not last:
                    rope_psum_copies(act, "l0", n, 0, bank[0])
                pair(turned, 0)
                pair(exps, 1)
                if not last:
                    value(n, 1 - p)
                if due(4 * (g - 1)):
                    act.wait_ge(sem("l0_out"), 4 * (g - 1))
                pair(headed, 0)
                pair(turned, 1)
                pair(exps, 2)
                if not last:
                    rope_psum_copies(act, "l0", n, 1, bank[1])
                pair(headed, 1)
                if not last:
                    rope_psum_copies(act, "l0", n, 2, bank[0])
                pair(turned, 2)
                pair(exps, 3)
                if not last:
                    rope_psum_copies(act, "l0", n, 3, bank[1])
                pair(headed, 2)
                if not last:
                    rope_psum_copies(act, "l0", n, 4, bank[0])
                pair(turned, 3)
                pair(headed, 3)

            rope_psum_copies(act, "l0", 0, 0, bank[0])
            value(0, 0)
            for h in range(GH):
                rope_psum_copies(act, "l0", 0, h + 1, bank[(h + 1) % 2])
            piped_groups(nc.scalar, body)

        def l0_gpsimd(pool):
            def body(g, p):
                for j in range(5):
                    rope_sin_part(pool, "l0", g, j)

            groups(nc.gpsimd, body)

        def l0_vector(dve):
            def body(g, p, last):
                def maxima(s):
                    dve.wait_ge(sem("l0_score"), 8 * g + s + 1)
                    if due(8 * g + s - 1):
                        dve.wait_ge(sem("l0_exp"), 8 * g + s - 1)
                    dve.tensor_tensor(logit[s % 2][:, 0, 0:3 * P], bank[3 + s % 2][:, 0:3 * P], keys[:, :],
                                      ALU.mult).then_inc(sem("l0_scaled"), 1)
                    dve.wait_ge(sem("l0_scaled"), 8 * g + s + 1)
                    for n, (at, to) in enumerate(((0, P), (P, 3 * P))):
                        done = dve.tensor_reduce(rmax[s % 2][:, n:n + 1], logit[s % 2][:, 0, at:to], AX.X,
                                                 ALU.max, negate=True)
                    done.then_inc(sem("l0_max"), 1)

                def normalise(s):
                    dve.wait_ge(sem("l0_exp"), 8 * g + s + 1)
                    dve.reciprocal(rsum[s % 2][:, 2:4], rsum[s % 2][:, 0:2]).then_inc(sem("l0_recip"), 1)
                    dve.wait_ge(sem("l0_recip"), 8 * g + s + 1)
                    for n, (at, to) in enumerate(((0, P), (P, 3 * P))):
                        done = dve.tensor_scalar(prob[s % 2][:, 0, at:to], prob[s % 2][:, 0, at:to],
                                                 rsum[s % 2][:, 2 + n:3 + n], None, ALU.mult)
                    done.then_inc(sem("l0_norm"), 1)

                def pair(step, h):
                    step(B * h)
                    step(B * h + 1)

                n = None if last else g + 1
                pair(maxima, 0)
                pair(normalise, 0)
                pair(maxima, 1)
                if not last:
                    if due(8 * (n - 1)):
                        dve.wait_ge(sem("l0_score"), 8 * (n - 1))
                    rope_sum(dve, "l0", n, 0, kT[1 - p][:, 0:T])
                pair(normalise, 1)
                pair(maxima, 2)
                pair(normalise, 2)
                if not last:
                    rope_sum(dve, "l0", n, 1, qT[1 - p][:, 0, :])
                pair(maxima, 3)
                if not last:
                    rope_sum(dve, "l0", n, 2, qT[1 - p][:, 1, :])
                pair(normalise, 3)
                if not last:
                    rope_sum(dve, "l0", n, 3, qT[1 - p][:, 2, :])
                    rope_sum(dve, "l0", n, 4, qT[1 - p][:, 3, :])
                for t in range(NT):
                    residual_add(dve, "l0", g, t, bank[OUT_BANKS[t]])
                if isinstance(g, int) and g == 1:
                    dve.wait_ge(sem("ld_ctx"), 16)
                    for t in range(0, B * CT, 4):
                        fake_quant(dve, q2[:, t:t + 4, :], 1, "quant_c", t)

            rope_sum(dve, "l0", 0, 0, kT[0][:, 0:T])
            for h in range(GH):
                rope_sum(dve, "l0", 0, h + 1, qT[0][:, h, :])
            piped_groups(nc.vector, body)

        TURN_BANKS = [5, 6, 7, 2]

        def ln_vector(dve, n, after=None):
            for t in range(NT):
                if after:
                    dve.wait_ge(sem(after[0]), after[1] + t)
                dve.bn_stats(stat[:, t, :], x[:, t, :]).then_inc(sem("ln_stat"), 1)
            for t in range(NT):
                dve.wait_ge(sem("ln_stat"), 2 * NT * n + t + 1)
                dve.bn_aggr(mv[:, t, :], stat[:, t, :]).then_inc(sem("ln_stat"), 1)
            dve.wait_ge(sem("ln_stat"), 2 * NT * (n + 1))
            dve.tensor_scalar(lnr[:, 0, :], mv[:, :, 1], LN_EPS, None, ALU.add).then_inc(sem("ln_var"), 1)
            dve.wait_ge(sem("ln_rstd"), n + 1)
            for t in range(NT):
                dve.tensor_scalar(x[:, t, :], x[:, t, :], mv[:, t, 0:1], lnr[:, 1, t:t + 1],
                                  ALU.subtract, ALU.mult).then_inc(sem("ln_x"), 1)

        def ln_gpsimd(pool, n):
            pool.wait_ge(sem("ln_var"), n + 1)
            pool.wait_ge(sem("half"), 1)
            pool.tensor_tensor(lnr[:, 1, :], lnr[:, 0, :], half[:, :], ALU.pow).then_inc(sem("ln_rstd"), 1)

        def ln_tensor(pe, n):
            for t in range(NT):
                pe.wait_ge(sem("ln_x"), NT * n + t + 1)
                for c in range(KC):
                    last = pe.transpose(bank[TURN_BANKS[t]][:, c * P:(c + 1) * P], x[:, t, c * P:(c + 1) * P],
                                        ident[:, :])
                last.then_inc(sem("ln_turn"), 1)

        def ln_split(dve, n):
            for t in range(NT):
                dve.wait_ge(sem("ln_xT"), NT * n + t + 1)
                cols = slice(t * P, (t + 1) * P)
                dve.tensor_tensor(xT_low[:, :, cols],
                                  bank[TURN_BANKS[t]][:, :].rearrange("p (c t) -> p c t", c=KC),
                                  xT_high[:, :, cols].bitcast(F32), ALU.subtract).then_inc(sem("xT_low"), 1)

        def ln_scalar(act, n, high=None):
            for t in range(NT):
                act.wait_ge(sem("ln_turn"), NT * n + t + 1)
                dst = xT[:, :, t * P:(t + 1) * P] if high is None else high[:, :, t * P:(t + 1) * P]
                act.activation(dst,
                               bank[TURN_BANKS[t]][:, :].rearrange("p (c t) -> p c t", c=KC), ACT.Copy)\
                   .then_inc(sem("ln_xT"), 1)

        def fake_quant(eng, t, k, done, seen=0):
            s, z, r = quant[:, 2 * k:2 * k + 1], quant[:, 2 * k + 1:2 * k + 2], quant[:, 4 + k:5 + k]
            src, dst = t if isinstance(t, tuple) else (t, t)
            for n, (a0, a1, o0, o1) in enumerate(((r, z, ALU.mult, ALU.add), (0.0, 255.0, ALU.max, ALU.min),
                                                  (ROUND, ROUND, ALU.add, ALU.subtract),
                                                  (z, s, ALU.subtract, ALU.mult))):
                if n:
                    if due(seen + n):
                        eng.wait_ge(sem(done), seen + n)
                eng.tensor_scalar(dst, src if n == 0 else dst, a0, a1, o0, o1).then_inc(sem(done), 1)

        def cross_vector(dve):
            q1 = attT[0]
            for t in range(NT):
                dve.wait_ge(sem("ln_xT"), t + 1)
                cols = slice(t * P, (t + 1) * P)
                fake_quant(dve, (xT[:, :, cols], q1[:, :, cols]), 0, "quant_x", 4 * t)
            for t in range(NT):
                dve.wait_ge(sem("cross"), t + 1)
                dve.tensor_tensor(x[:, t, :], x[:, t, :], bank[OUT_BANKS[t]][:, :], ALU.add)\
                   .then_inc(sem("cross_added"), 1)

        def cross_tensor(pe):
            q1 = attT[0]
            pe.wait_ge(sem("quant_c"), B * CT)
            for t in range(NT):
                pe.wait_ge(sem("quant_x"), 4 * (t + 1))
                for c in range(KC):
                    last = pe.matmul(bank[OUT_BANKS[t]][:, :], q1[:, c, t * P:(t + 1) * P],
                                     q2[:, (t // 2) * CT + c, :], start=(c == 0), stop=(c == KC - 1))
                last.then_inc(sem("cross"), 1)

        BRANCH_BANKS = [1, 3, 4, 5]

        def mix_tensor(pe):
            for t in range(NT):
                pe.wait_ge(sem("ln_xT"), NT * 1 + t + 1)
                for c in range(KC):
                    last = pe.matmul(bank[0][:, t * 24:(t + 1) * 24], xT[:, c, t * P:(t + 1) * P], wmix[:, c, :],
                                     start=(c == 0), stop=(c == KC - 1))
            last.then_inc(sem("mix_logits"), 1)
            for t in range(NT):
                for c in range(STREAMS):
                    last = pe.matmul(bank[BRANCH_BANKS[t]][:, c * P:(c + 1) * P], xT[:, c, t * P:(t + 1) * P],
                                     branch[:, :], start=True, stop=True)
                last.then_inc(sem("branch"), 1)

        def mix_scalar(act):
            for t in range(NT):
                act.wait_ge(sem("ln_x"), NT * 1 + t + 1)
                act.activation(tmp[t][:, :], x[:, t, :], ACT.Square, accum_out=ssq[:, 0, t:t + 1])\
                   .then_inc(sem("mix_ssq"), 1)
            ln_scalar(act, 1)

        def mix_gpsimd(pool):
            pool.wait_ge(sem("mix_mean"), 1)
            pool.tensor_tensor(ssq[:, 2, :], ssq[:, 1, :], half[:, :], ALU.pow).then_inc(sem("mix_rms"), 1)

        tally = [0]

        def step(dve, ins):
            tally[0] += 1
            ins.then_inc(sem("vector_step"), 1)
            dve.wait_ge(sem("vector_step"), tally[0])

        def rows4(t, j_outer=False):
            if j_outer:
                return t.rearrange("p t (i j) -> p t j i", i=4)
            return t.rearrange("p t (i j) -> p t i j", i=4)

        def vec4(t):
            return t.rearrange("p (t i) -> p t i", t=NT)

        def mix_vector(dve):
            def over_rows(v):
                return vec4(v).unsqueeze(3).broadcast_to([P, NT, 4, 4])

            def over_cols(v):
                return vec4(v).unsqueeze(2).broadcast_to([P, NT, 4, 4])

            dve.wait_ge(sem("mix_ssq"), NT)
            dve.tensor_scalar(ssq[:, 1, :], ssq[:, 0, :], 1.0 / D, 1.1920929e-07, ALU.mult, ALU.add)\
               .then_inc(sem("mix_mean"), 1)
            dve.wait_ge(sem("mix_rms"), 1)
            dve.wait_ge(sem("mix_logits"), 1)
            for t in range(NT):
                last = dve.scalar_tensor_tensor(mix[:, t, :], bank[0][:, t * 24:(t + 1) * 24], ssq[:, 2, t:t + 1],
                                                base[:, :], ALU.mult, ALU.add)
            step(dve, last)
            pp = mix[:, :, 16:24].rearrange("p t (k n) -> p t k n", k=2)
            e = soft[:, 0, :].rearrange("p (t k n) -> p t k n", t=NT, k=2)
            m = soft[:, 1, 0:8].rearrange("p (t k) -> p t k", t=NT)
            mb = m.unsqueeze(3).broadcast_to([P, NT, 2, 4])
            step(dve, dve.tensor_reduce(m, pp, AX.X, ALU.max))
            dve.tensor_tensor(e, pp, mb, ALU.subtract).then_inc(sem("soft_in"), 1)
            z4, t4, h4 = rows4(zlog[:, :, :]), rows4(ztmp[:, :, :]), rows4(hres[:, :, :])
            step(dve, dve.tensor_scalar(zlog[:, :, :], mix[:, :, 0:16], 1.0 / TAU, None, ALU.mult))
            for side in range(2):
                src = z4 if side == 0 else h4
                lines = src if side == 0 else rows4(hres[:, :, :], True)
                wide = over_rows if side == 0 else over_cols
                mx, ls = zsm[:, 0, :], zsm[:, 1, :]
                step(dve, dve.tensor_reduce(vec4(mx), lines, AX.X, ALU.max))
                dve.tensor_tensor(t4, src, wide(mx), ALU.subtract).then_inc(sem("sink_in"), 1)
                dve.wait_ge(sem("sink_exp"), side + 1)
                t_lines = t4 if side == 0 else rows4(ztmp[:, :, :], True)
                dve.tensor_reduce(vec4(zsm[:, 2, :]), t_lines, AX.X, ALU.add).then_inc(sem("sink_sum"), 1)
                dve.wait_ge(sem("sink_ln"), side + 1)
                step(dve, dve.tensor_tensor(ls, ls, mx, ALU.add))
                step(dve, dve.tensor_scalar(uv[:, side, :], ls, -1.0, None, ALU.mult))
                last = dve.tensor_tensor(h4, src, wide(uv[:, side, :]), ALU.add)
                if side == 0:
                    step(dve, last)
                else:
                    last.then_inc(sem("sink_zuv"), 1)
            dve.wait_ge(sem("soft_exp"), 1)
            step(dve, dve.tensor_reduce(soft[:, 1, 8:16].rearrange("p (t k) -> p t k", t=NT), e, AX.X, ALU.add))
            step(dve, dve.reciprocal(soft[:, 1, 16:24], soft[:, 1, 8:16]))
            rb = soft[:, 1, 16:24].rearrange("p (t k) -> p t k", t=NT).unsqueeze(3).broadcast_to([P, NT, 2, 4])
            step(dve, dve.tensor_tensor(e, e, rb, ALU.mult))
            dve.wait_ge(sem("soft_exp"), 2)
            step(dve, dve.tensor_scalar(gate[:, 2:3], gate[:, 1:2], 1.0, None, ALU.add))
            step(dve, dve.reciprocal(gate[:, 3:4], gate[:, 2:3]))

            first = SINK_BLOCK - 1
            dve.wait_ge(sem("sink_h"), 1)
            sink_rounds(dve, "dve", 0, first, h4, over_rows, over_cols)
            with nc.vector.Fori(0, SINK_ITERS // SINK_BLOCK - 1) as i:
                dve.wait_ge(sem("fac_ln"), i + 1)
                dve.tensor_tensor(uv[:, :, :], uv[:, :, :], zsm[:, 0:2, :], ALU.add).then_inc(sem("absorb"), 1)
                dve.wait_ge(sem("absorb"), i * 3 + 1)
                dve.tensor_tensor(t4, z4, over_rows(uv[:, 0, :]), ALU.add).then_inc(sem("absorb"), 1)
                dve.wait_ge(sem("absorb"), i * 3 + 2)
                dve.tensor_tensor(t4, t4, over_cols(uv[:, 1, :]), ALU.add).then_inc(sem("absorb"), 1)
                dve.wait_ge(sem("sink_h"), i + 2)
                sink_rounds(dve, "dve", i * SINK_BLOCK + first, SINK_BLOCK, h4, over_rows, over_cols)
            dve.wait_ge(sem("norm4"), 6 * (SINK_ITERS - 1))
            step(dve, dve.tensor_scalar(gate[:, 2:3], gate[:, 3:4], -1.0, 2.0, ALU.mult, ALU.add))
            step(dve, dve.tensor_scalar(zsm[:, 0, :], eye4[:, :], gate[:, 2:3], None, ALU.mult))
            step(dve, dve.scalar_tensor_tensor(hres[:, :, :], hres[:, :, :], gate[:, 3:4],
                                          zsm[:, 0, :].unsqueeze(1).broadcast_to([P, NT, 16]), ALU.mult, ALU.add))
            count = [0]

            def mark(ins):
                count[0] += 1
                ins.then_inc(sem("mixed"), 1)
                return count[0]

            for t in range(NT):
                y, acc = tmp[4 + t], qT[0][:, t, :]
                dve.wait_ge(sem("branch"), t + 1)
                y_at = 0
                at = [0] * STREAMS
                for j in range(STREAMS):
                    xj = x[:, t, j * P:(j + 1) * P]
                    yj = bank[BRANCH_BANKS[t]][:, j * P:(j + 1) * P]
                    pre = soft[:, 0, t * 8 + j:t * 8 + j + 1]
                    if due(y_at):
                        dve.wait_ge(sem("mixed"), y_at)
                    y_at = mark(dve.tensor_scalar(y[:, 0:P], yj, pre, None, ALU.mult) if j == 0 else
                                dve.scalar_tensor_tensor(y[:, 0:P], yj, pre, y[:, 0:P], ALU.mult, ALU.add))
                    for i in range(STREAMS):
                        acci = acc[:, i * P:(i + 1) * P]
                        h = hres[:, t, i * 4 + j:i * 4 + j + 1]
                        if due(at[i]):
                            dve.wait_ge(sem("mixed"), at[i])
                        at[i] = mark(dve.tensor_scalar(acci, xj, h, None, ALU.mult) if j == 0 else
                                     dve.scalar_tensor_tensor(acci, xj, h, acci, ALU.mult, ALU.add))
                if due(count[0]):
                    dve.wait_ge(sem("mixed"), count[0])
                for i in range(STREAMS):
                    mark(dve.scalar_tensor_tensor(x[:, t, i * P:(i + 1) * P], y[:, 0:P],
                                                  soft[:, 0, t * 8 + 4 + i:t * 8 + 5 + i],
                                                  acc[:, i * P:(i + 1) * P], ALU.mult, ALU.add))

        def sink_rounds(eng, who, r0, n, h4=None, over_rows=None, over_cols=None):
            for k in range(n):
                for side in range(2):
                    half_step = 2 * (r0 + k) + side
                    factor = zsm[:, 4 + side, :]
                    if who == "pool":
                        eng.wait_ge(sem("norm4"), 3 * half_step + 2)
                        if k:
                            if due(half_step):
                                eng.wait_ge(sem("gathered"), half_step)
                            eng.tensor_tensor(fac[:, side, :], fac[:, side, :], factor, ALU.mult)\
                               .then_inc(sem("gathered"), 1)
                        else:
                            eng.tensor_tensor(fac[:, side, :], factor, ones[:, 0:16], ALU.mult).then_inc(sem("gathered"), 1)
                        continue
                    lines = rows4(hres[:, :, :], side == 1)
                    wide = over_rows if side == 0 else over_cols
                    if due(3 * half_step):
                        eng.wait_ge(sem("norm4"), 3 * half_step)
                    eng.tensor_reduce(vec4(zsm[:, 2 + side, :]), lines, AX.X, ALU.add).then_inc(sem("norm4"), 1)
                    eng.wait_ge(sem("norm4"), 3 * half_step + 1)
                    if due(half_step - 1):
                        eng.wait_ge(sem("gathered"), half_step - 1)
                    eng.reciprocal(factor, zsm[:, 2 + side, :]).then_inc(sem("norm4"), 1)
                    eng.wait_ge(sem("norm4"), 3 * half_step + 2)
                    eng.tensor_tensor(h4, h4, wide(factor), ALU.mult).then_inc(sem("norm4"), 1)

        def sink_scalar(act):
            z, h = ztmp[:, :, :], hres[:, :, :]
            act.wait_ge(sem("soft_in"), 1)
            act.activation(soft[:, 0, :], soft[:, 0, :], ACT.Exp).then_inc(sem("soft_exp"), 1)
            act.activation(gate[:, 1:2], gate[:, 1:2], ACT.Exp).then_inc(sem("soft_exp"), 1)
            for side in range(2):
                act.wait_ge(sem("sink_in"), side + 1)
                act.activation(z, z, ACT.Exp).then_inc(sem("sink_exp"), 1)
                act.wait_ge(sem("sink_sum"), side + 1)
                act.activation(zsm[:, 1, :], zsm[:, 2, :], ACT.Ln).then_inc(sem("sink_ln"), 1)
            act.wait_ge(sem("sink_zuv"), 1)
            act.activation(h, h, ACT.Exp).then_inc(sem("sink_h"), 1)
            unit = 0
            for i, count in enumerate(KV_WINDOWS):
                for _ in range(count):
                    kv_copy(act, unit)
                    unit += 1
                if i < SINK_ITERS // SINK_BLOCK - 1:
                    if due(i * (2 * SINK_BLOCK) + 2 * (SINK_BLOCK - 1)):
                        act.wait_ge(sem("gathered"), i * (2 * SINK_BLOCK) + 2 * (SINK_BLOCK - 1))
                    act.activation(zsm[:, 0:2, :], fac[:, :, :], ACT.Ln).then_inc(sem("fac_ln"), 1)
                    act.wait_ge(sem("absorb"), i * 3 + 3)
                    act.activation(h, z, ACT.Exp).then_inc(sem("sink_h"), 1)

        def sink_gpsimd(pool):
            sink_rounds(pool, "pool", 0, SINK_BLOCK - 1)
            with nc.gpsimd.Fori(0, SINK_ITERS // SINK_BLOCK - 1) as i:
                pool.wait_ge(sem("fac_ln"), i + 1)
                sink_rounds(pool, "pool", i * SINK_BLOCK + SINK_BLOCK - 1, SINK_BLOCK)

        def row(k):
            return qT[k // 4][0:NG * GH, k % 4, :]

        def grow(b, p):
            return (logit if p == 0 else prob)[b][:, :, :].rearrange("p a b -> p (a b)")\
                .rearrange("p (h q) -> p h q", h=GH)

        def decay(b, blk):
            flat = probT[b][:, :, :].rearrange("p a b -> p (a b)")
            return flat[:, blk * 512:(blk + 1) * 512] if blk < 2 else tmp[6 + b][:, :]

        L1_OUT = [1, 0, 3, 4]

        def dt_tensor(pe):
            pe.wait_ge(sem("ld_l1"), 16 * 5)
            pe.wait_ge(sem("ln_xT"), NT * 3)
            for c in range(KC):
                last = pe.matmul(bank[0][0:NG * GH, :], win[:, c, :], xT[:, c, :], start=(c == 0), stop=(c == KC - 1))
            last.then_inc(sem("dt"), 1)
            pe.wait_ge(sem("dt_vector"), 4)
            for n in range(10):
                src, at = ((row(6), n * P), (row(5), (n - 4) * P), (row(7), (n - 8) * L))[(n >= 4) + (n >= 8)]
                last = pe.transpose(bank[1][:, n * 32:(n + 1) * 32], src[:, at:at + P], ident[0:32, 0:32])
            last.then_inc(sem("dt_turn"), 1)

        def dt_scalar(act):
            act.wait_ge(sem("ld_l1"), 16 * 5)
            act.activation(hvec[:, 2:3], hvec[:, 1:2], ACT.Exp).then_inc(sem("dt_scalar"), 1)
            act.wait_ge(sem("dt_vector"), 1)
            act.activation(row(1), row(1), ACT.Exp).then_inc(sem("dt_scalar"), 1)
            act.wait_ge(sem("dt_vector"), 2)
            act.activation(row(4), row(2), ACT.Ln).then_inc(sem("dt_scalar"), 1)
            act.wait_ge(sem("dt_vector"), 3)
            for b in range(B):
                last = act.activation(row(7)[:, b * L:b * L + P], row(6)[:, b * L:b * L + P], ACT.Exp, scale=-1.0,
                                      bias=row(6)[:, b * L + P - 1:b * L + P])
            last.then_inc(sem("dt_scalar"), 1)
            act.wait_ge(sem("dt_turn"), 1)
            act.activation(cols[:, :, :].rearrange("p a b -> p (a b)"), bank[1][:, 0:320], ACT.Copy)\
               .then_inc(sem("dt_scalar"), 1)

        def dt_vector(dve):
            dve.wait_ge(sem("dt_scalar"), 1)
            step(dve, dve.tensor_scalar(hvec[:, 3:4], hvec[:, 2:3], -1.0, None, ALU.mult))
            dve.wait_ge(sem("dt"), 1)
            step(dve, dve.tensor_scalar(row(0), bank[0][0:NG * GH, :], hvec[:, 0:1], None, ALU.add))
            dve.scalar_tensor_tensor(row(1), row(0), -1.0, row(0), ALU.mult, ALU.min).then_inc(sem("dt_vector"), 1)
            dve.wait_ge(sem("dt_scalar"), 2)
            dve.tensor_scalar(row(2), row(1), 1.0, None, ALU.add).then_inc(sem("dt_vector"), 1)
            dve.wait_ge(sem("dt_vector"), 2)
            step(dve, dve.scalar_tensor_tensor(row(3), row(2), -1.0, row(1), ALU.add, ALU.subtract))
            step(dve, dve.scalar_tensor_tensor(row(3), row(0), 0.0, row(3), ALU.max, ALU.subtract))
            dve.wait_ge(sem("dt_scalar"), 3)
            step(dve, dve.tensor_tensor(row(5), row(3), row(4), ALU.add))
            step(dve, dve.tensor_scalar(row(0), row(5), hvec[:, 3:4], None, ALU.mult))
            for t in range(NT):
                tile = slice(t * P, (t + 1) * P)
                last = dve.tensor_tensor_scan(row(6)[:, tile], ones[0:NG * GH, :], row(0)[:, tile], 0.0,
                                              ALU.mult, ALU.add)
            last.then_inc(sem("dt_vector"), 1)
            dve.wait_ge(sem("dt_scalar"), 4)
            for b in range(B):
                last = dve.tensor_tensor(row(7)[:, b * L:b * L + P], row(7)[:, b * L:b * L + P],
                                         row(5)[:, b * L:b * L + P], ALU.mult)
            last.then_inc(sem("dt_vector"), 1)

        def l1_load_rows(sp, g, p):
            for b in range(B):
                if due(2 * (g - 1)):
                    sp.wait_ge(sem("l1_dexp"), 2 * (g - 1))
                src = a["g_rows"][bass.ds(GH * g, GH), b * L:(b + 1) * L]
                sp.dma_start(grow(b, p), src.unsqueeze(0).broadcast_to([P, GH, L])).then_inc(sem(f"l1_rows{b}{p}"), 16)

        def l1_tensor(pe):
            def body(g, p):
                turn = 8 * (g - p) + 16

                def q(h, waits):
                    if due(waits):
                        pe.wait_ge(sem("l1_unproj"), waits)
                    project(pe, bank[(h + 1) % 2][:, :], wq[p], slice(h * HD, (h + 1) * HD), xT, "l1_proj")

                def gates(t):
                    if t < 2:
                        pe.wait_ge(sem("l1_unproj"), 5 * g + 4 + t)
                    else:
                        if due(4 * g + t - 1):
                            pe.wait_ge(sem("l1_gclamp"), 4 * g + t - 1)
                    for c in range(KC):
                        last = pe.matmul(bank[(t + 1) % 2][:, :], xT[:, c, t * P:(t + 1) * P], wg[p][:, c, :],
                                         start=(c == 0), stop=(c == KC - 1))
                    last.then_inc(sem("l1_gate"), 1)

                def scores(b):
                    for n, (kt, qt) in enumerate(((0, 0), (0, 1), (1, 1))):
                        if due(6 * g + 3 * (b - 1) + n + 1):
                            pe.wait_ge(sem("l1_w"), 6 * g + 3 * (b - 1) + n + 1)
                        pe.matmul(bank[3 + n][:, :], kT[p][:, b * L + kt * P:b * L + (kt + 1) * P],
                                  qT[p][:, :, b * L + qt * P:b * L + (qt + 1) * P], start=True, stop=True)\
                          .then_inc(sem("l1_score"), 1)

                def outputs(b):
                    pe.wait_ge(sem("l1_v"), g + 1)
                    for c in range(2):
                        n = 2 * b + c
                        pe.wait_ge(sem("l1_w"), 6 * g + 3 * b + (1 if c == 0 else 3))
                        if due(4 * g + n - 1):
                            pe.wait_ge(sem("l1_z"), 4 * g + n - 1)
                        for h in range(GH):
                            hs = slice(h * P, (h + 1) * P)
                            last = pe.matmul(bank[6 + c][:, hs], decay(b, c)[:, hs], v[p][:, 2 * b, :],
                                             start=True, stop=(c == 0))
                            if c:
                                last = pe.matmul(bank[6 + c][:, hs], decay(b, 2)[:, hs], v[p][:, 2 * b + 1, :],
                                                 start=False, stop=True)
                        last.then_inc(sem("l1_y"), 1)

                def turn_z(n):
                    pe.wait_ge(sem("l1_z"), 4 * g + n + 1)
                    pe.wait_ge(sem("l1_headed"), 4 * g + n)
                    for h in range(GH):
                        last = pe.transpose(bank[2][:, h * P:(h + 1) * P],
                                            q2[:, 4 * p + n, h * P:(h + 1) * P], ident[:, :])
                    last.then_inc(sem("l1_zturn"), 1)

                def out_tile(t):
                    pe.wait_ge(sem("l1_headed"), 4 * g + t + 1)
                    out_mm(pe, "l1", p, bank[L1_OUT[t]], t, [0, 1, 2, 3])

                pe.wait_ge(sem(f"l1_wkv{p}"), turn)
                if due(4 * (g - 1) + 2):
                    pe.wait_ge(sem("l1_added"), 4 * (g - 1) + 2)
                project(pe, bank[0][:, :], wkv[p], slice(0, HD), xT, "l1_proj")
                if due(4 * g):
                    pe.wait_ge(sem("l1_headed"), 4 * g)
                for t in range(NT):
                    for c in range(KC):
                        last = pe.matmul(bank[2][:, t * P:(t + 1) * P], xT[:, c, t * P:(t + 1) * P],
                                         wkv[p][:, c, HD:2 * HD], start=(c == 0), stop=(c == KC - 1))
                last.then_inc(sem("l1_kvdone"), 1)
                pe.wait_ge(sem(f"l1_wq{p}"), turn)
                q(0, 0)
                q(1, 5 * g + 1)
                q(2, 5 * g + 2)
                q(3, 5 * g + 3)
                pe.wait_ge(sem(f"l1_wg{p}"), turn)
                gates(0)
                gates(1)
                pe.wait_ge(sem("l1_rope"), 5 * g + 5)
                if due(4 * g):
                    pe.wait_ge(sem("l1_added"), 4 * g)
                scores(0)
                gates(2)
                gates(3)
                outputs(0)
                scores(1)
                pe.wait_ge(sem("l1_v"), g + 1)
                turn_z(0)
                turn_z(1)
                pe.wait_ge(sem(f"l1_wo{p}"), turn)
                pe.wait_ge(sem("l1_gclamp"), 4 * g + 4)
                out_tile(0)
                outputs(1)
                out_tile(1)
                turn_z(2)
                turn_z(3)
                pe.wait_ge(sem("l1_w"), 6 * g + 6)
                out_tile(2)
                out_tile(3)

            pe.wait_ge(sem("dt_scalar"), 5)
            groups(nc.tensor, body)

        def l1_scalar(act):
            def body(g, p):
                def decays(b):
                    act.wait_ge(sem(f"l1_rows{b}{p}"), 8 * (g - p) + 16)
                    if due(4 * (g - 1) + 2 * b + 2):
                        act.wait_ge(sem("l1_y"), 4 * (g - 1) + 2 * b + 2)
                    act.activation(decay(b, 1).rearrange("p (h q) -> p h q", h=GH), grow(b, p)[:, :, P:L], ACT.Exp)
                    act.wait_ge(sem("l1_dsub"), 2 * g + b + 1)
                    act.activation(decay(b, 0), decay(b, 0), ACT.Exp)
                    act.activation(decay(b, 2), decay(b, 2), ACT.Exp).then_inc(sem("l1_dexp"), 1)

                def sigmoid(t):
                    s = sig[t % 2]
                    act.wait_ge(sem("l1_gclamp"), 4 * g + t + 1)
                    if due(4 * g + t - 1):
                        act.wait_ge(sem("l1_sil"), 4 * g + t - 1)
                    at = 3 * (4 * g + t)
                    act.activation(s[:, :], q2[:, 4 * p + t, :], ACT.Exp, scale=-1.0).then_inc(sem("l1_sig"), 1)
                    act.wait_ge(sem("l1_sig"), at + 1)
                    act.activation(s[:, :], s[:, :], ACT.Ln, bias=ones[:, 0:1]).then_inc(sem("l1_sig"), 1)
                    act.wait_ge(sem("l1_sig"), at + 2)
                    act.activation(s[:, :], s[:, :], ACT.Exp, scale=-1.0).then_inc(sem("l1_sig"), 1)

                def squares(n):
                    act.wait_ge(sem("l1_y"), 4 * g + n + 1)
                    if due(4 * g + n - 1):
                        act.wait_ge(sem("l1_yrms"), 4 * g + n - 1)
                    for h in range(GH):
                        last = act.activation(ysq[:, n % 2, h * P:(h + 1) * P], bank[6 + n % 2][:, h * P:(h + 1) * P],
                                              ACT.Square, accum_out=yss[n % 2][:, 0, h:h + 1])
                    last.then_inc(sem("l1_ysq"), 1)

                def headed(n):
                    act.wait_ge(sem("l1_zturn"), 4 * g + n + 1)
                    act.activation(attT[p][:, :, n * P:(n + 1) * P],
                                   bank[2][:, :].rearrange("p (h t) -> p h t", h=GH), ACT.Copy,
                                   scale=dvec[:, 0:1]).then_inc(sem("l1_headed"), 1)

                rope_psum_copies(act, "l1", g, 0, bank[0])
                act.wait_ge(sem("l1_kvdone"), g + 1)
                if due(4 * (g - 1)):
                    act.wait_ge(sem("l1_y"), 4 * (g - 1))
                act.activation(v[p][:, 0:NT, :].rearrange("p a b -> p (a b)"), bank[2][:, :], ACT.Copy)\
                   .then_inc(sem("l1_v"), 1)
                for j in range(4):
                    rope_psum_copies(act, "l1", g, j + 1, bank[(j + 1) % 2])
                decays(0)
                sigmoid(0)
                sigmoid(1)
                decays(1)
                sigmoid(2)
                sigmoid(3)
                squares(0)
                squares(1)
                if due(4 * (g - 1)):
                    act.wait_ge(sem("l1_out"), 4 * (g - 1))
                headed(0)
                headed(1)
                squares(2)
                squares(3)
                headed(2)
                headed(3)

            groups(nc.scalar, body)

        def l1_gpsimd(pool):
            def body(g, p):
                for j in range(5):
                    rope_sin_part(pool, "l1", g, j)
                for t in range(NT):
                    pool.wait_ge(sem("l1_sig"), 3 * (4 * g + t + 1))
                    pool.tensor_tensor(q2[:, 4 * p + t, :], q2[:, 4 * p + t, :], sig[t % 2][:, :],
                                       ALU.mult).then_inc(sem("l1_sil"), 1)
                for n in range(NT):
                    pool.wait_ge(sem("l1_ymean"), 4 * g + n + 1)
                    if due(4 * g + n - 1):
                        pool.wait_ge(sem("l1_z"), 4 * g + n - 1)
                    pool.tensor_tensor(yss[n % 2][:, 2, :], yss[n % 2][:, 1, :], half[:, :], ALU.pow)\
                        .then_inc(sem("l1_yrms"), 1)

            groups(nc.gpsimd, body)

        def l1_vector(dve):
            def body(g, p):
                def exponents(b):
                    dve.wait_ge(sem(f"l1_rows{b}{p}"), 8 * (g - p) + 16)
                    if due(4 * (g - 1) + 2 * b + 2):
                        dve.wait_ge(sem("l1_y"), 4 * (g - 1) + 2 * b + 2)
                    for c in range(2):
                        for h in range(GH):
                            last = dve.scalar_tensor_tensor(decay(b, 2 * c)[:, h * P:(h + 1) * P],
                                                            grow(b, p)[:, h, c * P:(c + 1) * P],
                                                            gc[p][:, 2 * b + c, h:h + 1], lower[:, :],
                                                            ALU.subtract, ALU.add)
                    last.then_inc(sem("l1_dsub"), 1)

                def clamp(t):
                    dve.wait_ge(sem("l1_gate"), 4 * g + t + 1)
                    if due(4 * (g - 1) + t - 3):
                        dve.wait_ge(sem("l1_zturn"), 4 * (g - 1) + t - 3)
                    dve.tensor_scalar(q2[:, 4 * p + t, :], bank[(t + 1) % 2][:, :], -44.0, None, ALU.max)\
                       .then_inc(sem("l1_gclamp"), 1)

                def weights(b):
                    dve.wait_ge(sem("l1_dexp"), 2 * g + b + 1)
                    for n, col in enumerate((4 + 2 * b, 8 + b, 5 + 2 * b)):
                        dve.wait_ge(sem("l1_score"), 6 * g + 3 * b + n + 1)
                        for h in range(GH):
                            hs = slice(h * P, (h + 1) * P)
                            last = dve.scalar_tensor_tensor(decay(b, n)[:, hs], bank[3 + n][:, hs],
                                                            gc[p][:, col, h:h + 1], decay(b, n)[:, hs],
                                                            ALU.mult, ALU.mult)
                        last.then_inc(sem("l1_w"), 1)

                def mean(n):
                    dve.wait_ge(sem("l1_ysq"), 4 * g + n + 1)
                    dve.tensor_scalar(yss[n % 2][:, 1, :], yss[n % 2][:, 0, :], 1.0 / HD, 1e-5,
                                      ALU.mult, ALU.add).then_inc(sem("l1_ymean"), 1)

                def gated(n):
                    dve.wait_ge(sem("l1_yrms"), 4 * g + n + 1)
                    dve.wait_ge(sem("l1_sil"), 4 * g + n + 1)
                    z = q2[:, 4 * p + n, :]
                    for h in range(GH):
                        hs = slice(h * P, (h + 1) * P)
                        last = dve.scalar_tensor_tensor(z[:, hs], bank[6 + n % 2][:, hs],
                                                        yss[n % 2][:, 2, h:h + 1], z[:, hs], ALU.mult, ALU.mult)
                    last.then_inc(sem("l1_z"), 1)

                if due(6 * (g - 1)):
                    dve.wait_ge(sem("l1_w"), 6 * (g - 1))
                dve.tensor_copy(gc[p][:, :, :], cols[:, :, bass.ds(GH * g, GH)]).then_inc(sem("l1_gc"), 1)
                dve.wait_ge(sem("l1_gc"), g + 1)
                exponents(0)
                if due(6 * (g - 1)):
                    dve.wait_ge(sem("l1_score"), 6 * (g - 1))
                rope_sum(dve, "l1", g, 0, kT[p][:, 0:T])
                for h in range(GH):
                    rope_sum(dve, "l1", g, h + 1, qT[p][:, h, :])
                exponents(1)
                clamp(0)
                clamp(1)
                weights(0)
                clamp(2)
                clamp(3)
                mean(0)
                mean(1)
                gated(0)
                gated(1)
                weights(1)
                mean(2)
                mean(3)
                gated(2)
                gated(3)
                for t in range(NT):
                    residual_add(dve, "l1", g, t, bank[L1_OUT[t]])

            dve.wait_ge(sem("dt_scalar"), 5)
            dve.wait_ge(sem("rows_out"), 16)
            groups(nc.vector, body)

        KV_BANKS = [2, 7]
        KV_WINDOWS = [4, 5, 5, 6, 12]

        def flat(t):
            return t[:, :, :].rearrange("p a b -> p (a b)")

        def kv_weights_load(sp, g, p):
            sp.dma_start(kT[p][:, :].rearrange("p (c n) -> p c n", c=KC),
                         a["x_wkv"][bass.ds(g, 1)].rearrange("a p c n -> (a p) c n"))\
              .then_inc(sem(f"kv_w{p}"), 16)

        def kv_sync(sp):
            def move(g, p, more):
                if more:
                    sp.wait_ge(sem("kv_proj"), 4 * g + 4)
                    kv_weights_load(sp, g + 2, p)
                sp.wait_ge(sem("kv_copied"), 4 * g + 4)
                for dst, src in (("kv_keys", logit), ("kv_values", prob)):
                    sp.dma_start(a[dst][bass.ds(g, 1)].rearrange("a p n -> (a p) n"), flat(src[p]))\
                      .then_inc(sem(f"kv_out{p}"), 16)

            with nc.sync.Fori(0, NG // 2 - 1) as i:
                for p in range(2):
                    move(2 * i + p, p, True)
            for g in range(NG - 2, NG):
                move(g, g % 2, False)

        def kv_tensor(pe):
            def body(g, p):
                pe.wait_ge(sem(f"kv_w{p}"), 8 * (g - p) + 16)
                weights = kT[p][:, :].rearrange("p (c n) -> p c n", c=KC)
                for n in range(4):
                    if due(4 * g + n - 1):
                        pe.wait_ge(sem("kv_copied"), 4 * g + n - 1)
                    for i in range(2):
                        t = 2 * n + i
                        for c in range(KC):
                            last = pe.matmul(bank[KV_BANKS[n % 2]][:, i * 256:(i + 1) * 256],
                                             wg[t // CT][:, c, t % CT * P:(t % CT + 1) * P], weights[:, c, :],
                                             start=(c == 0), stop=(c == KC - 1))
                    last.then_inc(sem("kv_proj"), 1)

            for b in range(B):
                pe.wait_ge(sem(f"ld_ctxT{b}"), 16)
            groups(nc.tensor, body)

        def kv_copy(act, unit):
            g, n = unit // 4, unit % 4
            p = g % 2
            act.wait_ge(sem("kv_proj"), unit + 1)
            if n == 0 and g >= 2:
                act.wait_ge(sem(f"kv_out{p}"), 32 * (g // 2))
            src = bank[KV_BANKS[n % 2]][:, :].rearrange("p (t c) -> p t c", t=2)
            for dst, at in ((logit, 0), (prob, HD)):
                last = act.activation(flat(dst[p])[:, n * 256:(n + 1) * 256].rearrange("p (t c) -> p t c", t=2),
                                      src[:, :, at:at + HD], ACT.Copy)
            last.then_inc(sem("kv_copied"), 1)

        xT_high = over("xT_high", [P, KC, T], "q2")
        xT_low = over("xT_low", [P, KC, T], "xT")
        wq_high = [over(f"wq_high{i}", [P, KC, GH * HD], f"wg{i}") for i in range(2)]
        wq_low = [over(f"wq_low{i}", [P, KC, GH * HD], f"wq{i}") for i in range(2)]
        wo_high = over("wo_high", [P, GH, D], "q2", KC * T * 4)
        wo_low = [over(f"wo_low{i}", [P, GH, D], f"wo{i}") for i in range(2)]
        att_high = over("att_high", [P, GH, T], "attT0")
        att_low = over("att_low", [P, GH, T], "attT1")

        def raw_keys(p, half_):
            return tmp[4 * p + half_]

        def x_load(sp, g, p, first=False):
            def source(name):
                return a[name][bass.ds(g, 1)]

            if first:
                sp.wait_ge(sem("l1_rope"), 5 * NG)
                sp.wait_ge(sem("l1_out"), 4 * (NG - 1 + g))
            if due(2 * (g - 1)):
                sp.wait_ge(sem("x_kturn"), 2 * (g - 1))
            for half_ in range(2):
                sp.dma_start(raw_keys(p, half_)[:, :],
                             source("kv_keys")[:, :, half_ * 512:(half_ + 1) * 512].rearrange("a p n -> (a p) n"))\
                  .then_inc(sem(f"x_keys{p}"), 16)
            if due(4 * (g - 1)):
                sp.wait_ge(sem("x_proj"), 4 * (g - 1))
            sp.dma_start(wq[p][:, :, :], source("x_wq").rearrange("a p c n -> (a p) c n"))\
              .then_inc(sem(f"x_wq{p}"), 16)
            if due(8 * (g - 1)):
                sp.wait_ge(sem("x_value"), 8 * (g - 1))
            sp.dma_start(flat(v[p]), source("kv_values").rearrange("a p n -> (a p) n")).then_inc(sem(f"x_values{p}"), 16)
            if due(4 * (g - 1)):
                sp.wait_ge(sem("x_out"), 4 * (g - 1))
            sp.dma_start(wo[p][:, :, :], source("x_wo").rearrange("a p c n -> (a p) c n"))\
              .then_inc(sem(f"x_wo{p}"), 16)

        def x_wo_ready(g, last_group=False):
            return 4 * g + (4 if last_group else 6)

        def x_wq_ready(n):
            return 2 if isinstance(n, int) and n == 0 else 4 * n

        def x_tensor(pe):
            def query(n, p, h):
                if h == 0:
                    pe.wait_ge(sem("x_split"), x_wq_ready(n))
                if h < 2:
                    if due(4 * (n - 1) + 3 + h):
                        pe.wait_ge(sem("x_qmean"), 4 * (n - 1) + 3 + h)
                    if due(4 * (n - 2) + 3 + h):
                        pe.wait_ge(sem("x_added"), 4 * (n - 2) + 3 + h)
                else:
                    if due(4 * n + h - 1):
                        pe.wait_ge(sem("x_qmean"), 4 * n + h - 1)
                cols = slice(h * HD, (h + 1) * HD)
                for c in range(KC):
                    last = product(pe, bank[(h + 1) % 2][:, :], (wq_high[p][:, c, cols], wq_low[p][:, c, cols]),
                                   (xT_high[:, c, :], xT_low[:, c, :]), c == 0, c == KC - 1)
                last.then_inc(sem("x_proj"), 1)

            def query_sums(n, p, h):
                pe.wait_ge(sem("x_q"), 4 * n + h + 1)
                for t in range(NT):
                    last = pe.matmul(bank[(h + 1) % 2][:, t:t + 1], tmp[2 + h % 2][:, t * P:(t + 1) * P],
                                     ones[:, 0:1], start=True, stop=True)
                last.then_inc(sem("x_qss"), 1)

            def turn_keys(n, p):
                for half_ in range(2):
                    pe.wait_ge(sem("x_kn"), 2 * n + half_ + 1)
                    pe.wait_ge(sem("x_turned"), 16 * n)
                    for t in range(4):
                        last = pe.transpose(bank[5 + half_][:, t * P:(t + 1) * P],
                                            raw_keys(p, half_)[:, t * P:(t + 1) * P], ident[:, :])
                    last.then_inc(sem("x_kturn"), 1)

            def body(g, p, last_group):
                n, turn = g + 1, 8 * (g - p) + 16

                def ahead(step, *h):
                    if not last_group:
                        step(n, 1 - p, *h)

                def scores(s):
                    h, b = s // B, s % B
                    if s == 0:
                        if due(4 * (g - 1) + 2):
                            pe.wait_ge(sem("x_added"), 4 * (g - 1) + 2)
                        pe.wait_ge(sem("x_q"), 4 * g + 4)
                        pe.wait_ge(sem("x_k"), 2 * g + 2)
                    for c in range(2):
                        if due(16 * g + 2 * (s - 1) + c + 1):
                            pe.wait_ge(sem("x_scaled"), 16 * g + 2 * (s - 1) + c + 1)
                        pe.matmul(bank[3 + c][:, :], qT[p][:, h, b * L + c * P:b * L + (c + 1) * P],
                                  kT[p][:, b * C:(b + 1) * C], start=True, stop=True)\
                          .then_inc(sem("x_score"), 1)

                def turn_probs(s):
                    pe.wait_ge(sem("x_norm"), 8 * g + s + 1)
                    for half_ in range(2):
                        if due(16 * g + 2 * (s - 1) + half_ + 1):
                            pe.wait_ge(sem("x_turned"), 16 * g + 2 * (s - 1) + half_ + 1)
                        for kt in range(2):
                            for c in range(2):
                                last = pe.transpose(bank[5 + half_][:, kt * L + c * P:kt * L + (c + 1) * P],
                                                    prob[s % 2][:, c, (2 * half_ + kt) * P:(2 * half_ + kt + 1) * P],
                                                    ident[:, :])
                        last.then_inc(sem("x_turn"), 1)

                def values(s):
                    b = s % B
                    if due(8 * g + s - 1):
                        pe.wait_ge(sem("x_low"), 8 * g + s - 1)
                    for kt in range(CT):
                        if kt % 2 == 0:
                            pe.wait_ge(sem("x_turned"), 16 * g + 2 * s + kt // 2 + 1)
                        last = pe.matmul(bank[VALUE_BANKS[s % 2]][:, 0:L], v[p][:, b * CT + kt, :],
                                         probT[s % 2][:, kt, :], start=(kt == 0), stop=(kt == CT - 1))
                    last.then_inc(sem("x_value"), 1)

                scores(0)
                ahead(query, 0)
                scores(1)
                ahead(query_sums, 0)
                ahead(query, 1)
                scores(2)
                turn_probs(0)
                ahead(query_sums, 1)
                pe.wait_ge(sem(f"x_values{p}"), turn)
                for s in range(3, STEPS):
                    scores(s)
                    turn_probs(s - 2)
                    values(s - 3)
                ahead(query, 2)
                turn_probs(6)
                values(5)
                ahead(query_sums, 2)
                ahead(query, 3)
                turn_probs(7)
                values(6)
                ahead(query_sums, 3)
                ahead(turn_keys)
                def outputs(dst, t, heads):
                    for h in heads:
                        cols = slice(t * P, (t + 1) * P)
                        last = product(pe, dst[:, :], (att_high[:, h, cols], att_low[:, h, cols]),
                                       (wo_high[:, h, :], wo_low[p][:, h, :]), h == 0, h == GH - 1)
                    if heads[-1] == GH - 1:
                        last.then_inc(sem("x_out"), 1)

                pe.wait_ge(sem("x_split"), x_wo_ready(g, last_group))
                pe.wait_ge(sem("x_scaled"), 16 * g + 16)
                pe.wait_ge(sem("x_low"), 8 * g + 6)
                outputs(bank[3], 0, [0, 1, 2])
                values(7)
                outputs(bank[4], 1, [0, 1, 2])
                pe.wait_ge(sem("x_low"), 8 * g + 8)
                outputs(bank[3], 0, [3])
                outputs(bank[4], 1, [3])
                if last_group:
                    if due(4 * g):
                        pe.wait_ge(sem("x_added"), 4 * g)
                for t in (2, 3):
                    if not last_group:
                        pe.wait_ge(sem("x_qmean"), 4 * n + t + 1)
                    outputs(bank[OUT_BANKS[t]], t, [0, 1, 2, 3])

            for h in range(GH):
                query(0, 0, h)
                query_sums(0, 0, h)
            turn_keys(0, 0)
            piped_groups(nc.tensor, body)

        VALUE_BANKS = [2, 7]

        def x_scalar(act):
            def squares(n, p):
                if due(16 * (n - p) + 32):
                    act.wait_ge(sem(f"x_keys{p}"), 16 * (n - p) + 32)
                for t in range(B * CT):
                    last = act.activation(ysq[:, t // CT, t % CT * P:(t % CT + 1) * P],
                                          raw_keys(p, t // CT)[:, t % CT * P:(t % CT + 1) * P], ACT.Square,
                                          accum_out=kss[:, 0, t:t + 1])
                last.then_inc(sem("x_ksq"), 1)

            def query(n, p, h):
                act.wait_ge(sem("x_proj"), 4 * n + h + 1)
                if due(4 * n + h - 1):
                    act.wait_ge(sem("x_qss"), 4 * n + h - 1)
                if h == 0:
                    if due(16 * (n - 1)):
                        act.wait_ge(sem("x_score"), 16 * (n - 1))
                act.activation(tmp[2 + h % 2][:, :], bank[(h + 1) % 2][:, :], ACT.Square)
                act.activation(qT[p][:, h, :], bank[(h + 1) % 2][:, :], ACT.Copy).then_inc(sem("x_q"), 1)

            def keys_out(n, p):
                for half_ in range(2):
                    act.wait_ge(sem("x_kturn"), 2 * n + half_ + 1)
                    act.activation(kT[p][:, half_ * C:(half_ + 1) * C], bank[5 + half_][:, :], ACT.Copy,
                                   scale=dvec[:, 3:4]).then_inc(sem("x_k"), 1)

            def body(g, p, last_group):
                n = g + 1

                def ahead(step, *h):
                    if not last_group:
                        step(n, 1 - p, *h)

                def exps(s):
                    act.wait_ge(sem("x_max"), 8 * g + s + 1)
                    if due(16 * g + 2 * (s - 1)):
                        act.wait_ge(sem("x_turn"), 16 * g + 2 * (s - 1))
                    for c in range(2):
                        last = act.activation(prob[s % 2][:, c, :], logit[s % 2][:, c, :], ACT.Exp,
                                              bias=rmax[s % 2][:, c:c + 1], accum_out=rsum[s % 2][:, c:c + 1])
                    last.then_inc(sem("x_exp"), 1)

                def turned(s):
                    if due(8 * g + s - 1):
                        act.wait_ge(sem("x_value"), 8 * g + s - 1)
                    for half_ in range(2):
                        act.wait_ge(sem("x_turn"), 16 * g + 2 * s + half_ + 1)
                        act.activation(probT[s % 2][:, 2 * half_:2 * half_ + 2, :].rearrange("p a b -> p (a b)"),
                                       bank[5 + half_][:, :], ACT.Copy).then_inc(sem("x_turned"), 1)

                def headed(s):
                    h, b = s // B, s % B
                    if s == 0:
                        if due(4 * g):
                            act.wait_ge(sem("x_out"), 4 * g)
                    act.wait_ge(sem("x_value"), 8 * g + s + 1)
                    act.activation(att_high[:, h, b * L:(b + 1) * L], bank[VALUE_BANKS[s % 2]][:, 0:L],
                                   ACT.Copy).then_inc(sem("x_headed"), 1)

                exps(0)
                ahead(query, 0)
                ahead(squares)
                exps(1)
                ahead(query, 1)
                turned(0)
                exps(2)
                for s in range(3, STEPS):
                    turned(s - 2)
                    exps(s)
                    headed(s - 3)
                ahead(query, 2)
                turned(6)
                headed(5)
                ahead(query, 3)
                turned(7)
                headed(6)
                ahead(keys_out)
                headed(7)

            squares(0, 0)
            for h in range(GH):
                query(0, 0, h)
            keys_out(0, 0)
            piped_groups(nc.scalar, body)

        def split(pool, high, low, t, ready):
            one = ones[:, 0:1].broadcast_to([P, t.shape[2]])
            for c in range(t.shape[1]):
                last = pool.tensor_tensor(high[:, c, :], t[:, c, :], one, ALU.mult)
            last.then_inc(sem("x_split"), 1)
            pool.wait_ge(sem("x_split"), ready - 1)
            for c in range(t.shape[1]):
                last = pool.tensor_tensor(low[:, c, :], t[:, c, :], high[:, c, :].bitcast(F32), ALU.subtract)
            last.then_inc(sem("x_split"), 1)

        def x_gpsimd_first(pool):
            pool.wait_ge(sem("l1_gate"), 4 * (NG - 1))
            pool.wait_ge(sem("x_wq0"), 16)
            split(pool, wq_high[0], wq_low[0], wq[0], x_wq_ready(0))

        def x_gpsimd(pool):
            def key_pow(n):
                pool.wait_ge(sem("x_kmean"), n + 1)
                mean, rms = (kss[:, k, :].rearrange("p (b t) -> p b t", b=B) for k in (1, 2))
                pool.tensor_tensor(rms, mean, half[:, :].unsqueeze(1).broadcast_to([P, B, CT]), ALU.pow)\
                    .then_inc(sem("x_krms"), 1)

            def query_pow(n, p, h):
                pool.wait_ge(sem("x_qmean"), 4 * n + h + 1)
                pool.tensor_tensor(qss[p][:, 1, h, :], qss[p][:, 0, h, :], half[:, :], ALU.pow)\
                    .then_inc(sem("x_qrms"), 1)

            def body(g, p, last_group):
                if not last_group:
                    key_pow(g + 1)
                pool.wait_ge(sem(f"x_wo{p}"), 8 * (g - p) + 16)
                if due(4 * g):
                    pool.wait_ge(sem("x_out"), 4 * g)
                split(pool, wo_high, wo_low[p], wo[p], x_wo_ready(g, last_group))
                if not last_group:
                    query_pow(g + 1, 1 - p, 0)
                    query_pow(g + 1, 1 - p, 1)
                if not isinstance(g, int) or g < NG - 2:
                    if due(8 * (g - p) + 32):
                        pool.wait_ge(sem(f"x_wq{p}"), 8 * (g - p) + 32)
                    split(pool, wq_high[p], wq_low[p], wq[p], x_wq_ready(g + 2))
                if not last_group:
                    query_pow(g + 1, 1 - p, 2)
                    query_pow(g + 1, 1 - p, 3)

            key_pow(0)
            query_pow(0, 0, 0)
            query_pow(0, 0, 1)
            pool.wait_ge(sem("x_wq1"), 16)
            pool.wait_ge(sem("l1_gate"), 4 * NG)
            split(pool, wq_high[1], wq_low[1], wq[1], x_wq_ready(1))
            query_pow(0, 0, 2)
            query_pow(0, 0, 3)
            piped_groups(nc.gpsimd, body)

        def x_vector(dve):
            def key_mean(n, p):
                dve.wait_ge(sem("x_ksq"), n + 1)
                dve.tensor_scalar(kss[:, 1, :], kss[:, 0, :], 1.0 / HD, 1e-5, ALU.mult, ALU.add)\
                   .then_inc(sem("x_kmean"), 1)

            def norm_keys(n, p):
                dve.wait_ge(sem("x_krms"), n + 1)
                for half_ in range(2):
                    k = raw_keys(p, half_)[:, :].rearrange("p (t c) -> p t c", t=CT)
                    rms = kss[:, 2, half_ * CT:(half_ + 1) * CT].unsqueeze(2).broadcast_to([P, CT, HD])
                    dve.tensor_tensor(k, k, rms, ALU.mult).then_inc(sem("x_kn"), 1)

            def query_mean(n, p, h):
                dve.wait_ge(sem("x_qss"), 4 * n + h + 1)
                dve.tensor_scalar(qss[p][:, 0, h, :], bank[(h + 1) % 2][:, 0:NT], HD * 1e-5, None, ALU.add)\
                   .then_inc(sem("x_qmean"), 1)

            def body(g, p, last_group):
                n = g + 1

                def ahead(step, *h):
                    if not last_group:
                        step(n, 1 - p, *h)

                def logits(s):
                    h, b = s // B, s % B
                    dve.wait_ge(sem("x_qrms"), 4 * g + h + 1)
                    if due(8 * g + s - 1):
                        dve.wait_ge(sem("x_exp"), 8 * g + s - 1)
                    for c in range(2):
                        dve.wait_ge(sem("x_score"), 16 * g + 2 * s + c + 1)
                        dve.scalar_tensor_tensor(logit[s % 2][:, c, :], bank[3 + c][:, :],
                                                 qss[p][:, 1, h, 2 * b + c:2 * b + c + 1], amask[:, c, :],
                                                 ALU.mult, ALU.add).then_inc(sem("x_scaled"), 1)
                    dve.wait_ge(sem("x_scaled"), 16 * g + 2 * s + 2)
                    dve.tensor_reduce(rmax[s % 2][:, 0:2], logit[s % 2][:, :, :], AX.X, ALU.max, negate=True)\
                       .then_inc(sem("x_max"), 1)

                def normalise(s):
                    dve.wait_ge(sem("x_exp"), 8 * g + s + 1)
                    dve.reciprocal(rsum[s % 2][:, 2:4], rsum[s % 2][:, 0:2]).then_inc(sem("x_recip"), 1)
                    dve.wait_ge(sem("x_recip"), 8 * g + s + 1)
                    for c in range(2):
                        last = dve.tensor_scalar(prob[s % 2][:, c, :], prob[s % 2][:, c, :],
                                                 rsum[s % 2][:, 2 + c:3 + c], None, ALU.mult)
                    last.then_inc(sem("x_norm"), 1)

                def low(s):
                    h, b = s // B, s % B
                    dve.wait_ge(sem("x_headed"), 8 * g + s + 1)
                    at = (slice(None), h, slice(b * L, (b + 1) * L))
                    dve.tensor_tensor(att_low[at], bank[VALUE_BANKS[s % 2]][:, 0:L], att_high[at].bitcast(F32),
                                      ALU.subtract).then_inc(sem("x_low"), 1)

                logits(0)
                logits(1)
                normalise(0)
                ahead(key_mean)
                ahead(query_mean, 0)
                logits(2)
                normalise(1)
                ahead(norm_keys)
                ahead(query_mean, 1)
                for s in range(3, STEPS):
                    logits(s)
                    normalise(s - 1)
                    if s >= 4:
                        low(s - 4)
                normalise(7)
                low(4)
                ahead(query_mean, 2)
                low(5)
                ahead(query_mean, 3)
                low(6)
                low(7)
                for t in range(NT):
                    residual_add(dve, "x", g, t, bank[OUT_BANKS[t]])

            dve.wait_ge(sem("ld_l1"), 16 * 5)
            dve.tensor_tensor(dvec[:, 3:4], dvec[:, 1:2], dvec[:, 2:3], ALU.mult)
            key_mean(0, 0)
            norm_keys(0, 0)
            for h in range(GH):
                query_mean(0, 0, h)
            dve.wait_ge(sem("ld_mask"), 16)
            piped_groups(nc.vector, body)

        NR = LORA * RANK

        def ffn_tensor(pe):
            pe.wait_ge(sem("ld_ffn"), 16 * 5)
            for c in range(KC):
                pe.wait_ge(sem("ln_xT"), NT * 5)
                last = pe.matmul(bank[7][0:NR, :], loraA[:, c, :], xT[:, c, :], start=(c == 0), stop=(c == KC - 1))
            last.then_inc(sem("lora"), 1)
            for t in range(NT):
                dst = bank[OUT_BANKS[t]]
                for c in range(KC):
                    pe.matmul(dst[:, :], xT[:, c, t * P:(t + 1) * P], wq[0][:, c, :], start=(c == 0), stop=False)
                pe.wait_ge(sem("low"), 2)
                pe.matmul(dst[:, :], low[0:NR + 1, t * P:(t + 1) * P], loraB[:, :], start=False, stop=True)\
                  .then_inc(sem("ffn"), 1)

        def ffn_select(dve):
            dve.wait_ge(sem("ld_ffn"), 16 * 5)
            for b in range(B):
                step(dve, dve.tensor_scalar(sel[:, 8:12], starts[:, :], float(b), None, ALU.is_le))
                step(dve, dve.tensor_reduce(sel[:, 4:5], sel[:, 8:12], AX.X, ALU.add))
                step(dve, dve.tensor_scalar(sel[:, 5:6], sel[:, 4:5], lim[:, 0:1], None, ALU.is_ge))
                step(dve, dve.scalar_tensor_tensor(sel[:, b:b + 1], sel[:, 4:5], lim[:, 1:2], sel[:, 5:6],
                                              ALU.is_le, ALU.mult))

        def ffn_vector(dve):
            dve.wait_ge(sem("lora"), 1)
            dve.wait_ge(sem("low_ones"), 1)
            for b in range(B):
                dve.tensor_scalar(low[0:NR, b * L:(b + 1) * L], bank[7][0:NR, b * L:(b + 1) * L],
                                  sel[:, b:b + 1], None, ALU.mult).then_inc(sem("low"), 1)
            for t in range(NT):
                dve.wait_ge(sem("ffn"), t + 1)
                dve.tensor_tensor(x[:, t, :], x[:, t, :], bank[OUT_BANKS[t]][:, :], ALU.add)\
                   .then_inc(sem("ffn_added"), 1)

        block = ctx.enter_context(nc.Block())

        @block.sync
        def _(sp):
            sp.dma_start(xT[:, :, :], a["xT"]).then_inc(sem("ld_xT"), 16)
            load_group(sp, "l0", 0, 0)
            for dst, name in ((ident, "ident"), (cos, "cos"), (sin, "sin"), (keys, "keys"), (causal, "causal"),
                              (identb, "identb")):
                sp.dma_start(dst[:, :], a[name]).then_inc(sem("ld_const"), 16)
            sp.dma_start(x[:, :, :], a["x"]).then_inc(sem("ld_x"), 16)
            load_group(sp, "l0", 1, 1)
            for dst, name in ((quant[:, 0:4], "quant"), (base[:, :], "base"), (gate[:, 0:1], "gate")):
                sp.dma_start(dst, a[name].broadcast_to([P, dst.shape[1]])).then_inc(sem("ld_small"), 16)
            for dst, name in ((wmix[:, :, :], "wmix"), (branch[:, :], "branch"), (eye4[:, :], "eye4")):
                sp.dma_start(dst, a[name]).then_inc(sem("ld_small"), 16)
            sp.dma_start(q2[:, :, :], a["ctx"]).then_inc(sem("ld_ctx"), 16)
            for b in range(B):
                sp.dma_start(wg[b][:, :, :], a["ctxT"][b]).then_inc(sem(f"ld_ctxT{b}"), 16)
            with nc.sync.Fori(1, NG // 2) as i:
                for p in range(2):
                    load_group(sp, "l0", 2 * i + p, p)
            for dst, name in ((win[:, :, :], "win"), (hvec[:, 0:2], "hvec"), (lower[:, :], "lower"),
                              (ones[:, :], "ones"), (dvec[:, 0:3], "dvec")):
                sp.dma_start(dst, a[name]).then_inc(sem("ld_l1"), 16)
            sp.wait_ge(sem("l0_score"), 8 * NG)
            for g in range(2):
                kv_weights_load(sp, g, g)
            for g in range(2):
                load_group(sp, "l1", g, g, (), (("l0_kvdone", 1), ("l0_proj", 5), ("l0_out", 4)))
            kv_sync(sp)
            gate_load = (("wg", wg, a["l1_wg"], "gate", 4),)
            for g in range(2):
                sp.wait_ge(sem("kv_proj"), 4 * NG)
                sp.dma_start(wg[g][:, :, :], a["l1_wg"][g]).then_inc(sem(f"l1_wg{g}"), 16)
            for g in range(2):
                sp.wait_ge(sem(f"kv_out{g}"), 32 * NG // 2)
            sp.wait_ge(sem("dt_vector"), 3)
            sp.dma_start(a["g_rows"], row(6)).then_inc(sem("rows_out"), 16)
            sp.wait_ge(sem("rows_out"), 16)
            for g in range(2):
                l1_load_rows(sp, g, g)
            with nc.sync.Fori(1, NG // 2) as i:
                for p in range(2):
                    load_group(sp, "l1", 2 * i + p, p, gate_load)
                    l1_load_rows(sp, 2 * i + p, p)
            for g in range(2):
                x_load(sp, g, g, True)
            sp.dma_start(amask[:, :, :], a["amask"]).then_inc(sem("ld_mask"), 16)
            with nc.sync.Fori(1, NG // 2) as i:
                for p in range(2):
                    x_load(sp, 2 * i + p, p)
            sp.wait_ge(sem("x_proj"), 4 * (NG - 1))
            sp.dma_start(wq[0][:, :, :], a["ffn_w"]).then_inc(sem("ld_ffn"), 16)
            for dst, name in ((loraA[:, :, :], "loraA"), (loraB[:, :], "loraB"), (lim[:, :], "lim")):
                sp.dma_start(dst, a[name]).then_inc(sem("ld_ffn"), 16)
            sp.dma_start(starts[:, :], a["starts"].broadcast_to([LORA * RANK, 4])).then_inc(sem("ld_ffn"), 16)
            for t in range(NT):
                sp.wait_ge(sem("ln_x"), NT * 5 + t + 1)
                sp.dma_start(out[t * P:(t + 1) * P, :], x[:, t, :]).then_inc(sem("stored"), 16)
            sp.wait_ge(sem("stored"), 16 * NT)

        @block.scalar
        def _(act):
            act.preload_act_table_set("natural_log_exp_and_others")
            l0_scalar(act)
            ln_scalar(act, 0)
            mix_scalar(act)
            sink_scalar(act)
            ln_scalar(act, 2)
            dt_scalar(act)
            l1_scalar(act)
            ln_scalar(act, 3, xT_high)
            x_scalar(act)
            ln_scalar(act, 4)

        @block.gpsimd
        def _(pool):
            pool.memset(half[:, :], -0.5).then_inc(sem("half"), 1)
            pool.wait_ge(sem("ld_const"), 6 * 16)
            l0_gpsimd(pool)
            ln_gpsimd(pool, 0)
            ln_gpsimd(pool, 1)
            mix_gpsimd(pool)
            pool.wait_ge(sem("ld_l1"), 16 * 5)
            sink_gpsimd(pool)
            ln_gpsimd(pool, 2)
            l1_gpsimd(pool)
            x_gpsimd_first(pool)
            ln_gpsimd(pool, 3)
            pool.memset(low[:, :], 1.0).then_inc(sem("low_ones"), 1)
            x_gpsimd(pool)
            ln_gpsimd(pool, 4)
            ln_gpsimd(pool, 5)

        @block.tensor
        def _(pe):
            pe.wait_ge(sem("ld_xT"), 16)
            pe.wait_ge(sem("ld_const"), 6 * 16)
            l0_tensor(pe)
            ln_tensor(pe, 0)
            cross_tensor(pe)
            ln_tensor(pe, 1)
            mix_tensor(pe)
            kv_tensor(pe)
            pe.wait_ge(sem("kv_copied"), 4 * NG)
            ln_tensor(pe, 2)
            dt_tensor(pe)
            l1_tensor(pe)
            ln_tensor(pe, 3)
            pe.wait_ge(sem("xT_low"), NT)
            x_tensor(pe)
            ln_tensor(pe, 4)
            ffn_tensor(pe)

        @block.vector
        def _(dve):
            dve.wait_ge(sem("ld_const"), 6 * 16)
            dve.wait_ge(sem("ld_x"), 16)
            dve.wait_ge(sem("ld_small"), 6 * 16)
            dve.reciprocal(quant[:, 4:6], quant[:, 0:4:2])
            dve.tensor_scalar(gate[:, 1:2], gate[:, 0:1], -1.0, 80.0, ALU.mult, ALU.min).then_inc(sem("quant"), 1)
            l0_vector(dve)
            ln_vector(dve, 0, ("l0_added", 4 * (NG - 1) + 1))
            cross_vector(dve)
            ln_vector(dve, 1, ("cross_added", 1))
            mix_vector(dve)
            ln_vector(dve, 2, ("mixed", NT * 24 - (NT - 1)))
            dve.wait_ge(sem("ld_l1"), 16 * 5)
            dt_vector(dve)
            l1_vector(dve)
            ln_vector(dve, 3, ("l1_added", 4 * (NG - 1) + 1))
            ln_split(dve, 3)
            x_vector(dve)
            ffn_select(dve)
            ln_vector(dve, 4, ("x_added", 4 * (NG - 1) + 1))
            ffn_vector(dve)
            ln_vector(dve, 5, ("ffn_added", 1))


def kernel(**inputs):
    import numpy as np
    import concourse.bacc as bacc
    from concourse import mybir as mb
    from concourse.bass_utils import run_bass_kernel_spmd

    f32 = np.float32

    def feature_major(w):
        return w.T.reshape(KC, P, -1).transpose(1, 0, 2)

    def by_group(w):
        return w.reshape(NG, -1, KC, P).transpose(0, 3, 2, 1)

    def key_value(wk, wv):
        return np.concatenate([by_group(wk), by_group(wv)], axis=3)

    def out_by_group(w):
        return w.reshape(D, NG, GH, HD).transpose(1, 3, 2, 0)

    g = {k: np.asarray(v) for k, v in inputs.items()}
    rows = np.arange(L)
    freq = 1.0 / 10000.0 ** (np.arange(0, HD, 2, dtype=f32) / HD)
    angle = (rows.astype(f32)[:, None] * freq[None, :]).T
    cos, sin = np.cos(angle).astype(f32), np.sin(angle).astype(f32)
    key = np.where(rows < 35, 0.5, np.where(rows < 107, 1.5, 1.0)).astype(f32)
    first = np.where(rows[:P, None] >= 107, key[None, :P], f32(1.0))
    keys = (np.concatenate([first, np.broadcast_to(key, (P, L))], axis=1) * SCALE).astype(f32)
    upper = np.arange(P)[:, None] < np.arange(P)[None, :]
    arrays = {
        "x": g["x"].reshape(NT, P, D).transpose(1, 0, 2),
        "xT": feature_major(g["x"].reshape(T, D)),
        "ident": np.eye(P, dtype=f32),
        "identb": np.eye(P).astype(mb.dt.np(mb.dt.bfloat16)),
        "cos": np.concatenate([cos, cos]),
        "sin": np.concatenate([-sin, sin]),
        "keys": keys,
        "causal": np.where(upper, MASKED, 0.0).astype(mb.dt.np(mb.dt.bfloat16)),
        "l0_wq": by_group(g["L0_attn_wq"]),
        "l0_wkv": key_value(g["L0_attn_wk"], g["L0_attn_wv"]),
        "l0_wo": out_by_group(g["L0_attn_wo"]),
        "quant": np.concatenate([g["L0_xattn_x1_scale"], g["L0_xattn_x1_zp"],
                                 g["L0_xattn_x2_scale"], g["L0_xattn_x2_zp"]])[None, :],
        "ctx": g["ctx_4096"].reshape(B * CT, P, D).transpose(1, 0, 2),
        "base": np.concatenate([g["L0_ffn_H_res_base"].reshape(-1), g["L0_ffn_H_pre_base"],
                                g["L0_ffn_H_post_base"]])[None, :],
        "gate": g["L0_ffn_gate"][None, :],
        "wmix": feature_major(np.concatenate([g["L0_ffn_W_res"], g["L0_ffn_W_pre"], g["L0_ffn_W_post"]])),
        "branch": g["L0_ffn_W_branch"],
        "eye4": np.tile(np.eye(4, dtype=f32).reshape(1, 16), (P, 1)),
        "win": feature_major(g["L1_attn_Win"]),
        "hvec": np.stack([g["L1_attn_dt_bias"], g["L1_attn_A_log_bias"]], axis=1),
        "lower": np.where(upper.T, f32(MASKED), f32(0.0)),
        "ones": np.ones((P, P), f32),
        "dvec": np.stack([g["L1_attn_gnorm_w"], g["L1_xattn_q_norm_w"], g["L1_xattn_k_norm_w"]], axis=1),
        "l1_wq": by_group(g["L1_attn_Wq"]),
        "l1_wkv": key_value(g["L1_attn_Wk"], g["L1_attn_Wv"]),
        "l1_wo": out_by_group(g["L1_attn_Wo"]),
        "l1_wg": by_group(g["L1_attn_Wg"]),
        "x_wq": by_group(g["L1_xattn_Wq"]),
        "x_wkv": key_value(g["L1_xattn_Wk"], g["L1_xattn_Wv"]),
        "x_wo": out_by_group(g["L1_xattn_Wo"]),
        "ctxT": np.stack([feature_major(c) for c in g["ctx_4096"]]),
        "amask": g["mask_1x1xSxS2_ff0"].reshape(2, P, C).transpose(1, 0, 2),
        "ffn_w": feature_major(g["L1_ffn_weight"]),
        "loraA": feature_major(g["L1_ffn_lora_A"].reshape(LORA * RANK, D)),
        "loraB": np.concatenate([g["L1_ffn_lora_B"].transpose(0, 2, 1).reshape(LORA * RANK, D),
                                 g["L1_ffn_bias"][None, :]]),
        "lim": np.repeat(np.array([[2, 2], [3, 3], [4, 1000]], f32), RANK, axis=0),
        "starts": g["L1_ffn_lora_start_indices"].reshape(1, 4),

    }
    nc = bacc.Bacc("TRN2", target_bir_lowering=False, num_devices=1)
    arrays = {f"in_{n}": np.ascontiguousarray(v) for n, v in arrays.items()}
    aps = {n[3:]: nc.dram_tensor(n, v.shape, mb.dt.from_np(v.dtype), kind="ExternalInput").ap()
           for n, v in arrays.items()}
    aps["g_rows"] = nc.dram_tensor("g_rows", (NG * GH, T), mb.dt.float32, kind="Internal").ap()
    for name in ("kv_keys", "kv_values"):
        aps[name] = nc.dram_tensor(name, (NG, P, B * C), mb.dt.float32, kind="Internal").ap()
    out = nc.dram_tensor("out", (T, D), mb.dt.float32, kind="ExternalOutput").ap()
    decoder_kernel(nc, aps, out)
    r = run_bass_kernel_spmd(nc, [arrays], core_ids=[0])
    return r.results[0]["out"].reshape(B, L, D)
```
